# Optimizing a Trainium2 kernel written in Bass

```python
import numpy as np
import jax
import jax.numpy as jnp

def _softmax(x, axis=-1):
    return jax.nn.softmax(x, axis=axis)

def _gelu(x):
    return jax.nn.gelu(x, approximate=True)

def _silu(x):
    return jax.nn.silu(x)

def _sigmoid(x):
    return jax.nn.sigmoid(x)

def _layernorm(x, axis=-1, eps=1e-05):
    m = jnp.mean(x, axis=axis, keepdims=True)
    v = jnp.var(x, axis=axis, keepdims=True)
    return (x - m) / jnp.sqrt(v + eps)

def _scatter_add(tgt, idx, src, axis=0):
    return tgt.at[idx].add(src)

def _segment_sum(src, seg, n):
    return jax.ops.segment_sum(src, seg, n)
kernel_name = 'mk_recurrent_d2_jaxref_r4_fd02df'

def setup_inputs(seed: int=0):
    np.random.seed(seed)
    _w = jnp.asarray

    def _L0_attn_setup():
        import jax, jax.numpy as jnp
        import numpy as np
        D_MODEL = 256
        N_HEADS = 16
        HEAD_DIM = D_MODEL // N_HEADS
        WINDOW = 128
        LOCAL_BLOCK = 64
        LATENT_TOKENS = 64
        LATENT_D = 64
        LATENT_HEADS = 4
        LATENT_HD = LATENT_D // LATENT_HEADS
        NEG = -1000000000.0

        def _local_attention(q, k, v):
            B, H, S, hd = q.shape
            bs = min(S, max(WINDOW, LOCAL_BLOCK))
            nb = S // bs
            w = WINDOW
            L = bs + w - 1
            k_pad = jnp.pad(k, ((0, 0), (0, 0), (w - 1, 0), (0, 0)))
            v_pad = jnp.pad(v, ((0, 0), (0, 0), (w - 1, 0), (0, 0)))
            starts = jnp.arange(nb) * bs
            idx = starts[:, None] + jnp.arange(L)[None, :]
            kb = k_pad[:, :, idx]
            vb = v_pad[:, :, idx]
            qb = q.reshape(B, H, nb, bs, hd)
            q_pos = starts[:, None] + jnp.arange(bs)[None, :]
            k_gpos = starts[:, None] + jnp.arange(L)[None, :] - (w - 1)
            dist = q_pos[:, :, None] - k_gpos[:, None, :]
            allowed = (dist > 0) & (dist <= w) & (k_gpos[:, None, :] >= 0)
            scale = 1.0 / np.sqrt(hd)
            scores = jnp.einsum('bhnqd,bhnkd->bhnqk', qb, kb) * scale
            scores = jnp.where(allowed, scores, NEG)
            attn = jax.nn.softmax(scores, axis=-1)
            attn = jnp.where(allowed.any(-1)[None, None, :, :, None], attn, 0.0)
            out = jnp.einsum('bhnqk,bhnkd->bhnqd', attn, vb)
            return out.reshape(B, H, S, hd)
        key = jax.random.key(seed)
        ks = jax.random.split(key, 14)
        B, S = (2, 1024)
        s = 0.02
        f32 = jnp.float32
        return {'x': jax.random.normal(ks[0], (B, S, D_MODEL), f32), 'qkv_w': jax.random.normal(ks[1], (D_MODEL, 3 * D_MODEL), f32) * s, 'qkv_b': jnp.zeros((3 * D_MODEL,), f32), 'rq_w': jax.random.normal(ks[2], (D_MODEL, LATENT_D), f32) * s, 'rq_b': jnp.zeros((LATENT_D,), f32), 'rkv_w': jax.random.normal(ks[3], (D_MODEL, 2 * LATENT_D), f32) * s, 'rkv_b': jnp.zeros((2 * LATENT_D,), f32), 'rout_w': jax.random.normal(ks[4], (LATENT_D, D_MODEL), f32) * s, 'rout_b': jnp.zeros((D_MODEL,), f32), 'out_w': jax.random.normal(ks[5], (D_MODEL, D_MODEL), f32) * s, 'out_b': jnp.zeros((D_MODEL,), f32), 'gl_w': jax.random.normal(ks[6], (HEAD_DIM, 1), f32) * s, 'gr_w': jax.random.normal(ks[7], (HEAD_DIM, 1), f32) * s}
    _L0_attn_in = _L0_attn_setup()

    def _L0_ffn_setup():
        import jax, jax.numpy as jnp
        import numpy as np
        EPS = 1e-06
        LN_EPS = 1e-05

        def _absmean_core(W):
            gamma = jnp.mean(jnp.abs(W)) + EPS
            Ws = W / gamma
            Wq = jnp.sign(Ws) * jnp.minimum(jnp.round(jnp.abs(Ws)), 1.0)
            return (Wq, gamma)

        @jax.custom_vjp
        def absmean(W):
            return _absmean_core(W)[0]

        def _absmean_fwd(W):
            Wq, gamma = _absmean_core(W)
            return (Wq, gamma)

        def _absmean_bwd(gamma, g):
            return (g / gamma,)
        absmean.defvjp(_absmean_fwd, _absmean_bwd)

        def layernorm(x, w, b, eps=LN_EPS):
            mu = jnp.mean(x, axis=-1, keepdims=True)
            var = jnp.mean((x - mu) ** 2, axis=-1, keepdims=True)
            return (x - mu) * jax.lax.rsqrt(var + eps) * w + b
        key = jax.random.key(seed)
        k1, k2, k3 = jax.random.split(key, 3)
        d, h = (256, 1024)
        B, T = (8, 512)
        return {'x': jax.random.normal(k1, (B, T, d), jnp.float32), 'W_fc': jax.random.normal(k2, (h, d), jnp.float32), 'ln_w': jnp.ones((h,), jnp.float32), 'ln_b': jnp.zeros((h,), jnp.float32), 'W_proj': jax.random.normal(k3, (d, h), jnp.float32)}
    _L0_ffn_in = _L0_ffn_setup()

    def _L1_attn_setup():
        import jax, jax.numpy as jnp
        import numpy as np
        from jax import lax
        B_, L_, D_MODEL = (2, 256, 256)
        D_STATE, D_CONV, EXPAND = (16, 4, 2)
        D_INNER = EXPAND * D_MODEL
        DT_RANK = (D_MODEL + 15) // 16
        LN_EPS = 1e-05

        def _silu(v):
            return v * jax.nn.sigmoid(v)

        def _mamba_params(key):
            ks = jax.random.split(key, 6)
            g = lambda k, shp, sc: jax.random.normal(k, shp, jnp.float32) * sc
            return {'in_proj_w': g(ks[0], (2 * D_INNER, D_MODEL), D_MODEL ** (-0.5)), 'conv_w': g(ks[1], (D_INNER, D_CONV), D_CONV ** (-0.5)), 'conv_b': jnp.zeros((D_INNER,), jnp.float32), 'x_proj_w': g(ks[2], (DT_RANK + 2 * D_STATE, D_INNER), D_INNER ** (-0.5)), 'dt_proj_w': g(ks[3], (D_INNER, DT_RANK), DT_RANK ** (-0.5)), 'dt_proj_b': jax.random.uniform(ks[4], (D_INNER,), jnp.float32, -4.0, -2.0), 'A_log': jnp.log(jnp.broadcast_to(jnp.arange(1, D_STATE + 1, dtype=jnp.float32), (D_INNER, D_STATE))), 'D': jnp.ones((D_INNER,), jnp.float32), 'out_proj_w': g(ks[5], (D_MODEL, D_INNER), D_INNER ** (-0.5))}

        def _mamba(x, in_proj_w, conv_w, conv_b, x_proj_w, dt_proj_w, dt_proj_b, A_log, D, out_proj_w):
            b, l, _ = x.shape
            xz = x @ in_proj_w.T
            xi, z = jnp.split(xz, 2, axis=-1)
            xp = jnp.pad(xi, ((0, 0), (D_CONV - 1, 0), (0, 0)))
            xc = conv_b + sum((xp[:, k:k + l, :] * conv_w[:, k] for k in range(D_CONV)))
            xc = _silu(xc)
            dbl = xc @ x_proj_w.T
            dt = jax.nn.softplus(dbl[..., :DT_RANK] @ dt_proj_w.T + dt_proj_b)
            Bm = dbl[..., DT_RANK:DT_RANK + D_STATE]
            Cm = dbl[..., DT_RANK + D_STATE:]
            A = -jnp.exp(A_log)
            dA = jnp.exp(dt[..., None] * A)
            dBu = (dt * xc)[..., None] * Bm[:, :, None, :]

            def step(h, inp):
                dA_t, dBu_t, C_t = inp
                h = dA_t * h + dBu_t
                return (h, jnp.einsum('bdn,bn->bd', h, C_t))
            h0 = jnp.zeros((b, D_INNER, D_STATE), x.dtype)
            _, ys = lax.scan(step, h0, (dA.transpose(1, 0, 2, 3), dBu.transpose(1, 0, 2, 3), Cm.transpose(1, 0, 2)))
            y = ys.transpose(1, 0, 2) + xc * D
            y = y * _silu(z)
            return y @ out_proj_w.T
        key = jax.random.key(seed)
        kx, kf, kb = jax.random.split(key, 3)
        inp = {'x': jax.random.normal(kx, (B_, L_, D_MODEL), jnp.float32)}
        for pref, k in (('fwd_', kf), ('bwd_', kb)):
            for name, val in _mamba_params(k).items():
                inp[pref + name] = val
        inp['ln_gamma'] = jnp.ones((D_MODEL,), jnp.float32)
        inp['ln_beta'] = jnp.zeros((D_MODEL,), jnp.float32)
        return inp
    _L1_attn_in = _L1_attn_setup()

    def _L1_ffn_setup():
        import jax, jax.numpy as jnp
        import numpy as np
        D = 256
        I = 128
        E = 32
        K = 4
        T = 2 * 512
        C = 2 * T * K // E
        key = jax.random.key(seed)
        ks = jax.random.split(key, 9)
        bf = jnp.bfloat16
        std = 0.02
        x = jax.random.normal(ks[0], (2, 512, D), dtype=jnp.float32).astype(bf)
        gate_w = (std * jax.random.normal(ks[1], (E, D), dtype=jnp.float32)).astype(bf)
        bias = jnp.zeros((E,), jnp.float32)
        W1 = (std * jax.random.normal(ks[2], (E, D, I), dtype=jnp.float32)).astype(bf)
        W3 = (std * jax.random.normal(ks[3], (E, D, I), dtype=jnp.float32)).astype(bf)
        W2 = (std * jax.random.normal(ks[4], (E, I, D), dtype=jnp.float32)).astype(bf)
        sw1 = (std * jax.random.normal(ks[5], (I, D), dtype=jnp.float32)).astype(bf)
        sw3 = (std * jax.random.normal(ks[6], (I, D), dtype=jnp.float32)).astype(bf)
        sw2 = (std * jax.random.normal(ks[7], (D, I), dtype=jnp.float32)).astype(bf)
        return {'x': x, 'gate_w': gate_w, 'bias': bias, 'W1': W1, 'W3': W3, 'W2': W2, 'sw1': sw1, 'sw3': sw3, 'sw2': sw2}
    _L1_ffn_in = _L1_ffn_setup()
    _d = {'L0_attn_x': _L0_attn_in['x'], 'L0_attn_qkv_w': _L0_attn_in['qkv_w'], 'L0_attn_qkv_b': _L0_attn_in['qkv_b'], 'L0_attn_rq_w': _L0_attn_in['rq_w'], 'L0_attn_rq_b': _L0_attn_in['rq_b'], 'L0_attn_rkv_w': _L0_attn_in['rkv_w'], 'L0_attn_rkv_b': _L0_attn_in['rkv_b'], 'L0_attn_rout_w': _L0_attn_in['rout_w'], 'L0_attn_rout_b': _L0_attn_in['rout_b'], 'L0_attn_out_w': _L0_attn_in['out_w'], 'L0_attn_out_b': _L0_attn_in['out_b'], 'L0_attn_gl_w': _L0_attn_in['gl_w'], 'L0_attn_gr_w': _L0_attn_in['gr_w'], 'L0_ffn_W_fc': _L0_ffn_in['W_fc'], 'L0_ffn_ln_w': _L0_ffn_in['ln_w'], 'L0_ffn_ln_b': _L0_ffn_in['ln_b'], 'L0_ffn_W_proj': _L0_ffn_in['W_proj'], 'L1_attn_fwd_in_proj_w': _L1_attn_in['fwd_in_proj_w'], 'L1_attn_fwd_conv_w': _L1_attn_in['fwd_conv_w'], 'L1_attn_fwd_conv_b': _L1_attn_in['fwd_conv_b'], 'L1_attn_fwd_x_proj_w': _L1_attn_in['fwd_x_proj_w'], 'L1_attn_fwd_dt_proj_w': _L1_attn_in['fwd_dt_proj_w'], 'L1_attn_fwd_dt_proj_b': _L1_attn_in['fwd_dt_proj_b'], 'L1_attn_fwd_A_log': _L1_attn_in['fwd_A_log'], 'L1_attn_fwd_D': _L1_attn_in['fwd_D'], 'L1_attn_fwd_out_proj_w': _L1_attn_in['fwd_out_proj_w'], 'L1_attn_bwd_in_proj_w': _L1_attn_in['bwd_in_proj_w'], 'L1_attn_bwd_conv_w': _L1_attn_in['bwd_conv_w'], 'L1_attn_bwd_conv_b': _L1_attn_in['bwd_conv_b'], 'L1_attn_bwd_x_proj_w': _L1_attn_in['bwd_x_proj_w'], 'L1_attn_bwd_dt_proj_w': _L1_attn_in['bwd_dt_proj_w'], 'L1_attn_bwd_dt_proj_b': _L1_attn_in['bwd_dt_proj_b'], 'L1_attn_bwd_A_log': _L1_attn_in['bwd_A_log'], 'L1_attn_bwd_D': _L1_attn_in['bwd_D'], 'L1_attn_bwd_out_proj_w': _L1_attn_in['bwd_out_proj_w'], 'L1_attn_ln_gamma': _L1_attn_in['ln_gamma'], 'L1_attn_ln_beta': _L1_attn_in['ln_beta'], 'L1_ffn_gate_w': _L1_ffn_in['gate_w'], 'L1_ffn_bias': _L1_ffn_in['bias'], 'L1_ffn_W1': _L1_ffn_in['W1'], 'L1_ffn_W3': _L1_ffn_in['W3'], 'L1_ffn_W2': _L1_ffn_in['W2'], 'L1_ffn_sw1': _L1_ffn_in['sw1'], 'L1_ffn_sw3': _L1_ffn_in['sw3'], 'L1_ffn_sw2': _L1_ffn_in['sw2']}
    _x0 = _d['L0_attn_x']
    _d['L0_attn_x'] = jax.random.normal(jax.random.fold_in(jax.random.key(seed), 1), (16, 512, 256), dtype=_x0.dtype)
    del _x0
    return _d

def reference(L0_attn_x, L0_attn_qkv_w, L0_attn_qkv_b, L0_attn_rq_w, L0_attn_rq_b, L0_attn_rkv_w, L0_attn_rkv_b, L0_attn_rout_w, L0_attn_rout_b, L0_attn_out_w, L0_attn_out_b, L0_attn_gl_w, L0_attn_gr_w, L0_ffn_W_fc, L0_ffn_ln_w, L0_ffn_ln_b, L0_ffn_W_proj, L1_attn_fwd_in_proj_w, L1_attn_fwd_conv_w, L1_attn_fwd_conv_b, L1_attn_fwd_x_proj_w, L1_attn_fwd_dt_proj_w, L1_attn_fwd_dt_proj_b, L1_attn_fwd_A_log, L1_attn_fwd_D, L1_attn_fwd_out_proj_w, L1_attn_bwd_in_proj_w, L1_attn_bwd_conv_w, L1_attn_bwd_conv_b, L1_attn_bwd_x_proj_w, L1_attn_bwd_dt_proj_w, L1_attn_bwd_dt_proj_b, L1_attn_bwd_A_log, L1_attn_bwd_D, L1_attn_bwd_out_proj_w, L1_attn_ln_gamma, L1_attn_ln_beta, L1_ffn_gate_w, L1_ffn_bias, L1_ffn_W1, L1_ffn_W3, L1_ffn_W2, L1_ffn_sw1, L1_ffn_sw3, L1_ffn_sw2):

    def _L0_attn_ref(x, qkv_w, qkv_b, rq_w, rq_b, rkv_w, rkv_b, rout_w, rout_b, out_w, out_b, gl_w, gr_w):
        import jax, jax.numpy as jnp
        import numpy as np
        D_MODEL = 256
        N_HEADS = 16
        HEAD_DIM = D_MODEL // N_HEADS
        WINDOW = 128
        LOCAL_BLOCK = 64
        LATENT_TOKENS = 64
        LATENT_D = 64
        LATENT_HEADS = 4
        LATENT_HD = LATENT_D // LATENT_HEADS
        NEG = -1000000000.0

        def _local_attention(q, k, v):
            B, H, S, hd = q.shape
            bs = min(S, max(WINDOW, LOCAL_BLOCK))
            nb = S // bs
            w = WINDOW
            L = bs + w - 1
            k_pad = jnp.pad(k, ((0, 0), (0, 0), (w - 1, 0), (0, 0)))
            v_pad = jnp.pad(v, ((0, 0), (0, 0), (w - 1, 0), (0, 0)))
            starts = jnp.arange(nb) * bs
            idx = starts[:, None] + jnp.arange(L)[None, :]
            kb = k_pad[:, :, idx]
            vb = v_pad[:, :, idx]
            qb = q.reshape(B, H, nb, bs, hd)
            q_pos = starts[:, None] + jnp.arange(bs)[None, :]
            k_gpos = starts[:, None] + jnp.arange(L)[None, :] - (w - 1)
            dist = q_pos[:, :, None] - k_gpos[:, None, :]
            allowed = (dist > 0) & (dist <= w) & (k_gpos[:, None, :] >= 0)
            scale = 1.0 / np.sqrt(hd)
            scores = jnp.einsum('bhnqd,bhnkd->bhnqk', qb, kb) * scale
            scores = jnp.where(allowed, scores, NEG)
            attn = jax.nn.softmax(scores, axis=-1)
            attn = jnp.where(allowed.any(-1)[None, None, :, :, None], attn, 0.0)
            out = jnp.einsum('bhnqk,bhnkd->bhnqd', attn, vb)
            return out.reshape(B, H, S, hd)
        B, S, D = x.shape
        qkv = x @ qkv_w + qkv_b
        q, k, v = jnp.split(qkv, 3, axis=-1)

        def heads(t):
            return t.reshape(B, S, N_HEADS, HEAD_DIM).transpose(0, 2, 1, 3)
        local = _local_attention(heads(q), heads(k), heads(v))
        chunk = -(-S // min(LATENT_TOKENS, S))
        nlat = S // chunk
        pooled = x.reshape(B, nlat, chunk, D).mean(axis=2)
        chunk_ids = jnp.arange(S) // chunk
        rq = (x @ rq_w + rq_b).reshape(B, S, LATENT_HEADS, LATENT_HD).transpose(0, 2, 1, 3)
        rkv = pooled @ rkv_w + rkv_b
        rk, rv = jnp.split(rkv, 2, axis=-1)
        rk = rk.reshape(B, nlat, LATENT_HEADS, LATENT_HD).transpose(0, 2, 1, 3)
        rv = rv.reshape(B, nlat, LATENT_HEADS, LATENT_HD).transpose(0, 2, 1, 3)
        lscale = 1.0 / np.sqrt(LATENT_HD)
        lscores = jnp.einsum('bhsd,bhld->bhsl', rq, rk) * lscale
        lat_allowed = jnp.arange(nlat)[None, :] < chunk_ids[:, None]
        lscores = jnp.where(lat_allowed[None, None], lscores, NEG)
        lattn = jax.nn.softmax(lscores, axis=-1)
        lattn = jnp.where(lat_allowed.any(-1)[None, None, :, None], lattn, 0.0)
        lat_out = jnp.einsum('bhsl,bhld->bhsd', lattn, rv)
        lat_out = lat_out.transpose(0, 2, 1, 3).reshape(B, S, LATENT_D)
        remote = lat_out @ rout_w + rout_b
        remote_h = remote.reshape(B, S, N_HEADS, HEAD_DIM).transpose(0, 2, 1, 3)
        gate = jax.nn.sigmoid(local @ gl_w + remote_h @ gr_w)
        mixed = gate * local + (1.0 - gate) * remote_h
        mixed = mixed.transpose(0, 2, 1, 3).reshape(B, S, D)
        return mixed @ out_w + out_b

    def _L0_ffn_ref(x, W_fc, ln_w, ln_b, W_proj):
        import jax, jax.numpy as jnp
        import numpy as np
        EPS = 1e-06
        LN_EPS = 1e-05

        def _absmean_core(W):
            gamma = jnp.mean(jnp.abs(W)) + EPS
            Ws = W / gamma
            Wq = jnp.sign(Ws) * jnp.minimum(jnp.round(jnp.abs(Ws)), 1.0)
            return (Wq, gamma)

        @jax.custom_vjp
        def absmean(W):
            return _absmean_core(W)[0]

        def _absmean_fwd(W):
            Wq, gamma = _absmean_core(W)
            return (Wq, gamma)

        def _absmean_bwd(gamma, g):
            return (g / gamma,)
        absmean.defvjp(_absmean_fwd, _absmean_bwd)

        def layernorm(x, w, b, eps=LN_EPS):
            mu = jnp.mean(x, axis=-1, keepdims=True)
            var = jnp.mean((x - mu) ** 2, axis=-1, keepdims=True)
            return (x - mu) * jax.lax.rsqrt(var + eps) * w + b
        h = jnp.einsum('btd,hd->bth', x, absmean(W_fc))
        h = jax.nn.gelu(h, approximate=False)
        h = layernorm(h, ln_w, ln_b)
        return jnp.einsum('bth,dh->btd', h, absmean(W_proj))

    def _L1_attn_ref(x, fwd_in_proj_w, fwd_conv_w, fwd_conv_b, fwd_x_proj_w, fwd_dt_proj_w, fwd_dt_proj_b, fwd_A_log, fwd_D, fwd_out_proj_w, bwd_in_proj_w, bwd_conv_w, bwd_conv_b, bwd_x_proj_w, bwd_dt_proj_w, bwd_dt_proj_b, bwd_A_log, bwd_D, bwd_out_proj_w, ln_gamma, ln_beta):
        import jax, jax.numpy as jnp
        import numpy as np
        from jax import lax
        B_, L_, D_MODEL = (2, 256, 256)
        D_STATE, D_CONV, EXPAND = (16, 4, 2)
        D_INNER = EXPAND * D_MODEL
        DT_RANK = (D_MODEL + 15) // 16
        LN_EPS = 1e-05

        def _silu(v):
            return v * jax.nn.sigmoid(v)

        def _mamba_params(key):
            ks = jax.random.split(key, 6)
            g = lambda k, shp, sc: jax.random.normal(k, shp, jnp.float32) * sc
            return {'in_proj_w': g(ks[0], (2 * D_INNER, D_MODEL), D_MODEL ** (-0.5)), 'conv_w': g(ks[1], (D_INNER, D_CONV), D_CONV ** (-0.5)), 'conv_b': jnp.zeros((D_INNER,), jnp.float32), 'x_proj_w': g(ks[2], (DT_RANK + 2 * D_STATE, D_INNER), D_INNER ** (-0.5)), 'dt_proj_w': g(ks[3], (D_INNER, DT_RANK), DT_RANK ** (-0.5)), 'dt_proj_b': jax.random.uniform(ks[4], (D_INNER,), jnp.float32, -4.0, -2.0), 'A_log': jnp.log(jnp.broadcast_to(jnp.arange(1, D_STATE + 1, dtype=jnp.float32), (D_INNER, D_STATE))), 'D': jnp.ones((D_INNER,), jnp.float32), 'out_proj_w': g(ks[5], (D_MODEL, D_INNER), D_INNER ** (-0.5))}

        def _mamba(x, in_proj_w, conv_w, conv_b, x_proj_w, dt_proj_w, dt_proj_b, A_log, D, out_proj_w):
            b, l, _ = x.shape
            xz = x @ in_proj_w.T
            xi, z = jnp.split(xz, 2, axis=-1)
            xp = jnp.pad(xi, ((0, 0), (D_CONV - 1, 0), (0, 0)))
            xc = conv_b + sum((xp[:, k:k + l, :] * conv_w[:, k] for k in range(D_CONV)))
            xc = _silu(xc)
            dbl = xc @ x_proj_w.T
            dt = jax.nn.softplus(dbl[..., :DT_RANK] @ dt_proj_w.T + dt_proj_b)
            Bm = dbl[..., DT_RANK:DT_RANK + D_STATE]
            Cm = dbl[..., DT_RANK + D_STATE:]
            A = -jnp.exp(A_log)
            dA = jnp.exp(dt[..., None] * A)
            dBu = (dt * xc)[..., None] * Bm[:, :, None, :]

            def step(h, inp):
                dA_t, dBu_t, C_t = inp
                h = dA_t * h + dBu_t
                return (h, jnp.einsum('bdn,bn->bd', h, C_t))
            h0 = jnp.zeros((b, D_INNER, D_STATE), x.dtype)
            _, ys = lax.scan(step, h0, (dA.transpose(1, 0, 2, 3), dBu.transpose(1, 0, 2, 3), Cm.transpose(1, 0, 2)))
            y = ys.transpose(1, 0, 2) + xc * D
            y = y * _silu(z)
            return y @ out_proj_w.T
        yf = _mamba(x, fwd_in_proj_w, fwd_conv_w, fwd_conv_b, fwd_x_proj_w, fwd_dt_proj_w, fwd_dt_proj_b, fwd_A_log, fwd_D, fwd_out_proj_w)
        yb = _mamba(jnp.flip(x, 1), bwd_in_proj_w, bwd_conv_w, bwd_conv_b, bwd_x_proj_w, bwd_dt_proj_w, bwd_dt_proj_b, bwd_A_log, bwd_D, bwd_out_proj_w)
        yo = yf + jnp.flip(yb, 1)
        mu = jnp.mean(yo, axis=-1, keepdims=True)
        var = jnp.mean(jnp.square(yo - mu), axis=-1, keepdims=True)
        return ln_gamma * (yo - mu) / jnp.sqrt(var + LN_EPS) + ln_beta

    def _L1_ffn_ref(x, gate_w, bias, W1, W3, W2, sw1, sw3, sw2):
        import jax, jax.numpy as jnp
        import numpy as np
        D = 256
        I = 128
        E = 32
        K = 4
        T = 2 * 512
        C = 2 * T * K // E
        X = x.reshape(-1, D)
        logits = (X @ gate_w.T).astype(jnp.float32)
        scores = jax.nn.sigmoid(logits)
        _, idx = jax.lax.top_k(scores + bias[None, :], K)
        w = jnp.take_along_axis(scores, idx, axis=-1)
        w = w / jnp.clip(jnp.sum(w, axis=-1, keepdims=True), 1e-12, None)
        w = w.astype(x.dtype)
        eid = idx.reshape(-1)
        onehot = (eid[:, None] == jnp.arange(E)[None, :]).astype(jnp.int32)
        pos = jnp.take_along_axis(jnp.cumsum(onehot, axis=0) - 1, eid[:, None], axis=1)[:, 0]
        valid = pos < C
        posc = jnp.minimum(pos, C - 1)
        Xrep = jnp.repeat(X, K, axis=0)
        xe = jnp.zeros((E, C, D), x.dtype).at[eid, posc].add(jnp.where(valid[:, None], Xrep, jnp.zeros((), x.dtype)))
        h = jax.nn.silu(jnp.einsum('ecd,edi->eci', xe, W1)) * jnp.einsum('ecd,edi->eci', xe, W3)
        ye = jnp.einsum('eci,eid->ecd', h, W2)
        gflat = jnp.where(valid, w.reshape(-1), jnp.zeros((), x.dtype))
        yrows = ye[eid, posc] * gflat[:, None]
        out = yrows.reshape(-1, K, D).sum(axis=1)
        out = out + jax.nn.silu(X @ sw1.T) * (X @ sw3.T) @ sw2.T
        return out.reshape(x.shape)
    x = L0_attn_x
    xn = _layernorm(x, axis=-1)
    s = _L0_attn_ref(xn, L0_attn_qkv_w, L0_attn_qkv_b, L0_attn_rq_w, L0_attn_rq_b, L0_attn_rkv_w, L0_attn_rkv_b, L0_attn_rout_w, L0_attn_rout_b, L0_attn_out_w, L0_attn_out_b, L0_attn_gl_w, L0_attn_gr_w)
    g = _silu(_L0_ffn_ref(xn, L0_ffn_W_fc, L0_ffn_ln_w, L0_ffn_ln_b, L0_ffn_W_proj))
    x = x + s * g
    xn = _layernorm(x, axis=-1)
    s = _L1_attn_ref(xn, L1_attn_fwd_in_proj_w, L1_attn_fwd_conv_w, L1_attn_fwd_conv_b, L1_attn_fwd_x_proj_w, L1_attn_fwd_dt_proj_w, L1_attn_fwd_dt_proj_b, L1_attn_fwd_A_log, L1_attn_fwd_D, L1_attn_fwd_out_proj_w, L1_attn_bwd_in_proj_w, L1_attn_bwd_conv_w, L1_attn_bwd_conv_b, L1_attn_bwd_x_proj_w, L1_attn_bwd_dt_proj_w, L1_attn_bwd_dt_proj_b, L1_attn_bwd_A_log, L1_attn_bwd_D, L1_attn_bwd_out_proj_w, L1_attn_ln_gamma, L1_attn_ln_beta)
    g = _silu(_L1_ffn_ref(xn, L1_ffn_gate_w, L1_ffn_bias, L1_ffn_W1, L1_ffn_W3, L1_ffn_W2, L1_ffn_sw1, L1_ffn_sw3, L1_ffn_sw2))
    x = x + s * g
    return x

_drawn_inputs = setup_inputs


def setup_inputs(seed=0):
    import zlib

    import numpy as np

    out = dict(_drawn_inputs(seed))
    spreads = {'L0_attn_qkv_b': (0.0, 0.1),
     'L0_attn_rq_b': (0.0, 0.8),
     'L0_attn_rkv_b': (0.0, 0.357),
     'L0_attn_rout_b': (0.0, 0.1),
     'L0_attn_out_b': (0.0, 0.1),
     'L0_ffn_ln_w': (1.0, 0.2),
     'L0_ffn_ln_b': (0.0, 0.1),
     'L1_attn_fwd_conv_b': (0.0, 0.8),
     'L1_attn_fwd_D': (1.0, 0.6),
     'L1_attn_bwd_conv_b': (0.0, 0.8),
     'L1_attn_bwd_D': (1.0, 0.6),
     'L1_attn_ln_gamma': (1.0, 0.6),
     'L1_attn_ln_beta': (0.0, 0.8),
     'L1_ffn_bias': (0.0, 0.8)}
    factors = {'L0_attn_rq_w': 8.0,
     'L0_attn_rkv_w': 7.972,
     'L0_attn_gl_w': 8.0,
     'L0_attn_gr_w': 8.0,
     'L1_attn_fwd_in_proj_w': 8.0,
     'L1_attn_fwd_conv_w': 8.0,
     'L1_attn_fwd_x_proj_w': 8.0,
     'L1_attn_fwd_dt_proj_w': 8.0,
     'L1_attn_fwd_dt_proj_b': 28.111,
     'L1_attn_fwd_A_log': 8.0,
     'L1_attn_fwd_out_proj_w': 8.0,
     'L1_attn_bwd_in_proj_w': 8.0,
     'L1_attn_bwd_conv_w': 8.0,
     'L1_attn_bwd_x_proj_w': 8.0,
     'L1_attn_bwd_dt_proj_w': 8.0,
     'L1_attn_bwd_dt_proj_b': 23.079,
     'L1_attn_bwd_A_log': 8.0,
     'L1_attn_bwd_out_proj_w': 8.0,
     'L1_ffn_gate_w': 8.0,
     'L1_ffn_W1': 8.0,
     'L1_ffn_W3': 8.0,
     'L1_ffn_W2': 8.0,
     'L1_ffn_sw1': 8.0,
     'L1_ffn_sw3': 8.0,
     'L1_ffn_sw2': 8.0}
    for name, (base, spread) in spreads.items():
        noise = np.random.default_rng([zlib.crc32(name.encode()), seed]).standard_normal(out[name].shape)
        drawn = base * np.exp(spread * noise) if base else spread * noise
        out[name] = jnp.asarray(drawn.astype(out[name].dtype))
    for name, factor in factors.items():
        out[name] = (out[name] * factor).astype(out[name].dtype)
    return out
```

```python
import concourse.bass as bass
from concourse import mybir
from contextlib import ExitStack

import numpy as np

F32 = mybir.dt.float32
BF16 = mybir.dt.bfloat16
U32 = mybir.dt.uint32
ALU = mybir.AluOpType
ACT = mybir.ActivationFunctionType
AX = mybir.AxisListType

P = 128
B, S, D = 16, 512, 256
NBLK = S // P
KD = D // P
H, HD = 16, 16
G = 4
HG = H // G
LAT, LH = 64, 4
CH = S // LAT
HID = 1024
E, TOPK, CAP, I = 32, 4, 256, 128
VW = HD + 1
LN_EPS = 1e-5
NEG = -1e9
FAR = 1048576.0


DCHAIN = 86
MFIRST, MCHAIN = 18, 43


class Signal:

    def __init__(self, sem, per, first=0):
        self.sem, self.per, self.first, self.n = sem, per, first, 0

    def raised_by(self, ins, by=1):
        ins.then_inc(self.sem, by)
        self.n += by
        return ins

    def value(self, i, n):
        return i * self.per + (self.first + n)

    def whole(self):
        assert self.n == self.per, (str(self.sem), self.n, self.per)


def layer0(nc, A, X1, XNT, XE, slots_dram, gates_dram):
    ctx = ExitStack()
    with ctx:
        sb = lambda name, shape, dt=F32: ctx.enter_context(nc.sbuf_tensor("sb_" + name, shape, dt))
        sem = lambda name: ctx.enter_context(nc.semaphore(name))

        wq = sb("wq", [P, KD, G * HG * 32])
        wk = sb("wk", [P, KD, G * HG * 32])
        bq = sb("bq", [P, HG])
        bk = sb("bk", [P, HG])
        wv = sb("wv", [P, KD, D])
        bv = sb("bv", [1, D])
        wrq = sb("wrq", [P, KD, P])
        brq = sb("brq", [P, 1])
        wrk = sb("wrk", [P, KD, P])
        brk = sb("brk", [P, 1])
        wrv = sb("wrv", [P, KD, LAT])
        brv = sb("brv", [1, LAT])
        wro = sb("wro", [LAT, D])
        bro = sb("bro", [1, D])
        wo = sb("wo", [P, KD, D])
        bo = sb("bo", [1, D])
        gl = sb("gl", [P, HD])
        gr = sb("gr", [P, HD])
        wfc = sb("wfc", [P, KD, HID])
        wpj = sb("wpj", [P, HID // P, D])
        lnw = sb("lnw", [P, HID])
        lnb = sb("lnb", [P, HID])
        gate_h = sb("gate_h", [P, KD, E], BF16)
        gate_w = sb("gate_w", [P, KD, E])
        ebias = sb("ebias", [P, E])
        ident = sb("ident", [P, P])
        ident_h = sb("ident_h", [P, P], BF16)
        ones_row = sb("ones_row", [1, P])
        ones_sq = sb("ones_sq", [P, P])
        ones_h = sb("ones_h", [P, P], BF16)
        before = sb("before", [P, P], BF16)
        mask = sb("mask", [P, 2, 2, P], BF16)
        lmask = sb("lmask", [P, NBLK, LH, LAT], BF16)
        slot_of = sb("slot_of", [P, G])
        row_ok = sb("row_ok", [P, 1])
        lat_ok = sb("lat_ok", [P, 1])
        iota_e = sb("iota_e", [P, E])
        iota_s = sb("iota_s", [P, E])
        half = sb("half", [P, NBLK])
        absum = sb("absum", [P, 4])
        thr = sb("thr", [P, 2])
        nthr = sb("nthr", [P, 2])
        zero = sb("zero", [P, 2048])

        xa = sb("xa", [P, NBLK, D])
        xr = sb("xr", [P, NBLK, D])
        bnst = sb("bnst", [P, NBLK, 6])
        mv = sb("mv", [P, NBLK, 2])
        rstd = sb("rstd", [P, NBLK])
        xn = sb("xn", [P, NBLK, D])
        xnT = sb("xnT", [P, KD, S])
        pooled = sb("pooled", [P, KD, LAT])
        qT = sb("qT", [P, HG, S])
        kT = sb("kT", [P, HG, S])
        qX = sb("qX", [P, HG, G, S])
        rqX = sb("rqX", [P, G, S])
        vv = sb("vv", [P, NBLK, H, VW])
        rqT = sb("rqT", [P, S])
        rkT = sb("rkT", [P, LAT])
        rvv = sb("rvv", [LAT, LH, VW])
        nmax = sb("nmax", [P, 2, G])
        pr = sb("pr", [P, 2, G, 2 * P])
        prT = sb("prT", [P, 2, G, 2, P])
        rinv = sb("rinv", [P, H])
        linv = sb("linv", [P, LH])
        loc = sb("loc", [P, H, HD])
        lat = sb("lat", [P, LH, HD])
        latT = sb("latT", [LAT, P])
        rem = sb("rem", [P, H, HD])
        t1 = sb("t1", [P, H, HD])
        t2 = sb("t2", [P, H, HD])
        zg = sb("zg", [P, H])
        eg = sb("eg", [P, H])
        mix = sb("mix", [P, H, HD])
        mixT = sb("mixT", [P, KD, P])
        s0 = sb("s0", [P, NBLK, D])
        hid = sb("hid", [P, 2, HID])
        hst = sb("hst", [P, 2, 2, 6])
        hmv = sb("hmv", [P, 2, 2])
        hrs = sb("hrs", [P, 2])
        hidT = sb("hidT", [P, 2, HID // P, P])
        ff = sb("ff", [P, NBLK, D])
        x1 = sb("x1", [P, NBLK, D])
        xn2 = sb("xn2", [P, NBLK, D])
        xn2T = sb("xn2T", [P, KD, S])
        esc = sb("esc", [P, NBLK, E])
        sc = sb("sc", [P, NBLK, E])
        sbias = sb("sbias", [P, NBLK, E])
        top = sb("top", [P, NBLK, 8])
        topi = sb("topi", [P, NBLK, 8], U32)
        topf = sb("topf", [P, NBLK, TOPK])
        hot = sb("hot", [P, NBLK, TOPK, E])
        tmp = sb("tmp", [P, NBLK, TOPK, E])
        sel = sb("sel", [P, NBLK, E])
        sel_h = sb("sel_h", [P, NBLK, E], BF16)
        taken = sb("taken", [P, E])
        pos = sb("pos", [P, NBLK, E])
        over = sb("over", [P, NBLK, E])
        slotf = sb("slotf", [P, NBLK, TOPK])
        slot = sb("slot", [P, NBLK, TOPK], U32)
        gw = sb("gw", [P, NBLK, TOPK])
        gsum = sb("gsum", [P, NBLK])
        keep = sb("keep", [P, NBLK, TOPK])
        gout = sb("gout", [P, NBLK, TOPK])

        psS = ctx.enter_context(nc.psum_tensor("psS", [P, 4, 512], F32))
        psT = ctx.enter_context(nc.psum_tensor("psT", [P, 1024], F32))
        po = ctx.enter_context(nc.psum_tensor("po", [P, 2, 512], F32))

        w_in = sem("w_in")
        made = sem("made")
        prep = sem("prep")
        summed = sem("summed")
        zeroed = sem("zeroed")
        plain = [(wq, "wq"), (wk, "wk"), (wv, "wv"), (wrq, "wrq"), (wrk, "wrk"), (wrv, "wrv"),
                 (wo, "wo"), (wfc, "wfcT"), (wpj, "wpjT"), (gate_h, "gateT")]
        flat = [(bq, "bq"), (bk, "bk"), (brq, "brq"), (brk, "brk"), (wro, "wro")]
        rows = [(bv, "bv"), (brv, "brv"), (bro, "bro"), (bo, "bo")]
        spread = [(gl, "gl"), (gr, "gr"), (lnw, "lnw"), (lnb, "lnb"), (ebias, "ebias")]
        NLOAD = len(plain) + len(flat) + len(rows) + len(spread)
        with nc.Block() as block:
            @block.sync
            def _(sp):
                for t, n in plain:
                    sp.dma_start(t[:, :, :], A[n].rearrange("(t p) n -> p t n", p=P)).then_inc(w_in, 16)
                for t, n in flat:
                    sp.dma_start(t[:, :], A[n]).then_inc(w_in, 16)
                for t, n in rows:
                    sp.dma_start(t[:, :], A[n].unsqueeze(0)).then_inc(w_in, 16)
                for t, n in spread:
                    sp.dma_start(t[:, :], A[n].partition_broadcast(P)).then_inc(w_in, 16)
                sp.wait_ge(made, 1)
                sp.dma_start(XE.rearrange("(p n) d -> p n d", p=P)[:, 0:8, :],
                             zero[:, :].rearrange("p (n d) -> p n d", d=D)).then_inc(zeroed, 16)
                for k in range(1, E * CAP // P // 8):
                    sp.dma_start(XE.rearrange("(p n) d -> p n d", p=P)[:, 8 * k:8 * k + 8, :],
                                 zero[:, :].rearrange("p (n d) -> p n d", d=D)).then_inc(zeroed, 16)
                sp.wait_ge(zeroed, 16 * (E * CAP // P // 8))
                sp.wait_ge(w_in, 16 * NLOAD)

            @block.gpsimd
            def _(pool):
                g = nc.gpsimd
                m = [0]

                def link(ins):
                    ins.then_inc(made, 1)
                    m[0] += 1
                    pool.wait_ge(made, m[0])

                link(g.memset(zero[:, :], 0.0))
                link(g.memset(ones_sq[:, :], 1.0))
                link(g.memset(ones_h[:, :], 1.0))
                link(g.memset(ones_row[:, :], 1.0))
                link(g.memset(ident[:, :], 0.0))
                link(g.affine_select(out=ident[:, :], in_=ident[:, :], compare_op=ALU.not_equal, fill=1.0,
                                     base=0, pattern=[[-1, P]], channel_multiplier=1))
                link(g.memset(ident_h[:, :], 0.0))
                link(g.affine_select(out=ident_h[:, :], in_=ident_h[:, :], compare_op=ALU.not_equal, fill=1.0,
                                     base=0, pattern=[[-1, P]], channel_multiplier=1))
                link(g.affine_select(out=before[:, :], in_=ones_h[:, :], compare_op=ALU.is_gt, fill=0.0,
                                     base=0, pattern=[[1, P]], channel_multiplier=-1))
                link(g.memset(mask[:, :, :, :], 0.0))
                for r in range(2):
                    link(g.affine_select(out=mask[:, r, 0, :], in_=mask[:, r, 0, :], compare_op=ALU.is_ge, fill=NEG,
                                         base=0, pattern=[[1, P]], channel_multiplier=-1))
                    link(g.affine_select(out=mask[:, r, 0, :], in_=mask[:, r, 0, :], compare_op=ALU.is_gt, fill=NEG,
                                         base=0, pattern=[[1, P]], channel_multiplier=0))
                    link(g.affine_select(out=mask[:, r, 1, :], in_=mask[:, r, 1, :], compare_op=ALU.is_gt, fill=NEG,
                                         base=0, pattern=[[-1, P]], channel_multiplier=1))
                link(g.memset(lmask[:, :, :, :], 0.0))
                for j in range(NBLK):
                    link(g.affine_select(out=lmask[:, j, :, :], in_=lmask[:, j, :, :], compare_op=ALU.is_gt, fill=NEG,
                                         base=j * P - (CH - 1), pattern=[[0, LH], [-CH, LAT]], channel_multiplier=1))
                link(g.affine_select(out=slot_of[:, :], in_=ones_sq[:, 0:G], compare_op=ALU.is_ge, fill=0.0,
                                     base=0, pattern=[[-32, G]], channel_multiplier=1))
                link(g.affine_select(out=slot_of[:, :], in_=slot_of[:, :], compare_op=ALU.is_ge, fill=0.0,
                                     base=31, pattern=[[32, G]], channel_multiplier=-1))
                link(g.affine_select(out=row_ok[:, :], in_=ones_sq[:, 0:1], compare_op=ALU.is_gt, fill=0.0,
                                     base=0, pattern=[[0, 1]], channel_multiplier=1))
                link(g.affine_select(out=lat_ok[:, :], in_=ones_sq[:, 0:1], compare_op=ALU.is_gt, fill=0.0,
                                     base=-(CH - 1), pattern=[[0, 1]], channel_multiplier=1))
                link(g.iota(iota_e[:, :], [[1, E]], base=0, channel_multiplier=0,
                            allow_small_or_imprecise_dtypes=True))
                link(g.iota(iota_s[:, :], [[CAP, E]], base=0, channel_multiplier=0,
                            allow_small_or_imprecise_dtypes=True))
                link(g.memset(half[:, :], -0.5))
                link(g.memset(vv[:, :, :, HD:VW], 1.0))
                link(g.memset(rvv[:, :, HD:VW], 1.0))
                link(g.memset(taken[:, :], 0.0))
                link(g.memset(prT[:, :, :, :, :], 0.0))

            @block.vector
            def _(dve):
                v = nc.vector
                n = [0]

                def link(ins):
                    ins.then_inc(prep, 1)
                    n[0] += 1
                    dve.wait_ge(prep, n[0])

                dve.wait_ge(w_in, 16 * NLOAD)
                link(v.tensor_copy(gate_w[:, :, :], gate_h[:, :, :]))
                link(v.tensor_scalar(bq[:, :], bq[:, :], 0.25, None, ALU.mult))
                link(v.tensor_scalar(brq[:, :], brq[:, :], 0.25, None, ALU.mult))
                for k, w in enumerate((wfc, wpj)):
                    link(v.tensor_reduce(absum[:, k:k + 1], w[:, :, :], axis=AX.XY, op=ALU.add,
                                         apply_absolute_value=True))
                dve.wait_ge(summed, 1)
                link(v.tensor_scalar(thr[:, :], psT[:, 0:2], 1.0 / (HID * D), 1e-6, ALU.mult, ALU.add))
                link(v.tensor_scalar(nthr[:, :], thr[:, :], -0.5, None, ALU.mult))
                link(v.tensor_scalar(thr[:, :], thr[:, :], 0.5, None, ALU.mult))
                for k, (w, other) in enumerate(((wfc, hid), (wpj, hidT))):
                    o = other[:, :, :] if k == 0 else other[:, :, :, :].rearrange("p a b c -> p (a b c)")
                    o = o if k == 0 else o.rearrange("p (t n) -> p t n", n=D)
                    link(v.tensor_scalar(o, w[:, :, :], nthr[:, k:k + 1], None, ALU.is_lt))
                    link(v.scalar_tensor_tensor(w[:, :, :], w[:, :, :], thr[:, k:k + 1], o,
                                                ALU.is_gt, ALU.subtract))

            @block.tensor
            def _(pe):
                pe.wait_ge(made, 2)
                pe.wait_ge(prep, 5)
                nc.tensor.matmul(psT[:, 0:2], ones_sq[:, :], absum[:, 0:2], start=True, stop=True).then_inc(summed, 1)

        NU = NBLK * (HG + 1)
        sig = lambda name, per, first=0: Signal(sem(name), per, first)
        xa_in = sig("xa_in", 16)
        xr_in = sig("xr_in", 16)
        xa_free = sig("xa_free", 1, 1)
        xr_free = sig("xr_free", 1, 1)
        var_ok = sig("var_ok", 1)
        rstd_ok = sig("rstd_ok", 2)
        xn_ok = sig("xn_ok", 1)
        xnT_tr = sig("xnT_tr", 1)
        xnT_ok = sig("xnT_ok", 1)
        pooled_ok = sig("pooled_ok", 1)
        proj = sig("proj", 14)
        proj_a = sig("proj_a", 11)
        proj_v = sig("proj_v", 4)
        qx_ok = sig("qx_ok", HG + 1)
        s_ok = sig("s_ok", NU)
        max_ok = sig("max_ok", NU)
        exp_ok = sig("exp_ok", NU)
        tr_ok = sig("tr_ok", NU)
        cp_ok = sig("cp_ok", NU)
        pv_ok = sig("pv_ok", NU)
        lat_done = sig("lat_done", NBLK)
        gate_in = sig("gate_in", NBLK)
        gate_ok = sig("gate_ok", NBLK)
        mix_ok = sig("mix_ok", NBLK)
        post_t = sig("post_t", 4 * NBLK)
        post_cp = sig("post_cp", 4 * NBLK)
        h_ok = sig("h_ok", NBLK)
        gelu_ok = sig("gelu_ok", NBLK)
        hvar_ok = sig("hvar_ok", NBLK)
        hrs_ok = sig("hrs_ok", 2 * NBLK)
        hnorm_ok = sig("hnorm_ok", NBLK)
        haff_ok = sig("haff_ok", 2 * NBLK)
        ht_tr = sig("ht_tr", NBLK)
        ht_ok = sig("ht_ok", NBLK)
        pj_ok = sig("pj_ok", NBLK)
        ff_ok = sig("ff_ok", NBLK)
        silu_ok = sig("silu_ok", 1)
        x1_ok = sig("x1_ok", 1)
        var2_ok = sig("var2_ok", 1)
        rstd2_ok = sig("rstd2_ok", 2)
        xn2_ok = sig("xn2_ok", 1)
        xn2T_tr = sig("xn2T_tr", 1)
        xn2T_ok = sig("xn2T_ok", 1)
        logit_ok = sig("logit_ok", 1)
        esc_ok = sig("esc_ok", 1)
        sel_ok = sig("sel_ok", 1)
        count_ok = sig("count_ok", 1)
        slot_ok = sig("slot_ok", 1)
        stored = sig("stored", 16 * 4, 16 * 4)
        scattered = sig("scattered", 16 * NBLK * TOPK, 16 * NBLK * TOPK)
        dchain = sig("dchain", DCHAIN)
        alone_p, alone_v, alone_t = sem("alone_p"), sem("alone_v"), sem("alone_t")

        def span(u):
            if u % (HG + 1) == HG:
                return 0, LAT
            j = u // (HG + 1)
            return (0, P) if j == 0 else ((j - 1) * P, 2 * P)

        def scored(u):
            nk = span(u)[1]
            if nk == LAT:
                return psS[:, 2 * (u % 2), 0:LH * LAT].rearrange("p (h n) -> p h n", n=LAT)
            both = psS[:, 2 * (u % 2):2 * (u % 2) + 2, :].rearrange("p c (h n) -> p (c h) n", n=2 * P)
            return both[:, :, 2 * P - nk:2 * P]

        with nc.Block() as block:
            @block.sync
            def _(sp):
                sp.sem_inc(stored.sem, 16 * 4)
                with sp.Fori(0, B) as b:
                    sp.wait_ge(xa_free.sem, xa_free.value(b, 0))
                    sp.dma_start(xa[:, :, :], A["x"][bass.ds(b, 1), :, :].rearrange("a (j p) d -> p (a j) d", p=P)
                                 ).then_inc(xa_in.sem, 16)
                    sp.wait_ge(xr_free.sem, xr_free.value(b, 0))
                    sp.dma_start(xr[:, :, :], A["x"][bass.ds(b, 1), :, :].rearrange("a (j p) d -> p (a j) d", p=P)
                                 ).then_inc(xr_in.sem, 16)
                    sp.wait_ge(x1_ok.sem, x1_ok.value(b, 1))
                    sp.dma_start(X1[bass.ds(b, 1), :, :].rearrange("a (j p) d -> p (a j) d", p=P), x1[:, :, :]
                                 ).then_inc(stored.sem, 16)
                    sp.wait_ge(xn2T_ok.sem, xn2T_ok.value(b, 1))
                    sp.dma_start(XNT[bass.ds(b, 1), :, :].rearrange("a (t p) s -> p (a t) s", p=P), xn2T[:, :, :]
                                 ).then_inc(stored.sem, 16)
                    sp.wait_ge(slot_ok.sem, slot_ok.value(b, 1))
                    sp.dma_start(slots_dram[bass.ds(b, 1), :, :].rearrange("a p n -> (a p) n"),
                                 slot[:, :, :].rearrange("p a b -> p (a b)")).then_inc(stored.sem, 16)
                    sp.dma_start(gates_dram[bass.ds(b, 1), :, :].rearrange("a p n -> (a p) n"),
                                 gout[:, :, :].rearrange("p a b -> p (a b)")).then_inc(stored.sem, 16)
                sp.wait_ge(stored.sem, 16 * 4 * (B + 1))

            @block.gpsimd
            def _(pool):
                g = nc.gpsimd
                for k in range(NBLK * TOPK):
                    g.dma_start(zero[:, P * k:P * k + 8], ident[:, 0:8]).then_inc(scattered.sem, 16)
                with pool.Fori(0, B) as b:
                    def rsqrt(out, var, ready, ready_n, sig_):
                        pool.wait_ge(ready.sem, ready.value(b, ready_n))
                        pool.sem_inc(alone_p, 1)
                        sig_.raised_by(g.tensor_scalar(out, var, LN_EPS, None, ALU.add))
                        pool.wait_ge(sig_.sem, sig_.value(b, sig_.n))
                        w = out.shape[1]
                        sig_.raised_by(g.tensor_tensor(out, out, half[:, 0:w], ALU.pow))

                    rsqrt(rstd[:, :], mv[:, :, 1], var_ok, 1, rstd_ok)
                    for n in range(HG + 1):
                        pool.wait_ge(proj_a.sem, proj_a.value(b, n + 1 if n < HG else 2 * HG + 1))
                        pool.sem_inc(alone_p, 1)
                        for h in range(G):
                            src, dst = (qT[:, n, :], qX[:, n, h, :]) if n < HG else (rqT[:, :], rqX[:, h, :])
                            ins = g.tensor_scalar(dst, src, slot_of[:, h:h + 1], None, ALU.mult)
                        qx_ok.raised_by(ins)
                    for j in range(NBLK):
                        rsqrt(hrs[:, j % 2:j % 2 + 1], hmv[:, j % 2, 1:2], hvar_ok, j + 1, hrs_ok)
                        pool.wait_ge(hnorm_ok.sem, hnorm_ok.value(b, j + 1))
                        haff_ok.raised_by(g.tensor_tensor(hid[:, j % 2, :], hid[:, j % 2, :], lnw[:, :], ALU.mult))
                        pool.wait_ge(haff_ok.sem, haff_ok.value(b, haff_ok.n))
                        haff_ok.raised_by(g.tensor_tensor(hid[:, j % 2, :], hid[:, j % 2, :], lnb[:, :], ALU.add))
                    rsqrt(rstd[:, :], mv[:, :, 1], var2_ok, 1, rstd2_ok)
                    pool.wait_ge(slot_ok.sem, slot_ok.value(b, 1))
                    pool.sem_inc(alone_p, 1)
                    for j in range(NBLK):
                        for k in range(TOPK):
                            g.indirect_dma_start(
                                out=XE, out_offset=bass.IndirectOffsetOnAxis(ap=slot[:, j, k:k + 1], axis=0),
                                in_=xn2[:, j, :], in_offset=None, bounds_check=E * CAP - 1, oob_is_err=False,
                            ).then_inc(scattered.sem, 16)
                pool.wait_ge(scattered.sem, 16 * NBLK * TOPK * (B + 1))
                for s in (qx_ok, rstd_ok, hrs_ok, haff_ok, rstd2_ok):
                    s.whole()

            @block.scalar
            def _(act):
                a = nc.scalar
                with act.Fori(0, B) as b:
                    def wait(s, n):
                        act.wait_ge(s.sem, s.value(b, n))

                    wait(xnT_tr, 1)
                    xnT_ok.raised_by(a.activation(xnT[:, :, :].rearrange("p t s -> p (t s)"), psT[:, :], ACT.Copy))
                    for n in range(8):
                        wait(proj, n + 1)
                        dst, bias, sc_ = (qT, bq, 0.25) if n < HG else (kT, bk, 1.0)
                        g_ = n % HG
                        proj_a.raised_by(a.activation(dst[:, g_, :], psS[:, n % 4, :], ACT.Identity,
                                                      bias=bias[:, g_:g_ + 1], scale=sc_))
                    wait(proj, 13)
                    proj_a.raised_by(a.activation(rqT[:, :], psS[:, 0, :], ACT.Identity, bias=brq[:, 0:1], scale=0.25))
                    wait(proj, 14)
                    proj_a.raised_by(a.activation(rkT[:, :], psS[:, 1, 0:LAT], ACT.Identity,
                                                  bias=brk[:, 0:1], scale=1.0))
                    proj_a.raised_by(a.activation(rvv[:, :, 0:HD],
                                                  psS[0:LAT, 1, LAT:2 * LAT].rearrange("p (h d) -> p h d", d=HD),
                                                  ACT.Copy))
                    for u in range(NU):
                        k0, nk = span(u)
                        at = 2 * P - nk if nk > LAT else 0
                        wait(max_ok, u + 1)
                        if u >= 2:
                            wait(tr_ok, u - 1)
                        for h in range(G):
                            ins = a.activation(pr[:, u % 2, h, at:at + nk], scored(u)[:, h, :], ACT.Exp,
                                               bias=nmax[:, u % 2, h:h + 1], scale=1.0)
                        exp_ok.raised_by(ins)
                        if u > HG and u % (HG + 1) == 3:
                            q = u // (HG + 1)
                            wait(gate_in, q)
                            gate_ok.raised_by(a.activation(eg[:, :], zg[:, :], ACT.Exp, scale=-1.0))
                    wait(gate_in, NBLK)
                    gate_ok.raised_by(a.activation(eg[:, :], zg[:, :], ACT.Exp, scale=-1.0))

                    def gelu(j):
                        wait(h_ok, j + 1)
                        if j >= 2:
                            wait(ht_tr, j - 1)
                        gelu_ok.raised_by(a.activation(
                            hid[:, j % 2, :].rearrange("p (c n) -> p c n", c=2),
                            psS[:, 2 * (j % 2):2 * (j % 2) + 2, :], ACT.Gelu))

                    gelu(0)
                    gelu(1)
                    for j in range(NBLK):
                        wait(ht_tr, j + 1)
                        if j >= 2:
                            wait(pj_ok, j - 1)
                        ht_ok.raised_by(a.activation(hidT[:, j % 2, :, :].rearrange("p t n -> p (t n)"),
                                                     psT[:, :], ACT.Copy))
                        if j + 2 < NBLK:
                            gelu(j + 2)
                    wait(ff_ok, NBLK)
                    silu_ok.raised_by(a.activation(ff[:, :, :], ff[:, :, :], ACT.Silu))
                    wait(xn2T_tr, 1)
                    act.wait_ge(stored.sem, stored.value(b, 0))
                    xn2T_ok.raised_by(a.activation(xn2T[:, :, :].rearrange("p t s -> p (t s)"), psT[:, :], ACT.Copy))
                    wait(logit_ok, 1)
                    esc_ok.raised_by(a.activation(esc[:, :, :].rearrange("p a b -> p (a b)"), po[:, 0, 0:NBLK * E],
                                                  ACT.Exp, scale=-1.0))
                for s in (xnT_ok, proj_a, exp_ok, gate_ok, gelu_ok, ht_ok, silu_ok, xn2T_ok, esc_ok):
                    s.whole()

            @block.vector
            def _(dve):
                v = nc.vector
                xa_free.n = 0
                dve.sem_inc(xa_free.sem, 1)
                dve.sem_inc(xr_free.sem, 1)
                with dve.Fori(0, B) as b:
                    def wait(s, n):
                        dve.wait_ge(s.sem, s.value(b, n))

                    def link(ins):
                        dchain.raised_by(ins)
                        wait(dchain, dchain.n)

                    def tell(ins, s):
                        s.raised_by(ins)
                        wait(s, s.n)

                    def stats(src, ready):
                        for j in range(NBLK):
                            ins = v.bn_stats(bnst[:, j, :], src[:, j, :])
                        link(ins)
                        for j in range(NBLK):
                            if j == 0:
                                dve.sem_inc(alone_v, 1)
                            ins = v.bn_aggr(mv[:, j, :], bnst[:, j, :])
                        tell(ins, ready)

                    def normalize(dst, src, ready):
                        for j in range(NBLK):
                            ins = v.tensor_scalar(dst[:, j, :], src[:, j, :], mv[:, j, 0:1], rstd[:, j:j + 1],
                                                  ALU.subtract, ALU.mult)
                        return ins

                    wait(xa_in, 16)
                    stats(xa, var_ok)
                    wait(rstd_ok, 2)
                    tell(normalize(xn, xa, xn_ok), xn_ok)
                    xa_free.n += 1
                    dve.sem_inc(xa_free.sem, 1)
                    wait(xnT_ok, 1)
                    link(v.tensor_reduce(pooled[:, :, :], xnT[:, :, :].rearrange("p t (l c) -> p t l c", c=CH),
                                         axis=AX.X, op=ALU.add))
                    tell(v.tensor_scalar(pooled[:, :, :], pooled[:, :, :], 1.0 / CH, None, ALU.mult), pooled_ok)
                    for j in range(NBLK):
                        wait(proj, 9 + j)
                        tell(v.tensor_copy(vv[:, j, :, 0:HD],
                                           psS[:, j, 0:D].rearrange("p (h d) -> p h d", d=HD)), proj_v)

                    def maxima(u):
                        wait(s_ok, u + 1)
                        tell(v.tensor_reduce(nmax[:, u % 2, :], scored(u), axis=AX.X, op=ALU.max,
                                             negate=True), max_ok)

                    def copy_probs(u):
                        k0, nk = span(u)
                        wait(tr_ok, u + 1)
                        if u >= 2:
                            wait(pv_ok, u - 1)
                        if nk == LAT:
                            ins = v.tensor_copy(prT[0:LAT, u % 2, :, 0, :],
                                                psT[0:LAT, :].rearrange("p (h k q) -> p h k q", h=G, k=2)[:, :, 0, :])
                        elif nk == P:
                            ins = v.tensor_copy(prT[:, u % 2, :, 1, :],
                                                psT[:, :].rearrange("p (h k q) -> p h k q", h=G, k=2)[:, :, 1, :])
                        else:
                            ins = v.tensor_copy(prT[:, u % 2, :, :, :].rearrange("p h k q -> p (h k q)"), psT[:, :])
                        tell(ins, cp_ok)

                    def post(q, stage):
                        if stage == 0:
                            wait(pv_ok, (HG + 1) * (q + 1))
                            o = po[:, q % 2, 0:H * VW].rearrange("p (h d) -> p h d", d=VW)
                            l = po[:, q % 2, H * VW:(H + LH) * VW].rearrange("p (h d) -> p h d", d=VW)
                            link(v.reciprocal(rinv[:, :], o[:, :, HD]))
                            link(v.reciprocal(linv[:, :], l[:, :, HD]))
                            if q == 0:
                                link(v.tensor_scalar(rinv[:, :], rinv[:, :], row_ok[:, 0:1], None, ALU.mult))
                                link(v.tensor_scalar(linv[:, :], linv[:, :], lat_ok[:, 0:1], None, ALU.mult))
                            link(v.tensor_tensor(loc[:, :, :], o[:, :, 0:HD],
                                                 rinv[:, :].unsqueeze(2).to_broadcast([P, H, HD]), ALU.mult))
                            tell(v.tensor_tensor(lat[:, :, :], l[:, :, 0:HD],
                                                 linv[:, :].unsqueeze(2).to_broadcast([P, LH, HD]), ALU.mult), lat_done)
                        if stage == 1:
                            wait(post_t, 4 * q + 1)
                            tell(v.tensor_copy(latT[:, :], psT[0:LAT, 0:P]), post_cp)
                        if stage == 2:
                            wait(post_t, 4 * q + 2)
                            tell(v.tensor_copy(rem[:, :, :].rearrange("p h d -> p (h d)"), psT[:, 0:D]), post_cp)
                            link(v.tensor_tensor(t1[:, :, :], loc[:, :, :],
                                                 gl[:, :].unsqueeze(1).to_broadcast([P, H, HD]), ALU.mult))
                            link(v.tensor_tensor(t2[:, :, :], rem[:, :, :],
                                                 gr[:, :].unsqueeze(1).to_broadcast([P, H, HD]), ALU.mult))
                            link(v.tensor_tensor(t1[:, :, :], t1[:, :, :], t2[:, :, :], ALU.add))
                            tell(v.tensor_reduce(zg[:, :], t1[:, :, :], axis=AX.X, op=ALU.add), gate_in)
                        if stage == 3:
                            wait(gate_ok, q + 1)
                            link(v.tensor_scalar(eg[:, :], eg[:, :], 1.0, None, ALU.add))
                            link(v.reciprocal(eg[:, :], eg[:, :]))
                            link(v.tensor_tensor(t1[:, :, :], loc[:, :, :], rem[:, :, :], ALU.subtract))
                            link(v.tensor_tensor(t1[:, :, :], t1[:, :, :],
                                                 eg[:, :].unsqueeze(2).to_broadcast([P, H, HD]), ALU.mult))
                            tell(v.tensor_tensor(mix[:, :, :], t1[:, :, :], rem[:, :, :], ALU.add), mix_ok)
                            wait(post_t, 4 * q + 3)
                            tell(v.tensor_copy(mixT[:, :, :].rearrange("p t n -> p (t n)"), psT[:, 0:D]), post_cp)
                        if stage == 4:
                            wait(post_t, 4 * q + 4)
                            tell(v.tensor_copy(s0[:, q, :], psT[:, 0:D]), post_cp)

                    maxima(0)
                    maxima(1)
                    for u in range(NU):
                        copy_probs(u)
                        if u + 2 < NU:
                            maxima(u + 2)
                        if u > HG:
                            post(u // (HG + 1) - 1, u % (HG + 1))
                    for stage in range(HG + 1):
                        post(NBLK - 1, stage)

                    for j in range(NBLK):
                        wait(gelu_ok, j + 1)
                        link(v.bn_stats(hst[:, j % 2, 0, :], hid[:, j % 2, 0:512]))
                        link(v.bn_stats(hst[:, j % 2, 1, :], hid[:, j % 2, 512:1024]))
                        dve.sem_inc(alone_v, 1)
                        tell(v.bn_aggr(hmv[:, j % 2, :], hst[:, j % 2, :, :].rearrange("p a b -> p (a b)")), hvar_ok)
                        wait(hrs_ok, 2 * j + 2)
                        tell(v.tensor_scalar(hid[:, j % 2, :], hid[:, j % 2, :], hmv[:, j % 2, 0:1],
                                             hrs[:, j % 2:j % 2 + 1], ALU.subtract, ALU.mult), hnorm_ok)
                        if j >= 1:
                            wait(pj_ok, j)
                            tell(v.tensor_copy(ff[:, j - 1, :], po[:, (j - 1) % 2, 0:D]), ff_ok)
                    wait(pj_ok, NBLK)
                    tell(v.tensor_copy(ff[:, NBLK - 1, :], po[:, (NBLK - 1) % 2, 0:D]), ff_ok)

                    wait(silu_ok, 1)
                    wait(xr_in, 16)
                    dve.wait_ge(stored.sem, stored.value(b, 0))
                    dve.wait_ge(scattered.sem, scattered.value(b, 0))
                    link(v.tensor_tensor(s0[:, :, :], s0[:, :, :], ff[:, :, :], ALU.mult))
                    tell(v.tensor_tensor(x1[:, :, :], s0[:, :, :], xr[:, :, :], ALU.add), x1_ok)
                    xr_free.n += 1
                    dve.sem_inc(xr_free.sem, 1)
                    stats(x1, var2_ok)
                    wait(rstd2_ok, 2)
                    tell(normalize(xn2, x1, xn2_ok), xn2_ok)

                    wait(esc_ok, 1)
                    link(v.tensor_scalar(esc[:, :, :], esc[:, :, :], 1.0, None, ALU.add))
                    link(v.reciprocal(sc[:, :, :], esc[:, :, :]))
                    link(v.tensor_tensor(sbias[:, :, :], sc[:, :, :],
                                         ebias[:, :].unsqueeze(1).to_broadcast([P, NBLK, E]), ALU.add))
                    dve.sem_inc(alone_v, 1)
                    for j in range(NBLK):
                        ins = v.max(top[:, j, :], sbias[:, j, :])
                    link(ins)
                    dve.sem_inc(alone_v, 1)
                    for j in range(NBLK):
                        ins = v.max_index(topi[:, j, :], top[:, j, :], sbias[:, j, :])
                    link(ins)
                    link(v.tensor_copy(topf[:, :, :], topi[:, :, 0:TOPK]))
                    for j in range(NBLK):
                        link(v.tensor_tensor(hot[:, j, :, :], iota_e[:, :].unsqueeze(1).to_broadcast([P, TOPK, E]),
                                             topf[:, j, :].unsqueeze(2).to_broadcast([P, TOPK, E]), ALU.is_equal))
                    link(v.tensor_reduce(sel[:, :, :], hot[:, :, :, :].rearrange("p j k e -> p j e k"),
                                         axis=AX.X, op=ALU.add))
                    tell(v.tensor_copy(sel_h[:, :, :], sel[:, :, :]), sel_ok)
                    for j in range(NBLK):
                        link(v.tensor_tensor(tmp[:, j, :, :], hot[:, j, :, :],
                                             sc[:, j, :].unsqueeze(1).to_broadcast([P, TOPK, E]), ALU.mult))
                    link(v.tensor_reduce(gw[:, :, :], tmp[:, :, :, :], axis=AX.X, op=ALU.add))
                    link(v.tensor_reduce(gsum[:, :], gw[:, :, :], axis=AX.X, op=ALU.add))
                    link(v.tensor_scalar(gsum[:, :], gsum[:, :], 1e-12, None, ALU.max))
                    link(v.reciprocal(gsum[:, :], gsum[:, :]))
                    link(v.tensor_tensor(gw[:, :, :], gw[:, :, :],
                                         gsum[:, :].unsqueeze(2).to_broadcast([P, NBLK, TOPK]), ALU.mult))
                    wait(count_ok, 1)
                    cnt = po[:, 1, 0:(NBLK + 1) * E].rearrange("p (j e) -> p j e", e=E)
                    link(v.tensor_tensor(pos[:, :, :], cnt[:, 0:NBLK, :],
                                         taken[:, :].unsqueeze(1).to_broadcast([P, NBLK, E]), ALU.add))
                    link(v.tensor_tensor(taken[:, :], cnt[:, NBLK, :], taken[:, :], ALU.add))
                    link(v.tensor_scalar(over[:, :, :], pos[:, :, :], float(CAP), FAR, ALU.is_ge, ALU.mult))
                    link(v.tensor_tensor(pos[:, :, :], pos[:, :, :],
                                         iota_s[:, :].unsqueeze(1).to_broadcast([P, NBLK, E]), ALU.add))
                    link(v.tensor_tensor(pos[:, :, :], pos[:, :, :], over[:, :, :], ALU.add))
                    for j in range(NBLK):
                        link(v.tensor_tensor(tmp[:, j, :, :], hot[:, j, :, :],
                                             pos[:, j, :].unsqueeze(1).to_broadcast([P, TOPK, E]), ALU.mult))
                    link(v.tensor_reduce(slotf[:, :, :], tmp[:, :, :, :], axis=AX.X, op=ALU.add))
                    link(v.tensor_copy(slot[:, :, :], slotf[:, :, :]))
                    link(v.tensor_scalar(keep[:, :, :], slotf[:, :, :], float(E * CAP), None, ALU.is_lt))
                    tell(v.tensor_tensor(gout[:, :, :], gw[:, :, :], keep[:, :, :], ALU.mult), slot_ok)
                for s in (var_ok, xn_ok, pooled_ok, proj_v, max_ok, cp_ok, lat_done, gate_in, mix_ok, post_cp,
                          hvar_ok, hnorm_ok, ff_ok, x1_ok, var2_ok, xn2_ok, sel_ok, slot_ok, dchain):
                    s.whole()

            @block.tensor
            def _(pe):
                t = nc.tensor
                with pe.Fori(0, B) as b:
                    def wait(s, n):
                        pe.wait_ge(s.sem, s.value(b, n))

                    def flip(src, ready):
                        for j in range(NBLK):
                            for k in range(KD):
                                ins = t.transpose(psT[:, k * S + j * P:k * S + (j + 1) * P],
                                                  src[:, j, k * P:(k + 1) * P], ident[:, :])
                        ready.raised_by(ins)

                    def through(out, w, x, n=KD, last=True):
                        for k in range(n):
                            ins = t.matmul(out, w(k), x(k), start=(k == 0), stop=(last and k == n - 1))
                        return ins

                    wait(xn_ok, 1)
                    flip(xn, xnT_tr)
                    wait(xnT_ok, 1)
                    for n in range(8):
                        w, g_ = (wq, n) if n < HG else (wk, n - HG)
                        if n >= 4:
                            wait(proj_a, n - 3)
                        proj.raised_by(through(psS[:, n % 4, :], lambda k: w[:, k, g_ * P:(g_ + 1) * P],
                                               lambda k: xnT[:, k, :]))
                    for j in range(NBLK):
                        wait(proj_a, 5 + j)
                        through(psS[:, j, 0:D], lambda k: xnT[:, k, j * P:(j + 1) * P], lambda k: wv[:, k, :], last=False)
                        proj.raised_by(t.matmul(psS[:, j, 0:D], ones_row[:, :], bv[:, :], start=False, stop=True))
                    wait(proj_v, 1)
                    proj.raised_by(through(psS[:, 0, :], lambda k: wrq[:, k, :], lambda k: xnT[:, k, :]))
                    wait(proj_v, 2)
                    wait(pooled_ok, 1)
                    through(psS[:, 1, 0:LAT], lambda k: wrk[:, k, :], lambda k: pooled[:, k, :])
                    through(psS[0:LAT, 1, LAT:2 * LAT], lambda k: pooled[:, k, :], lambda k: wrv[:, k, :],
                            last=False)
                    proj.raised_by(t.matmul(psS[0:LAT, 1, LAT:2 * LAT], ones_row[:, 0:LAT], brv[:, :],
                                            start=False, stop=True))

                    def scores(u):
                        j, g_ = u // (HG + 1), u % (HG + 1)
                        k0, nk = span(u)
                        if u >= 2:
                            wait(exp_ok, u - 1)
                        if g_ == HG:
                            t.matmul(psS[:, 2 * (u % 2), 0:LH * LAT], ident_h[:, :],
                                     lmask[:, j, :, :].rearrange("p h n -> p (h n)"), start=True, stop=False)
                        else:
                            for c in range(2):
                                t.matmul(psS[:, 2 * (u % 2) + c, :], ident_h[:, :],
                                         mask[:, :, :, :].rearrange("p r k n -> p (r k n)"), start=True, stop=False)
                        for h in range(G):
                            qs = qX[:, g_, h, j * P:(j + 1) * P] if g_ < HG else rqX[:, h, j * P:(j + 1) * P]
                            ks = kT[:, g_, k0:k0 + nk] if g_ < HG else rkT[:, 0:LAT]
                            ins = t.matmul(scored(u)[:, h, :], qs, ks, start=False,
                                           stop=(h == G - 1 if g_ == HG else h % 2 == 1))
                        s_ok.raised_by(ins)

                    def turn(u):
                        k0, nk = span(u)
                        wait(exp_ok, u + 1)
                        if u >= 1:
                            wait(cp_ok, u)
                        if nk == LAT:
                            pe.sem_inc(alone_t, 1)
                        for h in range(G):
                            if nk == LAT:
                                ins = t.transpose(psT[0:LAT, 2 * h * P:(2 * h + 1) * P], pr[:, u % 2, h, 0:LAT], ident[:, :])
                            else:
                                for k in range(nk // P):
                                    k += 2 - nk // P
                                    c = 2 * h + k
                                    ins = t.transpose(psT[:, c * P:(c + 1) * P], pr[:, u % 2, h, k * P:(k + 1) * P],
                                                      ident[:, :])
                        tr_ok.raised_by(ins)

                    def values(u):
                        j, g_ = u // (HG + 1), u % (HG + 1)
                        k0, nk = span(u)
                        wait(cp_ok, u + 1)
                        for h in range(G):
                            hh = g_ * G + h
                            o = po[:, j % 2, hh * VW:(hh + 1) * VW]
                            if g_ == HG:
                                ins = t.matmul(o, prT[0:LAT, u % 2, h, 0, :], rvv[:, h, :], start=True, stop=True)
                            else:
                                ks = [0, 1] if nk > P else [1]
                                for k in ks:
                                    ins = t.matmul(o, prT[:, u % 2, h, k, :], vv[:, j - 1 + k, hh, :],
                                                   start=(k == ks[0]), stop=(k == 1))
                        pv_ok.raised_by(ins)

                    def post(q, stage):
                        if stage == 1:
                            wait(lat_done, q + 1)
                            pe.sem_inc(alone_t, 1)
                            post_t.raised_by(t.transpose(psT[0:LAT, 0:P], lat[:, :, :].rearrange("p h d -> p (h d)"),
                                                         ident[:, :]))
                        if stage == 2:
                            wait(post_cp, 4 * q + 1)
                            t.matmul(psT[:, 0:D], latT[:, :], wro[:, :], start=True, stop=False)
                            post_t.raised_by(t.matmul(psT[:, 0:D], ones_row[:, :], bro[:, :], start=False, stop=True))
                        if stage == 3:
                            wait(mix_ok, q + 1)
                            wait(post_cp, 4 * q + 2)
                            for k in range(KD):
                                ins = t.transpose(psT[:, k * P:(k + 1) * P],
                                                  mix[:, 8 * k:8 * k + 8, :].rearrange("p h d -> p (h d)"), ident[:, :])
                            post_t.raised_by(ins)
                        if stage == 4:
                            wait(post_cp, 4 * q + 3)
                            through(psT[:, 0:D], lambda k: mixT[:, k, :], lambda k: wo[:, k, :], last=False)
                            post_t.raised_by(t.matmul(psT[:, 0:D], ones_row[:, :], bo[:, :], start=False, stop=True))

                    wait(proj_v, 4)
                    wait(proj_a, 11)
                    wait(qx_ok, HG + 1)
                    scores(0)
                    scores(1)
                    for u in range(NU):
                        if u > HG and u % (HG + 1) > 1:
                            wait(post_cp, 4 * (u // (HG + 1) - 1) + u % (HG + 1) - 1)
                        elif u > 2 * HG + 1 and u % (HG + 1) == 0:
                            wait(post_cp, 4 * (u // (HG + 1) - 1))
                        turn(u)
                        if u + 2 < NU:
                            scores(u + 2)
                        if u > HG:
                            if u % (HG + 1):
                                wait(cp_ok, u + 1)
                            post(u // (HG + 1) - 1, u % (HG + 1))
                        values(u)
                    for stage in range(HG + 1):
                        post(NBLK - 1, stage)

                    def expand(j):
                        wait(gelu_ok, j - 1) if j >= 2 else wait(exp_ok, NU)
                        for c in range(2):
                            ins = through(psS[:, 2 * (j % 2) + c, :], lambda k: xnT[:, k, j * P:(j + 1) * P],
                                          lambda k: wfc[:, k, c * 512:(c + 1) * 512])
                        h_ok.raised_by(ins)

                    expand(0)
                    expand(1)
                    wait(post_cp, 4 * NBLK)
                    for j in range(NBLK):
                        wait(haff_ok, 2 * j + 2)
                        if j >= 1:
                            wait(ht_ok, j)
                        for k in range(HID // P):
                            ins = t.transpose(psT[:, k * P:(k + 1) * P], hid[:, j % 2, k * P:(k + 1) * P], ident[:, :])
                        ht_tr.raised_by(ins)
                        if j + 2 < NBLK:
                            expand(j + 2)
                        wait(ht_ok, j + 1)
                        if j >= 2:
                            wait(ff_ok, j - 1)
                        pj_ok.raised_by(through(po[:, j % 2, 0:D], lambda k: hidT[:, j % 2, k, :],
                                                lambda k: wpj[:, k, :], HID // P))

                    wait(xn2_ok, 1)
                    flip(xn2, xn2T_tr)
                    wait(ff_ok, NBLK)
                    wait(xn2T_ok, 1)
                    for j in range(NBLK):
                        ins = through(po[:, 0, j * E:(j + 1) * E], lambda k: xn2T[:, k, j * P:(j + 1) * P],
                                      lambda k: gate_w[:, k, :])
                    logit_ok.raised_by(ins)
                    wait(sel_ok, 1)
                    for j in range(NBLK + 1):
                        for k in range(min(j + 1, NBLK)):
                            m = before if k == j else ones_h
                            ins = t.matmul(po[:, 1, j * E:(j + 1) * E], m[:, :], sel_h[:, k, :],
                                           start=(k == 0), stop=(k == min(j, NBLK - 1)))
                    count_ok.raised_by(ins)
                for s in (xnT_tr, proj, s_ok, tr_ok, pv_ok, post_t, h_ok, ht_tr, pj_ok, xn2T_tr, logit_ok, count_ok):
                    s.whole()


DI = 512
M = DI // P
NS = 16
RK = 16
TAPS = 4
NP_ = NS // 2
W = NP_ * M
NA, NH, NQ = 4, 2, 2


def layer1_mixer(nc, A, XNT, S1):
    ctx = ExitStack()
    with ctx:
        sb = lambda name, shape, dt=F32: ctx.enter_context(nc.sbuf_tensor("m_" + name, shape, dt))
        sem = lambda name: ctx.enter_context(nc.semaphore("m_" + name))
        win = sb("win", [P, 2, KD, 2 * DI])
        wbc = sb("wbc", [P, 2, M, 6 * NS])
        wdr = sb("wdr", [P, 2, M, RK])
        wdt = sb("wdt", [RK, 2, DI])
        wout = sb("wout", [P, 2, M, D])
        cw = sb("cw", [P, 2, M, TAPS])
        cb = sb("cb", [P, 2, M])
        db = sb("db", [P, 2, M])
        dd = sb("dd", [P, 2, M])
        al = sb("al", [P, 2, M, NS])
        gam = sb("gam", [P, D])
        bet = sb("bet", [P, D])
        ident = sb("ident", [P, P])
        pick = sb("pick", [6 * NS, 2 * NS, P], BF16)
        half = sb("half", [P, NBLK])

        xT = sb("xT", [P, KD, S])
        xi = sb("xi", [P, M, TAPS - 1 + S])
        z = sb("z", [P, 2, M, S])
        xc = sb("xc", [P, 2, M, S])
        dt = sb("dt", [P, 2, M, S])
        u = sb("u", [P, 2, M, S])
        rest = sb("rest", [P, M, S])
        bc = sb("bc", [6 * NS, 2, S], BF16)
        bcr = sb("bcr", [6 * NS, S])
        bcm = sb("bcm", [6 * NS, S], BF16)
        dtr = sb("dtr", [RK, S])
        Bs = sb("Bs", [P, 2, 2, S])
        Cs = sb("Cs", [P, 2, 2, S])
        dA = sb("dA", [P, NA, 2, S])
        dBu = sb("dBu", [P, NH, 2, S])
        hh = sb("hh", [P, 2, S])
        hC = sb("hC", [P, NQ, 2, S])
        yt = sb("yt", [P, S])
        yo0 = sb("yo0", [P, NBLK, D])
        yo = sb("yo", [P, NBLK, D])
        bnst = sb("bnst", [P, NBLK, 6])
        mv = sb("mv", [P, NBLK, 2])
        rstd = sb("rstd", [P, NBLK])
        psY = ctx.enter_context(nc.psum_tensor("psY", [P, M, S], F32))
        psB = ctx.enter_context(nc.psum_tensor("psB", [P, 2, S], F32))
        psP = ctx.enter_context(nc.psum_tensor("psP", [P, 2, S], F32))

        w_in, made, prep = sem("w_in"), sem("made"), sem("prep")
        loads = []
        for d, n in enumerate(("f", "b")):
            loads += [(win[:, d], A[n + "_win"].rearrange("(t p) n -> p t n", p=P)),
                      (wbc[:, d], A[n + "_wbc"].rearrange("(t p) n -> p t n", p=P)),
                      (wdr[:, d], A[n + "_wdr"].rearrange("(t p) n -> p t n", p=P)),
                      (wdt[:, d], A[n + "_wdt"]),
                      (wout[:, d], A[n + "_wout"].rearrange("(t p) n -> p t n", p=P)),
                      (cw[:, d], A[n + "_cw"].rearrange("(t p) n -> p t n", p=P)),
                      (cb[:, d], A[n + "_cb"]), (db[:, d], A[n + "_db"]), (dd[:, d], A[n + "_dd"]),
                      (al[:, d], A[n + "_al"].rearrange("(t p) n -> p t n", p=P))]
        loads += [(gam[:, :], A["gam"].partition_broadcast(P)), (bet[:, :], A["bet"].partition_broadcast(P))]
        with nc.Block() as block:
            @block.sync
            def _(sp):
                for t, s in loads:
                    sp.dma_start(t, s).then_inc(w_in, 16)
                sp.wait_ge(w_in, 16 * len(loads))

            @block.gpsimd
            def _(pool):
                g = nc.gpsimd
                m = [0]

                def link(ins):
                    ins.then_inc(made, 1)
                    m[0] += 1
                    pool.wait_ge(made, m[0])

                link(g.memset(ident[:, :], 0.0))
                link(g.affine_select(out=ident[:, :], in_=ident[:, :], compare_op=ALU.not_equal, fill=1.0,
                                     base=0, pattern=[[-1, P]], channel_multiplier=1))
                link(g.memset(pick[:, :, :], 0.0))
                for k in range(3):
                    link(g.affine_select(out=pick[:, :, :], in_=pick[:, :, :], compare_op=ALU.not_equal,
                                         fill=1.0, base=-32 * k, pattern=[[-1, 2 * NS], [0, P]],
                                         channel_multiplier=1))
                link(g.memset(half[:, :], -0.5))
                link(g.memset(xi[:, :, 0:TAPS - 1], 0.0))
                link(g.memset(z[:, 1, :, :], 0.0))
                link(g.memset(yo0[:, :, :], 0.0))

            @block.scalar
            def _(act):
                act.wait_ge(w_in, 16 * len(loads))
                nc.scalar.activation(al[:, :, :, :], al[:, :, :, :], ACT.Exp).then_inc(prep, 1)

            @block.vector
            def _(dve):
                dve.wait_ge(prep, 1)
                nc.vector.tensor_scalar(al[:, :, :, :], al[:, :, :, :], -1.0, None, ALU.mult).then_inc(prep, 1)

        sig = lambda name, per, first=0: Signal(sem(name), per, first)
        xT_in = sig("xT_in", 16, 16)
        p_ok = sig("p_ok", 36, 14)
        pa = sig("pa", 26, 13)
        pv = sig("pv", 10, 1)
        conv_ok = sig("conv_ok", 2 * M, M)
        xc_ok = sig("xc_ok", 2, 1)
        z_ok = sig("z_ok", 2, 1)
        bc_ok = sig("bc_ok", 2, 1)
        na_ok = sig("na_ok", 2, 1)
        e_ok = sig("e_ok", 2, 1)
        l_ok = sig("l_ok", 2, 1)
        rest_ok = sig("rest_ok", 2, 1)
        t_ok = sig("t_ok", 4 * M, 2 * M)
        dt_ok = sig("dt_ok", 2 * M, M)
        u_ok = sig("u_ok", 2 * M, M)
        bcast = sig("bcast", 4 * NP_, 2)
        bcopy = sig("bcopy", 4 * NP_, 1)
        dA_ok = sig("dA_ok", 2 * W)
        dBu_ok = sig("dBu_ok", 2 * W, 1)
        scan_ok = sig("scan_ok", 2 * W, NA)
        hC_ok = sig("hC_ok", 2 * W, M)
        y_ok = sig("y_ok", 2 * W, M)
        fin_ok = sig("fin_ok", 2 * M)
        mvar = sig("mvar", 1)
        mrstd = sig("mrstd", 2)
        s1_ok = sig("s1_ok", 1)
        s1_out = sig("s1_out", 16, 16)
        mchain = sig("mchain", MCHAIN, MFIRST)
        alone_v, alone_p = sem("alone_v"), sem("alone_p")

        JOBS = [("xi", m) for m in range(M)] + [("out", j) for j in range(NBLK)] + [("z", m) for m in range(M)] + \
               [("bc", 0), ("dtr", 0)] + [("dt", m) for m in range(M)]
        PEEL = [x for x in JOBS if x[0] != "out"]
        on_dve = lambda kind: kind in ("out", "bc")
        UNIT_OF = {}
        for m in range(M):
            UNIT_OF[("xi", m)] = m
            UNIT_OF[("out", m)] = 4 + m
            UNIT_OF[("z", m)] = 8 + m
            UNIT_OF[("dt", m)] = 16 + m
        UNIT_OF[("bc", 0)] = 14
        UNIT_OF[("dtr", 0)] = 15
        AHEAD = 3

        class Place:

            def __init__(self, b, d):
                self.b, self.d = b, d

            def ph(self, s, per_phase, n):
                if self.b is None:
                    return n
                return s.value(self.b, self.d * per_phase + n)

        def job_count(pl, kind, idx):
            jobs = PEEL if pl.b is None else JOBS
            return pl.ph(p_ok, 18, jobs.index((kind, idx)) + 1)

        def evac_before(pl, pos):
            jobs = PEEL if pl.b is None else JOBS
            if pos >= 2:
                seen = jobs[:pos - 1]
                k = jobs[pos - 2][0]
                n = sum(on_dve(x[0]) == on_dve(k) for x in seen)
                return (pv, pl.ph(pv, 5, n)) if on_dve(k) else (pa, pl.ph(pa, 13, n))
            if pl.b is None:
                return None
            return (pa, pl.ph(pa, 13, pos - 1))

        with nc.Block() as block:
            @block.sync
            def _(sp):
                sp.sem_inc(s1_out.sem, 16)
                sp.dma_start(xT[:, :, :], XNT[0].rearrange("(t p) s -> p t s", p=P)).then_inc(xT_in.sem, 16)

                def store(b, slot):
                    sp.wait_ge(s1_ok.sem, s1_ok.value(b, 1))
                    sp.dma_start(slot, yo[:, :, :]).then_inc(s1_out.sem, 16)

                with sp.Fori(0, B - 1) as b:
                    store(b, S1[bass.ds(b, 1), :, :].rearrange("a (j p) d -> p (a j) d", p=P))
                    sp.wait_ge(p_ok.sem, p_ok.value(b, 12))
                    sp.dma_start(xT[:, :, :], XNT[bass.ds(b + 1, 1), :, :].rearrange("a (t p) s -> p (a t) s", p=P)
                                 ).then_inc(xT_in.sem, 16)
                store(B - 1, S1[B - 1].rearrange("(j p) d -> p j d", p=P))
                sp.wait_ge(p_ok.sem, p_ok.value(B - 1, 12))
                sp.dma_start(xT[:, :, :], XNT[B - 1].rearrange("(t p) s -> p t s", p=P)).then_inc(xT_in.sem, 16)
                store(B, S1[B].rearrange("(j p) d -> p j d", p=P))
                sp.wait_ge(s1_out.sem, 16 * (B + 2))

            @block.tensor
            def _(pe):
                t = nc.tensor

                def job(pl, kind, idx):
                    jobs = PEEL if pl.b is None else JOBS
                    dn = pl.d if pl.b is None else 1 - pl.d
                    pos = jobs.index((kind, idx))
                    before = evac_before(pl, pos)
                    if before:
                        pe.wait_ge(before[0].sem, before[1])
                    o = psP[:, pos % 2, :]
                    if kind in ("xi", "z"):
                        if kind == "xi" and idx == 0 and dn == 0:
                            pe.wait_ge(xT_in.sem, 16 if pl.b is None else xT_in.value(pl.b, 16))
                        c = (0 if kind == "xi" else DI) + idx * P
                        for k in range(KD):
                            x = xT[:, k, :] if dn == 0 or kind == "z" else xT[:, k, ::-1]
                            ins = t.matmul(o, win[:, dn, k, c:c + P], x, start=(k == 0), stop=(k == KD - 1))
                    elif kind == "bc":
                        pe.wait_ge(xc_ok.sem, pl.ph(xc_ok, 1, 1))
                        for k in range(M):
                            ins = t.matmul(o[0:6 * NS, :], wbc[:, dn, k, :], xc[:, dn, k, :],
                                           start=(k == 0), stop=(k == M - 1))
                    elif kind == "dtr":
                        for k in range(M):
                            ins = t.matmul(o[0:RK, :], wdr[:, dn, k, :], xc[:, dn, k, :],
                                           start=(k == 0), stop=(k == M - 1))
                    elif kind == "dt":
                        pe.wait_ge(pa.sem, pl.ph(pa, 13, 9))
                        ins = t.matmul(o, wdt[:, dn, idx * P:(idx + 1) * P], dtr[:, :], start=True, stop=True)
                    else:
                        for m in range(M):
                            y = z[:, dn, m, idx * P:(idx + 1) * P]
                            ins = t.matmul(o[:, 0:D], y, wout[:, dn, m, :], start=(m == 0), stop=(m == M - 1))
                    p_ok.raised_by(ins) if pl.b is not None else ins.then_inc(p_ok.sem, 1)

                def spread(pl, d, j, c, n):
                    pe.wait_ge(bcopy.sem, pl.ph(bcopy, 2 * NP_, n))
                    for k in range(2):
                        ins = t.matmul(psB[:, k, :], pick[:, c * NS + 2 * j + k, :], bc[:, d, :], start=True, stop=True)
                    bcast.raised_by(ins)

                pl0 = Place(None, 0)
                for kind, idx in PEEL:
                    job(pl0, kind, idx)
                pe.wait_ge(bc_ok.sem, 1)
                for c in range(2):
                    if c:
                        pe.wait_ge(bcopy.sem, 1)
                    for k in range(2):
                        ins = t.matmul(psB[:, k, :], pick[:, c * NS + k, :], bc[:, 0, :], start=True, stop=True)
                    ins.then_inc(bcast.sem, 1)
                pe.sem_inc(y_ok.sem, M)
                with pe.Fori(0, B) as b:
                    for d in range(2):
                        pl = Place(b, d)
                        for w in range(W):
                            j, m = w // M, w % M
                            if j == 0:
                                pe.wait_ge(fin_ok.sem, pl.ph(fin_ok, M, m + 1))
                            pe.wait_ge(hC_ok.sem, pl.ph(hC_ok, W, w + 1))
                            for k in range(2):
                                ins = t.matmul(psY[:, m, :], ident[:, :], hC[:, w % NQ, k, :],
                                               start=(j == 0 and k == 0), stop=(j == NP_ - 1 and k == 1))
                            y_ok.raised_by(ins)
                            for kind, idx in JOBS:
                                if UNIT_OF[(kind, idx)] == w:
                                    job(pl, kind, idx)
                            if m in (0, 1):
                                nj, nd = (j + 1, d) if j + 1 < NP_ else (0, 1 - d)
                                if nj == 0 and m == 0:
                                    pe.wait_ge(bc_ok.sem, pl.ph(bc_ok, 1, 1))
                                spread(pl, nd, nj, m, 2 * j + m + 1)
                plE = Place(B, 0)
                for j in range(NBLK):
                    if j < 2:
                        pe.wait_ge(fin_ok.sem, fin_ok.value(B, M))
                        pe.wait_ge(pa.sem, pa.value(B, 0))
                    else:
                        pe.wait_ge(pv.sem, pv.value(B, j - 1))
                    for m in range(M):
                        y = z[:, 1, m, j * P:(j + 1) * P]
                        ins = t.matmul(psP[:, j % 2, 0:D], y, wout[:, 1, m, :], start=(m == 0), stop=(m == M - 1))
                    ins.then_inc(p_ok.sem, 1)
                for s in (p_ok, bcast, y_ok):
                    s.whole()

            @block.scalar
            def _(act):
                a = nc.scalar

                def raise_(pl, s, ins):
                    s.raised_by(ins) if pl.b is not None else ins.then_inc(s.sem, 1)

                def evac(pl, kind, idx):
                    dn = pl.d if pl.b is None else 1 - pl.d
                    jobs = PEEL if pl.b is None else JOBS
                    pos = jobs.index((kind, idx))
                    act.wait_ge(p_ok.sem, job_count(pl, kind, idx))
                    src = psP[:, pos % 2, :]
                    if kind == "xi":
                        if pl.b is not None:
                            act.wait_ge(t_ok.sem, pl.ph(t_ok, 2 * M, 0))
                        ins = a.activation(xi[:, idx, TAPS - 1:], src, ACT.Copy)
                    elif kind == "z":
                        ins = a.activation(z[:, dn, idx, :], src, ACT.Copy)
                    elif kind == "dtr":
                        ins = a.activation(dtr[:, :], psP[0:RK, pos % 2, :], ACT.Copy)
                    else:
                        ins = a.activation(dt[:, dn, idx, :], src, ACT.Identity, bias=db[:, dn, idx:idx + 1], scale=1.0)
                    raise_(pl, pa, ins)

                def silus(pl):
                    dn = pl.d if pl.b is None else 1 - pl.d
                    act.wait_ge(conv_ok.sem, pl.ph(conv_ok, M, M))
                    raise_(pl, xc_ok, a.activation(xc[:, dn, :, :], xc[:, dn, :, :], ACT.Silu))
                    act.wait_ge(pa.sem, pl.ph(pa, 13, 8))
                    raise_(pl, z_ok, a.activation(z[:, dn, :, :], z[:, dn, :, :], ACT.Silu))

                def exp_abs(pl):
                    dn = pl.d if pl.b is None else 1 - pl.d
                    act.wait_ge(pa.sem, pl.ph(pa, 13, 13))
                    raise_(pl, na_ok, a.activation(u[:, dn, :, :], dt[:, dn, :, :], ACT.Abs))
                    act.wait_ge(na_ok.sem, pl.ph(na_ok, 1, 1))
                    raise_(pl, e_ok, a.activation(u[:, dn, :, :], u[:, dn, :, :], ACT.Exp, scale=-1.0))

                def log1(pl):
                    dn = pl.d if pl.b is None else 1 - pl.d
                    act.wait_ge(rest_ok.sem, pl.ph(rest_ok, 1, 1))
                    raise_(pl, l_ok, a.activation(xi[:, :, TAPS - 1:], rest[:, :, :], ACT.Ln, bias=1.0))

                def copy_bc(pl, nj, c, n):
                    act.wait_ge(bcast.sem, pl.ph(bcast, 2 * NP_, n))
                    dst = (Bs, Cs)[c][:, nj % 2, :, :]
                    raise_(pl, bcopy, a.activation(dst, psB[:, :, :], ACT.Copy))

                pl0 = Place(None, 0)
                for kind, idx in PEEL:
                    if kind == "bc":
                        silus(pl0)
                    if not on_dve(kind):
                        evac(pl0, kind, idx)
                exp_abs(pl0)
                log1(pl0)
                copy_bc(pl0, 0, 0, 1)
                with act.Fori(0, B) as b:
                    for d in range(2):
                        pl = Place(b, d)
                        for w in range(W):
                            j, m = w // M, w % M
                            if w == 0:
                                act.wait_ge(dt_ok.sem, pl.ph(dt_ok, M, 0))
                            act.wait_ge(scan_ok.sem, pl.ph(scan_ok, W, w + 1 - NA))
                            for k in range(2):
                                ins = a.activation(dA[:, (d * W + w) % NA, k, :], dt[:, d, m, :], ACT.Exp,
                                                   scale=al[:, d, m, 2 * j + k:2 * j + k + 1])
                            dA_ok.raised_by(ins)
                            for kind, idx in JOBS:
                                if UNIT_OF[(kind, idx)] + AHEAD == w and not on_dve(kind):
                                    evac(pl, kind, idx)
                            if w == 15:
                                silus(pl)
                            if w == 24:
                                exp_abs(pl)
                            if w == 26:
                                log1(pl)
                            if m == 0:
                                act.wait_ge(hC_ok.sem, pl.ph(hC_ok, W, (j - 1) * M + 1))
                                copy_bc(pl, j, 1, 2 * j)
                            if m == M - 1:
                                act.wait_ge(dBu_ok.sem, pl.ph(dBu_ok, W, j * M))
                                copy_bc(pl, (j + 1) % NP_, 0, 2 * j + 1)
                for s in (na_ok, pa, xc_ok, z_ok, e_ok, l_ok, bcopy, dA_ok):
                    s.whole()

            @block.gpsimd
            def _(pool):
                g = nc.gpsimd

                def raise_(pl, s, ins):
                    s.raised_by(ins) if pl.b is not None else ins.then_inc(s.sem, 1)

                def soft(pl, m):
                    dn = pl.d if pl.b is None else 1 - pl.d
                    pool.wait_ge(rest_ok.sem, pl.ph(rest_ok, 1, 1))
                    raise_(pl, t_ok, g.tensor_tensor(u[:, dn, m, :], u[:, dn, m, :], rest[:, m, :], ALU.subtract))
                    pool.wait_ge(l_ok.sem, pl.ph(l_ok, 1, 1))
                    pool.wait_ge(t_ok.sem, pl.ph(t_ok, 2 * M, 2 * m + 1))
                    raise_(pl, t_ok, g.tensor_tensor(u[:, dn, m, :], u[:, dn, m, :], xi[:, m, TAPS - 1:], ALU.add))

                def inputs(pl, m):
                    dn = pl.d if pl.b is None else 1 - pl.d
                    pool.wait_ge(dt_ok.sem, pl.ph(dt_ok, M, m + 1))
                    raise_(pl, u_ok, g.tensor_tensor(u[:, dn, m, :], dt[:, dn, m, :], xc[:, dn, m, :], ALU.mult))

                pl0 = Place(None, 0)
                for m in range(M):
                    soft(pl0, m)
                for m in range(M):
                    inputs(pl0, m)

                pool.sem_inc(dBu_ok.sem, 1)

                def rsqrt(value):
                    pool.wait_ge(mvar.sem, value)
                    pool.sem_inc(alone_p, 1)
                    mrstd.raised_by(g.tensor_scalar(rstd[:, :], mv[:, :, 1], LN_EPS, None, ALU.add))

                with pool.Fori(0, B) as b:
                    for d in range(2):
                        pl = Place(b, d)
                        for w in range(W):
                            j, m = w // M, w % M
                            pool.wait_ge(bcopy.sem, pl.ph(bcopy, 2 * NP_, 2 * j))
                            pool.wait_ge(u_ok.sem, pl.ph(u_ok, M, 0 if j else m + 1 - M))
                            pool.wait_ge(scan_ok.sem, pl.ph(scan_ok, W, w + 1 - NH))
                            dBu_ok.raised_by(g.tensor_tensor(
                                dBu[:, w % NH, :, :], u[:, d, m, :].unsqueeze(1).to_broadcast([P, 2, S]),
                                Bs[:, j % 2, :, :], ALU.mult))
                            if d == 0 and w == 10:
                                rsqrt(mvar.value(b, 1))
                                pool.wait_ge(mrstd.sem, mrstd.value(b, 1))
                                mrstd.raised_by(g.tensor_tensor(rstd[:, :], rstd[:, :], half[:, :], ALU.pow))
                            if 25 <= w < 25 + M:
                                soft(pl, w - 25)
                            if 28 <= w < 28 + M:
                                inputs(pl, w - 28)
                pool.wait_ge(mvar.sem, mvar.value(B, 1))
                g.tensor_scalar(rstd[:, :], mv[:, :, 1], LN_EPS, None, ALU.add).then_inc(mrstd.sem, 1)
                pool.wait_ge(mrstd.sem, mrstd.value(B, 1))
                g.tensor_tensor(rstd[:, :], rstd[:, :], half[:, :], ALU.pow).then_inc(mrstd.sem, 1)
                for s in (t_ok, u_ok, dBu_ok, mrstd):
                    s.whole()

            @block.vector
            def _(dve):
                v = nc.vector

                def raise_(pl, s, ins, n, per):
                    s.raised_by(ins) if pl.b is not None else ins.then_inc(s.sem, 1)
                    dve.wait_ge(s.sem, pl.ph(s, per, n))

                c = [0]

                def link(pl, ins):
                    ins.then_inc(mchain.sem, 1)
                    c[0] += 1
                    dve.wait_ge(mchain.sem, c[0] if pl.b is None else mchain.value(pl.b, c[0]))

                def conv(pl, m):
                    dn = pl.d if pl.b is None else 1 - pl.d
                    n = m + 1
                    dve.wait_ge(pa.sem, pl.ph(pa, 13, n))
                    y = xc[:, dn, m, :]
                    link(pl, v.tensor_scalar(y, xi[:, m, 0:S], cw[:, dn, m, 0:1], cb[:, dn, m:m + 1], ALU.mult, ALU.add))
                    for k in range(1, TAPS):
                        ins = v.scalar_tensor_tensor(y, xi[:, m, k:k + S], cw[:, dn, m, k:k + 1], y, ALU.mult, ALU.add)
                        if k < TAPS - 1:
                            link(pl, ins)
                    raise_(pl, conv_ok, ins, m + 1, M)

                def split(pl):
                    dn = pl.d if pl.b is None else 1 - pl.d
                    jobs = PEEL if pl.b is None else JOBS
                    o = psP[0:6 * NS, jobs.index(("bc", 0)) % 2, :]
                    dve.wait_ge(p_ok.sem, job_count(pl, "bc", 0))
                    link(pl, v.tensor_copy(bc[:, dn, :], o))
                    raise_(pl, pv, v.tensor_tensor(bcr[:, :], o, bc[:, dn, :], ALU.subtract),
                           1 if pl.b is None else 5, 5)
                    link(pl, v.tensor_copy(bcm[:, :], bcr[:, :]))
                    link(pl, v.tensor_copy(bc[32:64, dn, :], bcr[32:64, :]))
                    link(pl, v.tensor_tensor(bcr[:, :], bcr[:, :], bcm[:, :], ALU.subtract))
                    raise_(pl, bc_ok, v.tensor_copy(bc[64:96, dn, :], bcr[64:96, :]), 1, 1)

                def remainder(pl):
                    dn = pl.d if pl.b is None else 1 - pl.d
                    dve.wait_ge(e_ok.sem, pl.ph(e_ok, 1, 1))
                    raise_(pl, rest_ok, v.tensor_scalar(rest[:, :, :], u[:, dn, :, :], 1.0, -1.0,
                                                        ALU.add, ALU.add), 1, 1)

                def steps(pl, m):
                    dn = pl.d if pl.b is None else 1 - pl.d
                    dve.wait_ge(t_ok.sem, pl.ph(t_ok, 2 * M, 2 * m + 2))
                    raise_(pl, dt_ok, v.scalar_tensor_tensor(dt[:, dn, m, :], dt[:, dn, m, :], 0.0, u[:, dn, m, :],
                                                             ALU.max, ALU.add), m + 1, M)

                def out(pl, dn, j, count, value):
                    dve.wait_ge(p_ok.sem, count)
                    o = psP[:, j % 2, 0:D]
                    if dn == 0:
                        ins = v.tensor_copy(yo0[:, j, :], o)
                    else:
                        if j == 0:
                            dve.wait_ge(s1_out.sem, s1_out.value(pl.b, 0))
                        ins = v.tensor_tensor(yo[:, j, :], o, yo0[:, j, :], ALU.add)
                    ins.then_inc(pv.sem, 1)
                    pv.n += 1
                    dve.wait_ge(pv.sem, value)

                def stats(pl, value):
                    for j in range(NBLK):
                        ins = v.bn_stats(bnst[:, j, :], yo[:, j, :])
                    link(pl, ins)
                    dve.sem_inc(alone_v, 1)
                    for j in range(NBLK):
                        ins = v.bn_aggr(mv[:, j, :], bnst[:, j, :])
                    ins.then_inc(mvar.sem, 1)
                    dve.wait_ge(mvar.sem, value)

                def norm(pl, ready):
                    dve.wait_ge(mrstd.sem, ready)
                    for j in range(NBLK):
                        ins = v.tensor_scalar(yo[:, j, :], yo[:, j, :], mv[:, j, 0:1], rstd[:, j:j + 1],
                                              ALU.subtract, ALU.mult)
                    link(pl, ins)
                    link(pl, v.tensor_tensor(yo[:, :, :], yo[:, :, :], gam[:, :].unsqueeze(1).to_broadcast([P, NBLK, D]),
                                             ALU.mult))
                    v.tensor_tensor(yo[:, :, :], yo[:, :, :], bet[:, :].unsqueeze(1).to_broadcast([P, NBLK, D]),
                                    ALU.add).then_inc(s1_ok.sem, 1)

                def finish(pl, m, ready):
                    dn = 1 - pl.d
                    dve.wait_ge(y_ok.sem, ready)
                    link(pl, v.scalar_tensor_tensor(yt[:, :], xc[:, dn, m, :], dd[:, dn, m:m + 1], psY[:, m, :],
                                                    ALU.mult, ALU.add))
                    return v.tensor_tensor(z[:, dn, m, :], yt[:, :] if dn == 0 else yt[:, ::-1], z[:, dn, m, :], ALU.mult)

                def y_value(pl, m):
                    return pl.ph(y_ok, W, m + 1 - M)

                def y_free(pl, w):
                    return pl.ph(y_ok, W, w + 1 - NQ)

                pl0 = Place(None, 0)
                for m in range(M):
                    conv(pl0, m)
                split(pl0)
                remainder(pl0)
                for m in range(M):
                    steps(pl0, m)
                dve.sem_inc(scan_ok.sem, NA)
                link(pl0, v.memset(psY[:, :, :], 0.0))
                dve.sem_inc(hC_ok.sem, M)
                link(pl0, v.memset(xc[:, 1, :, :], 0.0))
                assert c[0] == MFIRST, ("MFIRST", c[0])
                c[0] = 0
                with dve.Fori(0, B) as b:
                    for d in range(2):
                        pl = Place(b, d)
                        for w in range(W):
                            j, m = w // M, w % M
                            if j == 0:
                                ins = finish(pl, m, y_value(pl, m))
                                fin_ok.raised_by(ins)
                                dve.wait_ge(fin_ok.sem, pl.ph(fin_ok, M, m + 1))
                            dve.wait_ge(dA_ok.sem, pl.ph(dA_ok, W, w + 1))
                            dve.wait_ge(dBu_ok.sem, pl.ph(dBu_ok, W, w + 1))
                            dve.wait_ge(hC_ok.sem, pl.ph(hC_ok, W, w))
                            for k in range(2):
                                ins = v.tensor_tensor_scan(hh[:, k, :], dA[:, (d * W + w) % NA, k, :],
                                                           dBu[:, w % NH, k, :], 0.0, ALU.mult, ALU.add)
                            scan_ok.raised_by(ins)
                            dve.wait_ge(scan_ok.sem, pl.ph(scan_ok, W, w + 1))
                            dve.wait_ge(bcopy.sem, pl.ph(bcopy, 2 * NP_, 2 * j + 1))
                            dve.wait_ge(y_ok.sem, y_free(pl, w))
                            hC_ok.raised_by(v.tensor_tensor(hC[:, w % NQ, :, :], hh[:, :, :], Cs[:, j % 2, :, :],
                                                            ALU.mult))
                            if 4 <= w < 4 + M:
                                conv(pl, w - 4)
                            if 5 <= w < 5 + NBLK:
                                out(pl, 1 - d, w - 5, pl.ph(p_ok, 18, w), pl.ph(pv, 5, w - 4))
                            if d == 0 and w == 9:
                                stats(pl, mvar.value(b, 1))
                            if d == 0 and w == 12:
                                norm(pl, mrstd.value(b, 2))
                            if w == 15:
                                split(pl)
                            if w == 22:
                                remainder(pl)
                            if 26 <= w < 26 + M:
                                steps(pl, w - 26)
                assert c[0] == MCHAIN, ("MCHAIN", c[0])
                plE = Place(B, 0)
                c[0] = 0
                for m in range(M):
                    ins = finish(plE, m, y_value(plE, m))
                    ins.then_inc(fin_ok.sem, 1)
                    dve.wait_ge(fin_ok.sem, fin_ok.value(B, m + 1))
                for j in range(NBLK):
                    out(plE, 1, j, p_ok.value(B, j + 1), pv.value(B, 0) + j + 1)
                pv.n -= NBLK
                stats(plE, mvar.value(B, 1))
                norm(plE, mrstd.value(B, 2))
                for s in (conv_ok, pv, bc_ok, rest_ok, dt_ok, scan_ok, hC_ok, fin_ok):
                    s.whole()


def experts(nc, A, XE, YE):
    ctx = ExitStack()
    with ctx:
        sb = lambda name, shape, dt=F32: ctx.enter_context(nc.sbuf_tensor("e_" + name, shape, dt))
        sem = lambda name: ctx.enter_context(nc.semaphore("e_" + name))
        NB_ = 2
        CB = CAP // P
        ident = sb("ident", [P, P])
        xe = sb("xe", [P, NB_, CB, D])
        w_h = sb("w_h", [P, NB_, 3, 2 * P], BF16)
        w = sb("w", [P, NB_, 3, 2 * P])
        xeT = sb("xeT", [P, NB_, KD, CAP])
        hs = sb("hs", [P, NB_, CAP])
        hT = sb("hT", [P, NB_, CAP])
        ye = sb("ye", [P, NB_, CB, D])
        psX = ctx.enter_context(nc.psum_tensor("psX", [P, NB_, KD * CAP], F32))
        psH = ctx.enter_context(nc.psum_tensor("psH", [P, NB_, 2, CAP], F32))
        psO = ctx.enter_context(nc.psum_tensor("psO", [P, NB_, CB * D], F32))
        made = sem("made")
        with nc.Block() as block:
            @block.gpsimd
            def _(pool):
                nc.gpsimd.memset(ident[:, :], 0.0).then_inc(made, 1)
                pool.wait_ge(made, 1)
                nc.gpsimd.affine_select(out=ident[:, :], in_=ident[:, :], compare_op=ALU.not_equal, fill=1.0,
                                        base=0, pattern=[[-1, P]], channel_multiplier=1).then_inc(made, 1)
                pool.wait_ge(made, 2)

        sig = lambda name, per, first=0: Signal(sem(name), per, first)
        each = lambda name, per, first=0: [sig(name + str(c), per, first) for c in range(2)]
        x_in = each("x_in", 16)
        w_in = each("w_in", 48)
        w_ok = sig("w_ok", 2, 2)
        tr_ok = sig("tr_ok", 2, 2)
        xT_ok = sig("xT_ok", 2, 2)
        h_ok = sig("h_ok", 2, 2)
        sil_ok = sig("sil_ok", 2, 2)
        hT_ok = sig("hT_ok", 2, 2)
        o_ok = sig("o_ok", 2, 2)
        ye_ok = sig("ye_ok", 2, 2)
        y_out = each("y_out", 16, 16)
        alone_w = sem("alone_w")
        with nc.Block() as block:
            @block.sync
            def _(sp):
                for c in range(2):
                    sp.sem_inc(y_out[c].sem, 16)
                with sp.Fori(0, E // 2) as i:
                    for c in range(2):
                        sp.wait_ge(tr_ok.sem, tr_ok.value(i, c - 1))
                        sp.dma_start(xe[:, c, :, :], XE[bass.ds(2 * CAP * i + CAP * c, CAP), :].rearrange(
                            "(j p) d -> p j d", p=P)).then_inc(x_in[c].sem, 16)
                        sp.wait_ge(w_ok.sem, w_ok.value(i, c - 1))
                        for k, n in enumerate(("W1", "W3")):
                            sp.dma_start(w_h[:, c, k, :].rearrange("p (t n) -> p t n", n=I),
                                         A[n][bass.ds(2 * i + c, 1), :, :].rearrange("a (t p) n -> p (a t) n", p=P)
                                         ).then_inc(w_in[c].sem, 16)
                        sp.dma_start(w_h[:, c, 2, :], A["W2"][bass.ds(2 * i + c, 1), :, :].rearrange("a p n -> (a p) n")
                                     ).then_inc(w_in[c].sem, 16)

            @block.gpsimd
            def _(pool):
                pool.sem_inc(w_ok.sem, 2)
                with pool.Fori(0, E // 2) as i:
                    for c in range(2):
                        pool.wait_ge(w_in[c].sem, w_in[c].value(i, 48))
                        pool.wait_ge(o_ok.sem, o_ok.value(i, c - 1))
                        pool.sem_inc(alone_w, 1)
                        w_ok.raised_by(nc.gpsimd.tensor_copy(w[:, c, :, :], w_h[:, c, :, :]))

            @block.tensor
            def _(pe):
                t = nc.tensor
                pe.sem_inc(tr_ok.sem, 2)
                pe.sem_inc(h_ok.sem, 2)
                pe.sem_inc(o_ok.sem, 2)

                def flip(i, c):
                    pe.wait_ge(x_in[c].sem, x_in[c].value(i, 16))
                    pe.wait_ge(xT_ok.sem, xT_ok.value(i, c - 1))
                    for j in range(CB):
                        for k in range(KD):
                            ins = t.transpose(psX[:, c, k * CAP + j * P:k * CAP + (j + 1) * P],
                                              xe[:, c, j, k * P:(k + 1) * P], ident[:, :])
                    tr_ok.raised_by(ins)

                def hidden(i, c):
                    pe.wait_ge(w_ok.sem, w_ok.value(i, c + 1))
                    pe.wait_ge(xT_ok.sem, xT_ok.value(i, c + 1))
                    pe.wait_ge(hT_ok.sem, hT_ok.value(i, c - 1))
                    for n in range(2):
                        for k in range(KD):
                            ins = t.matmul(psH[:, c, n, :], w[:, c, n, k * I:(k + 1) * I], xeT[:, c, k, :],
                                           start=(k == 0), stop=(k == KD - 1))
                    h_ok.raised_by(ins)

                def output(i, c):
                    pe.wait_ge(hT_ok.sem, hT_ok.value(i, c + 1))
                    pe.wait_ge(ye_ok.sem, ye_ok.value(i, c - 1))
                    for j in range(CB):
                        ins = t.matmul(psO[:, c, j * D:(j + 1) * D], hT[:, c, j * P:(j + 1) * P], w[:, c, 2, :],
                                       start=True, stop=True)
                    o_ok.raised_by(ins)

                with pe.Fori(0, E // 2) as i:
                    flip(i, 0)
                    flip(i, 1)
                    hidden(i, 0)
                    hidden(i, 1)
                    output(i, 0)
                    output(i, 1)

            @block.vector
            def _(dve):
                v = nc.vector
                dve.sem_inc(xT_ok.sem, 2)
                dve.sem_inc(hT_ok.sem, 2)
                with dve.Fori(0, E // 2) as i:
                    for c in range(2):
                        dve.wait_ge(tr_ok.sem, tr_ok.value(i, c + 1))
                        dve.wait_ge(h_ok.sem, h_ok.value(i, c - 1))
                        xT_ok.raised_by(v.tensor_copy(xeT[:, c, :, :].rearrange("p t n -> p (t n)"), psX[:, c, :]))
                    for c in range(2):
                        dve.wait_ge(sil_ok.sem, sil_ok.value(i, c + 1))
                        dve.wait_ge(o_ok.sem, o_ok.value(i, c - 1))
                        hT_ok.raised_by(v.tensor_tensor(hT[:, c, :], hs[:, c, :], psH[:, c, 1, :], ALU.mult))

            @block.scalar
            def _(act):
                a = nc.scalar
                act.sem_inc(sil_ok.sem, 2)
                act.sem_inc(ye_ok.sem, 2)
                with act.Fori(0, E // 2) as i:
                    for c in range(2):
                        act.wait_ge(h_ok.sem, h_ok.value(i, c + 1))
                        act.wait_ge(hT_ok.sem, hT_ok.value(i, c - 1))
                        sil_ok.raised_by(a.activation(hs[:, c, :], psH[:, c, 0, :], ACT.Silu))
                    for c in range(2):
                        act.wait_ge(o_ok.sem, o_ok.value(i, c + 1))
                        act.wait_ge(y_out[c].sem, y_out[c].value(i, 0))
                        ye_ok.raised_by(a.activation(ye[:, c, :, :].rearrange("p j d -> p (j d)"), psO[:, c, :], ACT.Copy))
                        act.wait_ge(ye_ok.sem, ye_ok.value(i, c + 1))
                        act.dma_start(YE[bass.ds(2 * CAP * i + CAP * c, CAP), :].rearrange("(j p) d -> p j d", p=P),
                                      ye[:, c, :, :]).then_inc(y_out[c].sem, 16)
                for c in range(2):
                    act.wait_ge(y_out[c].sem, 16 * (E // 2 + 1))


def combine(nc, A, X1, XNT, YE, S1, slots_dram, gates_dram, OUT):
    ctx = ExitStack()
    with ctx:
        sb = lambda name, shape, dt=F32: ctx.enter_context(nc.sbuf_tensor("c_" + name, shape, dt))
        sem = lambda name: ctx.enter_context(nc.semaphore("c_" + name))
        NROW = NBLK * TOPK
        sw_h = sb("sw_h", [P, 3, 2 * P], BF16)
        sw = sb("sw", [P, 3, 2 * P])
        xT = sb("xT", [P, 2, KD, S])
        x1 = sb("x1", [P, 2, NBLK, D])
        s1 = sb("s1", [P, 2, NBLK, D])
        hs = sb("hs", [P, S])
        hT = sb("hT", [P, S])
        slot = sb("slot", [P, 2, NROW], U32)
        gates = sb("gates", [P, 2, NROW])
        yr = sb("yr", [P, 2, NROW, D])
        acc = sb("acc", [P, NBLK, D])
        g1 = sb("g1", [P, NBLK, D])
        res = sb("res", [P, 2, NBLK, D])
        psH = ctx.enter_context(nc.psum_tensor("psHc", [P, 2, S], F32))
        psO = ctx.enter_context(nc.psum_tensor("psOc", [P, NBLK, D], F32))
        w_in, made, prep = sem("w_in"), sem("made"), sem("prep")
        with nc.Block() as block:
            @block.sync
            def _(sp):
                for k, n in enumerate(("sw1T", "sw3T")):
                    sp.dma_start(sw_h[:, k, :].rearrange("p (t n) -> p t n", n=I),
                                 A[n].rearrange("(t p) n -> p t n", p=P)).then_inc(w_in, 16)
                sp.dma_start(sw_h[:, 2, :], A["sw2T"]).then_inc(w_in, 16)
                sp.wait_ge(w_in, 48)

            @block.gpsimd
            def _(pool):
                nc.gpsimd.memset(yr[:, :, :, :], 0.0).then_inc(made, 1)
                pool.wait_ge(made, 1)

            @block.vector
            def _(dve):
                dve.wait_ge(w_in, 48)
                nc.vector.tensor_copy(sw[:, :, :], sw_h[:, :, :]).then_inc(prep, 1)
                dve.wait_ge(prep, 1)

        sig = lambda name, per, first=0: Signal(sem(name), per, first)
        each = lambda name, per, first=0: [sig(name + str(c), per, first) for c in range(2)]
        xT_in = each("xT_in", 16)
        x1_in = each("x1_in", 16)
        s1_in = each("s1_in", 16)
        r_in = each("r_in", 32)
        y_in = each("y_in", 16 * NROW)
        h_ok = sig("h_ok", 2, 2)
        sil_ok = sig("sil_ok", 2, 2)
        hT_ok = sig("hT_ok", 2, 2)
        o_ok = sig("o_ok", 2, 2)
        acc_ok = sig("acc_ok", 2, 2)
        g_ok = sig("g_ok", 2, 2)
        out_ok = sig("out_ok", 2, 2)
        stored = each("stored", 16, 16)
        cchain = sig("cchain", 2 * TOPK)
        alone_c = sem("alone_c")
        with nc.Block() as block:
            @block.sync
            def _(sp):
                for c in range(2):
                    sp.sem_inc(stored[c].sem, 16)
                with sp.Fori(0, B // 2) as i:
                    for c in range(2):
                        seq = lambda T: T[bass.ds(2 * i + c, 1), :, :]
                        sp.wait_ge(acc_ok.sem, acc_ok.value(i, c - 1))
                        sp.dma_start(slot[:, c, :], seq(slots_dram).rearrange("a p n -> (a p) n")).then_inc(r_in[c].sem, 16)
                        sp.dma_start(gates[:, c, :], seq(gates_dram).rearrange("a p n -> (a p) n")).then_inc(r_in[c].sem, 16)
                        sp.wait_ge(h_ok.sem, h_ok.value(i, c - 1))
                        sp.dma_start(xT[:, c, :, :], seq(XNT).rearrange("a (t p) s -> p (a t) s", p=P)).then_inc(xT_in[c].sem, 16)
                        sp.wait_ge(out_ok.sem, out_ok.value(i, c - 1))
                        sp.dma_start(x1[:, c, :, :], seq(X1).rearrange("a (j p) d -> p (a j) d", p=P)).then_inc(x1_in[c].sem, 16)
                        sp.dma_start(s1[:, c, :, :], S1[bass.ds(2 * i + c + 1, 1), :, :].rearrange("a (j p) d -> p (a j) d", p=P)
                                     ).then_inc(s1_in[c].sem, 16)

            @block.gpsimd
            def _(pool):
                g = nc.gpsimd
                with pool.Fori(0, B // 2) as i:
                    for c in range(2):
                        pool.wait_ge(r_in[c].sem, r_in[c].value(i, 32))
                        pool.sem_inc(alone_c, 1)
                        for r in range(NROW):
                            g.indirect_dma_start(
                                out=yr[:, c, r, :], out_offset=None, in_=YE,
                                in_offset=bass.IndirectOffsetOnAxis(ap=slot[:, c, r:r + 1], axis=0),
                                bounds_check=E * CAP - 1, oob_is_err=False).then_inc(y_in[c].sem, 16)

            @block.tensor
            def _(pe):
                t = nc.tensor
                pe.sem_inc(h_ok.sem, 2)
                pe.sem_inc(o_ok.sem, 2)
                with pe.Fori(0, B // 2) as i:
                    for c in range(2):
                        pe.wait_ge(xT_in[c].sem, xT_in[c].value(i, 16))
                        pe.wait_ge(hT_ok.sem, hT_ok.value(i, c))
                        for n in range(2):
                            for k in range(KD):
                                ins = t.matmul(psH[:, n, :], sw[:, n, k * I:(k + 1) * I], xT[:, c, k, :],
                                               start=(k == 0), stop=(k == KD - 1))
                        h_ok.raised_by(ins)
                        pe.wait_ge(hT_ok.sem, hT_ok.value(i, c + 1))
                        pe.wait_ge(acc_ok.sem, acc_ok.value(i, c))
                        for j in range(NBLK):
                            ins = t.matmul(psO[:, j, :], hT[:, j * P:(j + 1) * P], sw[:, 2, :], start=True, stop=True)
                        o_ok.raised_by(ins)

            @block.scalar
            def _(act):
                a = nc.scalar
                act.sem_inc(sil_ok.sem, 2)
                act.sem_inc(g_ok.sem, 2)
                with act.Fori(0, B // 2) as i:
                    for c in range(2):
                        act.wait_ge(h_ok.sem, h_ok.value(i, c + 1))
                        act.wait_ge(hT_ok.sem, hT_ok.value(i, c))
                        sil_ok.raised_by(a.activation(hs[:, :], psH[:, 0, :], ACT.Silu))
                        act.wait_ge(acc_ok.sem, acc_ok.value(i, c + 1))
                        act.wait_ge(out_ok.sem, out_ok.value(i, c))
                        g_ok.raised_by(a.activation(g1[:, :, :], acc[:, :, :], ACT.Silu))
                        act.wait_ge(out_ok.sem, out_ok.value(i, c + 1))
                        act.dma_start(OUT[bass.ds(2 * i + c, 1), :, :].rearrange("a (j p) d -> p (a j) d", p=P),
                                      res[:, c, :, :]).then_inc(stored[c].sem, 16)
                for c in range(2):
                    act.wait_ge(stored[c].sem, 16 * (B // 2 + 1))

            @block.vector
            def _(dve):
                v = nc.vector
                for s in (hT_ok, acc_ok, out_ok):
                    dve.sem_inc(s.sem, 2)
                with dve.Fori(0, B // 2) as i:
                    def link(ins):
                        cchain.raised_by(ins)
                        dve.wait_ge(cchain.sem, cchain.value(i, cchain.n))

                    for c in range(2):
                        dve.wait_ge(sil_ok.sem, sil_ok.value(i, c + 1))
                        dve.wait_ge(o_ok.sem, o_ok.value(i, c))
                        hT_ok.raised_by(v.tensor_tensor(hT[:, :], hs[:, :], psH[:, 1, :], ALU.mult))
                        dve.wait_ge(o_ok.sem, o_ok.value(i, c + 1))
                        dve.wait_ge(g_ok.sem, g_ok.value(i, c))
                        dve.wait_ge(y_in[c].sem, y_in[c].value(i, 16 * NROW))
                        for k in range(TOPK):
                            for j in range(NBLK):
                                r = j * TOPK + k
                                ins = v.scalar_tensor_tensor(acc[:, j, :], yr[:, c, r, :], gates[:, c, r:r + 1],
                                                             psO[:, j, :] if k == 0 else acc[:, j, :], ALU.mult, ALU.add)
                            if k < TOPK - 1:
                                link(ins)
                        acc_ok.raised_by(ins)
                        dve.wait_ge(g_ok.sem, g_ok.value(i, c + 1))
                        dve.wait_ge(s1_in[c].sem, s1_in[c].value(i, 16))
                        dve.wait_ge(stored[c].sem, stored[c].value(i, 0))
                        link(v.tensor_tensor(res[:, c, :, :], g1[:, :, :], s1[:, c, :, :], ALU.mult))
                        dve.wait_ge(x1_in[c].sem, x1_in[c].value(i, 16))
                        ins = v.tensor_tensor(res[:, c, :, :], res[:, c, :, :], x1[:, c, :, :], ALU.add)
                        out_ok.raised_by(ins)
                assert cchain.n == 2 * TOPK, cchain.n


def program(nc, A, out):
    X1 = nc.dram_tensor("x1_rows", [B, S, D], F32).ap()
    XNT = nc.dram_tensor("xn_feature_major", [B, D, S], F32).ap()
    XE = nc.dram_tensor("expert_rows", [E * CAP, D], F32).ap()
    YE = nc.dram_tensor("expert_outputs", [E * CAP, D], F32).ap()
    S1 = nc.dram_tensor("mixed_rows", [B + 1, S, D], F32).ap()
    slots = nc.dram_tensor("token_slots", [B, P, NBLK * TOPK], U32).ap()
    gates = nc.dram_tensor("token_gates", [B, P, NBLK * TOPK], F32).ap()
    layer0(nc, A, X1, XNT, XE, slots, gates)
    layer1_mixer(nc, A, XNT, S1)
    experts(nc, A, XE, YE)
    combine(nc, A, X1, XNT, YE, S1, slots, gates, out)


def layouts(i):
    c = np.ascontiguousarray

    def slots32(w, heads):
        o = np.zeros((w.shape[0], heads, 32), w.dtype)
        o[:, :, :HD] = w.reshape(w.shape[0], heads, HD)
        return c(o.reshape(w.shape[0], heads * 32))

    def slots32_column(v, heads):
        o = np.zeros((heads, 32), v.dtype)
        o[:, :HD] = v.reshape(heads, HD)
        return c(o.reshape(-1, P).T)

    q, qb = i["L0_attn_qkv_w"], i["L0_attn_qkv_b"]
    r, rb = i["L0_attn_rkv_w"], i["L0_attn_rkv_b"]
    A = {"x": c(i["L0_attn_x"]),
         "wq": slots32(q[:, 0:D], H), "wk": slots32(q[:, D:2 * D], H), "wv": c(q[:, 2 * D:]),
         "bq": slots32_column(qb[0:D], H), "bk": slots32_column(qb[D:2 * D], H), "bv": c(qb[2 * D:]),
         "wrq": slots32(i["L0_attn_rq_w"], LH), "brq": slots32_column(i["L0_attn_rq_b"], LH),
         "wrk": slots32(r[:, :LAT], LH), "brk": slots32_column(rb[:LAT], LH), "wrv": c(r[:, LAT:]), "brv": c(rb[LAT:]),
         "wro": c(i["L0_attn_rout_w"]), "bro": c(i["L0_attn_rout_b"]),
         "wo": c(i["L0_attn_out_w"]), "bo": c(i["L0_attn_out_b"]),
         "gl": c(i["L0_attn_gl_w"][:, 0]), "gr": c(i["L0_attn_gr_w"][:, 0]),
         "wfcT": c(i["L0_ffn_W_fc"].T), "wpjT": c(i["L0_ffn_W_proj"].T),
         "lnw": c(i["L0_ffn_ln_w"]), "lnb": c(i["L0_ffn_ln_b"]),
         "gateT": c(i["L1_ffn_gate_w"].T), "ebias": c(i["L1_ffn_bias"]),
         "gam": c(i["L1_attn_ln_gamma"]), "bet": c(i["L1_attn_ln_beta"]),
         "W1": c(i["L1_ffn_W1"]), "W3": c(i["L1_ffn_W3"]), "W2": c(i["L1_ffn_W2"]),
         "sw1T": c(i["L1_ffn_sw1"].T), "sw3T": c(i["L1_ffn_sw3"].T), "sw2T": c(i["L1_ffn_sw2"].T)}
    column = lambda v: c(v.reshape(M, P).T)
    for way, n in (("fwd", "f"), ("bwd", "b")):
        g = lambda k: i["L1_attn_" + way + "_" + k]
        xp = g("x_proj_w")
        A[n + "_win"] = c(g("in_proj_w").T)
        A[n + "_wbc"] = c(np.concatenate([xp[RK:].T] * 3, axis=1))
        A[n + "_wdr"] = c(xp[:RK].T)
        A[n + "_wdt"] = c(g("dt_proj_w").T)
        A[n + "_wout"] = c(g("out_proj_w").T)
        A[n + "_cw"] = c(g("conv_w"))
        A[n + "_cb"], A[n + "_db"], A[n + "_dd"] = column(g("conv_b")), column(g("dt_proj_b")), column(g("D"))
        A[n + "_al"] = c(g("A_log"))
    return A


def kernel(**inputs):
    import concourse.bacc as bacc
    from concourse.bass_utils import run_bass_kernel_spmd

    arrays = layouts({k: np.asarray(v) for k, v in inputs.items()})
    nc = bacc.Bacc("TRN2", target_bir_lowering=False, num_devices=1)
    A = {k: nc.dram_tensor(k, a.shape, mybir.dt.from_np(a.dtype), kind="ExternalInput").ap() for k, a in arrays.items()}
    out = nc.dram_tensor("out", (B, S, D), F32, kind="ExternalOutput").ap()
    program(nc, A, out)
    r = run_bass_kernel_spmd(nc, [arrays], core_ids=[0])
    return r.results[0]["out"]
```

```python
import concourse.bass as bass
from concourse import mybir
from contextlib import ExitStack

import numpy as np

F32 = mybir.dt.float32
BF16 = mybir.dt.bfloat16
U32 = mybir.dt.uint32
ALU = mybir.AluOpType
ACT = mybir.ActivationFunctionType
AX = mybir.AxisListType

P = 128
B, S, D = 16, 512, 256
NBLK = S // P
KD = D // P
H, HD = 16, 16
G = 4
HG = H // G
HT = P // HD
QT = H // HT
LAT, LH = 64, 4
CH = S // LAT
HID = 1024
E, TOPK, CAP, I = 32, 4, 256, 128
VW = HD + 1
LN_EPS = 1e-5
NEG = -1e9
FAR = 1048576.0


DCHAIN = 84
MFIRST, MCHAIN = 14, 35


class Signal:

    def __init__(self, sem, per, first=0):
        self.sem, self.per, self.first, self.n = sem, per, first, 0

    def raised_by(self, ins, by=1):
        ins.then_inc(self.sem, by)
        self.n += by
        return ins

    def value(self, i, n):
        return i * self.per + (self.first + n)

    def whole(self):
        assert self.n == self.per, (str(self.sem), self.n, self.per)


def layer0(nc, A, X1, XNT, XE, slots_dram, gates_dram):
    ctx = ExitStack()
    with ctx:
        sb = lambda name, shape, dt=F32: ctx.enter_context(nc.sbuf_tensor("sb_" + name, shape, dt))
        sem = lambda name: ctx.enter_context(nc.semaphore(name))

        wq = sb("wq", [P, KD, D])
        wk = sb("wk", [P, KD, D])
        bq = sb("bq", [P, QT])
        bk = sb("bk", [P, QT])
        wv = sb("wv", [P, KD, D])
        bv = sb("bv", [1, D])
        wrq = sb("wrq", [P, KD, P])
        brq = sb("brq", [P, 1])
        wrk = sb("wrk", [P, KD, P])
        brk = sb("brk", [P, 1])
        wrv = sb("wrv", [P, KD, LAT])
        brv = sb("brv", [1, LAT])
        wro = sb("wro", [LAT, D])
        bro = sb("bro", [1, D])
        wo = sb("wo", [P, KD, D])
        bo = sb("bo", [1, D])
        gl = sb("gl", [P, HD])
        gr = sb("gr", [P, HD])
        wfc = sb("wfc", [P, KD, HID])
        wpj = sb("wpj", [P, HID // P, D])
        lnw = sb("lnw", [P, HID // P])
        lnb = sb("lnb", [P, HID // P])
        wmean = sb("wmean", [P, D])
        ffb = sb("ffb", [P, D])
        gate_h = sb("gate_h", [P, KD, E], BF16)
        gate_w = sb("gate_w", [P, KD, E])
        ebias = sb("ebias", [P, E])
        ident = sb("ident", [P, P])
        ident_h = sb("ident_h", [P, P], BF16)
        ones_row = sb("ones_row", [1, P])
        ones_sq = sb("ones_sq", [P, P])
        ones_h = sb("ones_h", [P, P], BF16)
        before = sb("before", [P, P], BF16)
        mask = sb("mask", [P, 2, 2, P], BF16)
        lmask = sb("lmask", [P, NBLK, LH, LAT], BF16)
        slot_of = sb("slot_of", [P, HT])
        row_ok = sb("row_ok", [P, 1])
        qscale = sb("qscale", [P, HT])
        qbias = sb("qbias", [P, QT, HT])
        rqbias = sb("rqbias", [P, HT])
        lat_ok = sb("lat_ok", [P, 1])
        iota_e = sb("iota_e", [P, E])
        iota_s = sb("iota_s", [P, E])
        half = sb("half", [P, NBLK])
        absum = sb("absum", [P, 4])
        thr = sb("thr", [P, 2])
        nthr = sb("nthr", [P, 2])
        zero = sb("zero", [P, 2048])

        xa = sb("xa", [P, NBLK, D])
        xr = sb("xr", [P, NBLK, D])
        bnst = sb("bnst", [P, NBLK, 6])
        mv = sb("mv", [P, NBLK, 2])
        rstd = sb("rstd", [P, NBLK])
        xn = sb("xn", [P, NBLK, D])
        xnT = sb("xnT", [P, KD, S])
        pooled = sb("pooled", [P, KD, LAT])
        kT = sb("kT", [P, QT, S])
        qX = sb("qX", [P, QT, HT, S])
        rqX = sb("rqX", [P, G, S])
        vv = sb("vv", [P, NBLK, H, VW])
        rkT = sb("rkT", [P, LAT])
        rvv = sb("rvv", [LAT, LH, VW])
        nmax = sb("nmax", [P, 2, G])
        pr = sb("pr", [P, 2, G, 2 * P])
        prT = sb("prT", [P, 2, G, 2, P])
        rinv = sb("rinv", [P, H])
        linv = sb("linv", [P, LH])
        loc = sb("loc", [P, H, HD])
        lat = sb("lat", [P, LH, HD])
        latT = sb("latT", [LAT, P])
        rem = sb("rem", [P, H, HD])
        t1 = sb("t1", [P, H, HD])
        t2 = sb("t2", [P, H, HD])
        zg = sb("zg", [P, H])
        eg = sb("eg", [P, H])
        mix = sb("mix", [P, H, HD])
        mixT = sb("mixT", [P, KD, P])
        s0 = sb("s0", [P, NBLK, D])
        hid = sb("hid", [P, 2, HID])
        hst = sb("hst", [P, 2, 2, 6])
        hmv = sb("hmv", [P, 2, 2])
        hrs = sb("hrs", [P, 2])
        hidT = sb("hidT", [P, 2, HID // P, P])
        ff = sb("ff", [P, NBLK, D])
        x1 = sb("x1", [P, NBLK, D])
        xn2 = sb("xn2", [P, NBLK, D])
        xn2T = sb("xn2T", [P, KD, S])
        esc = sb("esc", [P, NBLK, E])
        sc = sb("sc", [P, NBLK, E])
        sbias = sb("sbias", [P, NBLK, E])
        top = sb("top", [P, NBLK, 8])
        topi = sb("topi", [P, NBLK, 8], U32)
        topf = sb("topf", [P, NBLK, TOPK])
        hot = sb("hot", [P, NBLK, TOPK, E])
        tmp = sb("tmp", [P, NBLK, TOPK, E])
        sel = sb("sel", [P, NBLK, E])
        sel_h = sb("sel_h", [P, NBLK, E], BF16)
        taken = sb("taken", [P, E])
        pos = sb("pos", [P, NBLK, E])
        over = sb("over", [P, NBLK, E])
        slotf = sb("slotf", [P, NBLK, TOPK])
        slot = sb("slot", [P, NBLK, TOPK], U32)
        gw = sb("gw", [P, NBLK, TOPK])
        gsum = sb("gsum", [P, NBLK])
        keep = sb("keep", [P, NBLK, TOPK])
        gout = sb("gout", [P, NBLK, TOPK])

        psS = ctx.enter_context(nc.psum_tensor("psS", [P, 4, 512], F32))
        psT = ctx.enter_context(nc.psum_tensor("psT", [P, 1024], F32))
        po = ctx.enter_context(nc.psum_tensor("po", [P, 2, 512], F32))

        w_in = sem("w_in")
        made = sem("made")
        all_made = sem("all_made")
        prep = sem("prep")
        summed = sem("summed")
        zeroed = sem("zeroed")
        plain = [(wq, "wq"), (wk, "wk"), (wv, "wv"), (wrq, "wrq"), (wrk, "wrk"), (wrv, "wrv"),
                 (wo, "wo"), (wfc, "wfcT"), (wpj, "wpjT"), (gate_h, "gateT")]
        flat = [(bq, "bq"), (bk, "bk"), (brq, "brq"), (brk, "brk"), (wro, "wro"), (lnw, "lnw"), (lnb, "lnb")]
        rows = [(bv, "bv"), (brv, "brv"), (bro, "bro"), (bo, "bo")]
        spread = [(gl, "gl"), (gr, "gr"), (ebias, "ebias")]
        NLOAD = len(plain) + len(flat) + len(rows) + len(spread)
        with nc.Block() as block:
            @block.sync
            def _(sp):
                for t, n in plain:
                    sp.dma_start(t[:, :, :], A[n].rearrange("(t p) n -> p t n", p=P)).then_inc(w_in, 16)
                for t, n in flat:
                    sp.dma_start(t[:, :], A[n]).then_inc(w_in, 16)
                for t, n in rows:
                    sp.dma_start(t[:, :], A[n].unsqueeze(0)).then_inc(w_in, 16)
                for t, n in spread:
                    sp.dma_start(t[:, :], A[n].partition_broadcast(P)).then_inc(w_in, 16)
                sp.wait_ge(made, 1)
                sp.dma_start(XE.rearrange("(p n) d -> p n d", p=P)[:, 0:8, :],
                             zero[:, :].rearrange("p (n d) -> p n d", d=D)).then_inc(zeroed, 16)
                for k in range(1, E * CAP // P // 8):
                    sp.dma_start(XE.rearrange("(p n) d -> p n d", p=P)[:, 8 * k:8 * k + 8, :],
                                 zero[:, :].rearrange("p (n d) -> p n d", d=D)).then_inc(zeroed, 16)
                sp.wait_ge(zeroed, 16 * (E * CAP // P // 8))
                sp.wait_ge(w_in, 16 * NLOAD)

            @block.gpsimd
            def _(pool):
                g = nc.gpsimd
                m = [0]

                def link(ins):
                    ins.then_inc(made, 1)
                    m[0] += 1
                    pool.wait_ge(made, m[0])

                link(g.memset(zero[:, :], 0.0))
                link(g.memset(ones_sq[:, :], 1.0))
                link(g.memset(ones_h[:, :], 1.0))
                link(g.memset(ones_row[:, :], 1.0))
                link(g.memset(ident[:, :], 0.0))
                link(g.affine_select(out=ident[:, :], in_=ident[:, :], compare_op=ALU.not_equal, fill=1.0,
                                     base=0, pattern=[[-1, P]], channel_multiplier=1))
                link(g.memset(ident_h[:, :], 0.0))
                link(g.affine_select(out=ident_h[:, :], in_=ident_h[:, :], compare_op=ALU.not_equal, fill=1.0,
                                     base=0, pattern=[[-1, P]], channel_multiplier=1))
                link(g.affine_select(out=before[:, :], in_=ones_h[:, :], compare_op=ALU.is_gt, fill=0.0,
                                     base=0, pattern=[[1, P]], channel_multiplier=-1))
                link(g.memset(mask[:, :, :, :], 0.0))
                for r in range(2):
                    link(g.affine_select(out=mask[:, r, 0, :], in_=mask[:, r, 0, :], compare_op=ALU.is_ge, fill=NEG,
                                         base=0, pattern=[[1, P]], channel_multiplier=-1))
                    link(g.affine_select(out=mask[:, r, 0, :], in_=mask[:, r, 0, :], compare_op=ALU.is_gt, fill=NEG,
                                         base=0, pattern=[[1, P]], channel_multiplier=0))
                    link(g.affine_select(out=mask[:, r, 1, :], in_=mask[:, r, 1, :], compare_op=ALU.is_gt, fill=NEG,
                                         base=0, pattern=[[-1, P]], channel_multiplier=1))
                link(g.memset(lmask[:, :, :, :], 0.0))
                for j in range(NBLK):
                    link(g.affine_select(out=lmask[:, j, :, :], in_=lmask[:, j, :, :], compare_op=ALU.is_gt, fill=NEG,
                                         base=j * P - (CH - 1), pattern=[[0, LH], [-CH, LAT]], channel_multiplier=1))
                link(g.affine_select(out=slot_of[:, :], in_=ones_sq[:, 0:HT], compare_op=ALU.is_ge, fill=0.0,
                                     base=0, pattern=[[-HD, HT]], channel_multiplier=1))
                link(g.affine_select(out=slot_of[:, :], in_=slot_of[:, :], compare_op=ALU.is_ge, fill=0.0,
                                     base=HD - 1, pattern=[[HD, HT]], channel_multiplier=-1))
                link(g.affine_select(out=row_ok[:, :], in_=ones_sq[:, 0:1], compare_op=ALU.is_gt, fill=0.0,
                                     base=0, pattern=[[0, 1]], channel_multiplier=1))
                link(g.affine_select(out=lat_ok[:, :], in_=ones_sq[:, 0:1], compare_op=ALU.is_gt, fill=0.0,
                                     base=-(CH - 1), pattern=[[0, 1]], channel_multiplier=1))
                link(g.iota(iota_e[:, :], [[1, E]], base=0, channel_multiplier=0,
                            allow_small_or_imprecise_dtypes=True))
                link(g.iota(iota_s[:, :], [[CAP, E]], base=0, channel_multiplier=0,
                            allow_small_or_imprecise_dtypes=True))
                link(g.memset(half[:, :], -0.5))
                link(g.memset(vv[:, :, :, HD:VW], 1.0))
                link(g.memset(rvv[:, :, HD:VW], 1.0))
                link(g.memset(taken[:, :], 0.0))
                link(g.memset(xn2[:, :, :], 0.0))
                link(g.iota(slotf[:, :, :], [[1, NBLK * TOPK]], base=0, channel_multiplier=NBLK * TOPK,
                            allow_small_or_imprecise_dtypes=True))
                link(g.memset(prT[:, :, :, :, :], 0.0))
                pool.sem_inc(all_made, 1)

            @block.vector
            def _(dve):
                v = nc.vector
                n = [0]

                def link(ins):
                    ins.then_inc(prep, 1)
                    n[0] += 1
                    dve.wait_ge(prep, n[0])

                dve.wait_ge(w_in, 16 * NLOAD)
                dve.wait_ge(all_made, 1)
                link(v.tensor_copy(gate_w[:, :, :], gate_h[:, :, :]))
                for k, w in enumerate((wfc, wpj)):
                    link(v.tensor_reduce(absum[:, k:k + 1], w[:, :, :], axis=AX.XY, op=ALU.add,
                                         apply_absolute_value=True))
                dve.wait_ge(summed, 1)
                link(v.tensor_scalar(thr[:, :], psT[:, 0:2], 1.0 / (HID * D), 1e-6, ALU.mult, ALU.add))
                link(v.tensor_scalar(nthr[:, :], thr[:, :], -0.5, None, ALU.mult))
                link(v.tensor_scalar(thr[:, :], thr[:, :], 0.5, None, ALU.mult))
                for k, (w, other) in enumerate(((wfc, hid), (wpj, hidT))):
                    o = other[:, :, :] if k == 0 else other[:, :, :, :].rearrange("p a b c -> p (a b c)")
                    o = o if k == 0 else o.rearrange("p (t n) -> p t n", n=D)
                    link(v.tensor_scalar(o, w[:, :, :], nthr[:, k:k + 1], None, ALU.is_lt))
                    link(v.scalar_tensor_tensor(w[:, :, :], w[:, :, :], thr[:, k:k + 1], o,
                                                ALU.is_gt, ALU.subtract))
                for k in range(HID // P):
                    link(v.tensor_scalar(hid[:, 0, k * P:(k + 1) * P], ones_sq[:, :], lnb[:, k:k + 1], None, ALU.mult))
                dve.wait_ge(summed, 2)
                link(v.tensor_copy(ffb[:, :], psT[:, 0:D]))
                for k in range(HID // P):
                    link(v.tensor_scalar(wpj[:, k, :], wpj[:, k, :], lnw[:, k:k + 1], None, ALU.mult))
                dve.wait_ge(summed, 3)
                link(v.tensor_scalar(wmean[:, :], psT[:, 0:D], 1.0 / HID, None, ALU.mult))
                link(v.tensor_tensor(wpj[:, :, :], wpj[:, :, :],
                                     wmean[:, :].unsqueeze(1).to_broadcast([P, HID // P, D]), ALU.subtract))
                link(v.tensor_scalar(qscale[:, :], slot_of[:, :], 0.25, None, ALU.mult))
                for g_ in range(QT):
                    link(v.tensor_scalar(qbias[:, g_, :], qscale[:, :], bq[:, g_:g_ + 1], None, ALU.mult))
                link(v.tensor_scalar(rqbias[:, :], qscale[:, :], brq[:, 0:1], None, ALU.mult))
                link(v.tensor_copy(slot[:, :, :], slotf[:, :, :]))

            @block.tensor
            def _(pe):
                pe.wait_ge(made, 2)
                pe.wait_ge(prep, 3)
                nc.tensor.matmul(psT[:, 0:2], ones_sq[:, :], absum[:, 0:2], start=True, stop=True).then_inc(summed, 1)
                pe.wait_ge(prep, 10 + HID // P)
                for k in range(HID // P):
                    ins = nc.tensor.matmul(psT[:, 0:D], hid[:, 0, k * P:(k + 1) * P], wpj[:, k, :],
                                           start=(k == 0), stop=(k == HID // P - 1))
                ins.then_inc(summed, 1)
                pe.wait_ge(prep, 11 + 2 * (HID // P))
                for k in range(HID // P):
                    ins = nc.tensor.matmul(psT[:, 0:D], ones_sq[:, :], wpj[:, k, :],
                                           start=(k == 0), stop=(k == HID // P - 1))
                ins.then_inc(summed, 1)

        NU = NBLK * (HG + 1)
        sig = lambda name, per, first=0: Signal(sem(name), per, first)
        xa_in = sig("xa_in", 16, 16)
        xr_in = sig("xr_in", 16)
        xa_free = sig("xa_free", 1, 1)
        xr_free = sig("xr_free", 1, 1)
        var_ok = sig("var_ok", 1, 1)
        rstd_ok = sig("rstd_ok", 2, 2)
        xn_ok = sig("xn_ok", 1, 1)
        xnT_tr = sig("xnT_tr", 1, 1)
        xnT_ok = sig("xnT_ok", 1, 1)
        pooled_ok = sig("pooled_ok", 1, 1)
        proj = sig("proj", 10, 10)
        proj_a = sig("proj_a", 7, 7)
        proj_v = sig("proj_v", 4, 4)
        s_ok = sig("s_ok", NU)
        max_ok = sig("max_ok", NU)
        exp_ok = sig("exp_ok", NU)
        tr_ok = sig("tr_ok", NU)
        cp_ok = sig("cp_ok", NU)
        pv_ok = sig("pv_ok", NU)
        lat_done = sig("lat_done", NBLK)
        gate_in = sig("gate_in", NBLK)
        gate_ok = sig("gate_ok", NBLK)
        mix_ok = sig("mix_ok", NBLK)
        post_t = sig("post_t", 4 * NBLK)
        post_cp = sig("post_cp", 4 * NBLK)
        h_ok = sig("h_ok", NBLK)
        gelu_ok = sig("gelu_ok", NBLK)
        hvar_ok = sig("hvar_ok", NBLK)
        hrs_ok = sig("hrs_ok", 2 * NBLK)
        ht_tr = sig("ht_tr", NBLK)
        ht_ok = sig("ht_ok", NBLK)
        pj_ok = sig("pj_ok", NBLK)
        ff_ok = sig("ff_ok", NBLK)
        silu_ok = sig("silu_ok", 1)
        x1_ok = sig("x1_ok", 1)
        var2_ok = sig("var2_ok", 1)
        rstd2_ok = sig("rstd2_ok", 2)
        xn2_ok = sig("xn2_ok", 1)
        xn2T_tr = sig("xn2T_tr", 1)
        xn2T_ok = sig("xn2T_ok", 1)
        logit_ok = sig("logit_ok", 1)
        esc_ok = sig("esc_ok", 1)
        sel_ok = sig("sel_ok", 1)
        count_ok = sig("count_ok", 1)
        slot_ok = sig("slot_ok", 1, 1)
        stored = sig("stored", 16 * 4, 16 * 4)
        scattered = sig("scattered", 16 * NBLK * TOPK)
        dchain = sig("dchain", DCHAIN)
        headchain = sig("headchain", 2, 2)
        alone_p, alone_v, alone_t = sem("alone_p"), sem("alone_v"), sem("alone_t")

        def in_head(b, s, n):
            return n if b is None else s.value(b, n)

        def raise_head(b, s, ins):
            ins.then_inc(s.sem, 1) if b is None else s.raised_by(ins)

        def span(u):
            if u % (HG + 1) == HG:
                return 0, LAT
            j = u // (HG + 1)
            return (0, P) if j == 0 else ((j - 1) * P, 2 * P)

        def scored(u):
            nk = span(u)[1]
            if nk == LAT:
                return psS[:, 2 * (u % 2), 0:LH * LAT].rearrange("p (h n) -> p h n", n=LAT)
            both = psS[:, 2 * (u % 2):2 * (u % 2) + 2, :].rearrange("p c (h n) -> p (c h) n", n=2 * P)
            return both[:, :, 2 * P - nk:2 * P]

        with nc.Block() as block:
            @block.sync
            def _(sp):
                sp.sem_inc(stored.sem, 16 * 4)
                rows = lambda T, n: T[bass.ds(n, 1), :, :].rearrange("a (j p) d -> p (a j) d", p=P)

                def traffic(b, following):
                    sp.wait_ge(xr_free.sem, xr_free.value(b, 0))
                    sp.dma_start(xr[:, :, :], rows(A["x"], b)).then_inc(xr_in.sem, 16)
                    sp.wait_ge(xa_free.sem, xa_free.value(b, 0))
                    sp.dma_start(xa[:, :, :], rows(A["x"], following)).then_inc(xa_in.sem, 16)
                    sp.wait_ge(x1_ok.sem, x1_ok.value(b, 1))
                    sp.dma_start(rows(X1, b), x1[:, :, :]).then_inc(stored.sem, 16)
                    sp.wait_ge(xn2T_ok.sem, xn2T_ok.value(b, 1))
                    sp.dma_start(XNT[bass.ds(b, 1), :, :].rearrange("a (t p) s -> p (a t) s", p=P), xn2T[:, :, :]
                                 ).then_inc(stored.sem, 16)
                    sp.wait_ge(slot_ok.sem, slot_ok.value(b, 1))
                    sp.dma_start(slots_dram[bass.ds(b, 1), :, :].rearrange("a p n -> (a p) n"),
                                 slot[:, :, :].rearrange("p a b -> p (a b)")).then_inc(stored.sem, 16)
                    sp.dma_start(gates_dram[bass.ds(b, 1), :, :].rearrange("a p n -> (a p) n"),
                                 gout[:, :, :].rearrange("p a b -> p (a b)")).then_inc(stored.sem, 16)

                sp.dma_start(xa[:, :, :], rows(A["x"], 0)).then_inc(xa_in.sem, 16)
                with sp.Fori(0, B - 1) as b:
                    traffic(b, b + 1)
                traffic(B - 1, B - 1)
                sp.wait_ge(stored.sem, 16 * 4 * (B + 1))

            @block.gpsimd
            def _(pool):
                g = nc.gpsimd
                def scatter():
                    for j in range(NBLK):
                        for k in range(TOPK):
                            g.indirect_dma_start(
                                out=XE, out_offset=bass.IndirectOffsetOnAxis(ap=slot[:, j, k:k + 1], axis=0),
                                in_=xn2[:, j, :], in_offset=None, bounds_check=E * CAP - 1, oob_is_err=False,
                            ).then_inc(scattered.sem, 16)

                def rsqrt(out, var, ready, ready_n, sig_, b, n=0):
                    pool.wait_ge(ready.sem, in_head(b, ready, ready_n))
                    pool.sem_inc(alone_p, 1)
                    raise_head(b, sig_, g.tensor_scalar(out, var, LN_EPS, None, ALU.add))
                    pool.wait_ge(sig_.sem, in_head(b, sig_, n + 1))
                    w = out.shape[1]
                    raise_head(b, sig_, g.tensor_tensor(out, out, half[:, 0:w], ALU.pow))

                rsqrt(rstd[:, :], mv[:, :, 1], var_ok, 1, rstd_ok, None)
                with pool.Fori(0, B) as b:
                    pool.wait_ge(slot_ok.sem, slot_ok.value(b, 0))
                    pool.sem_inc(alone_p, 1)
                    scatter()
                    rsqrt(rstd[:, :], mv[:, :, 1], var_ok, 1, rstd_ok, b)
                    for j in range(NBLK):
                        rsqrt(hrs[:, j % 2:j % 2 + 1], hmv[:, j % 2, 1:2], hvar_ok, j + 1, hrs_ok, b, 2 * j)
                    rsqrt(rstd[:, :], mv[:, :, 1], var2_ok, 1, rstd2_ok, b)
                pool.wait_ge(slot_ok.sem, B + 1)
                pool.sem_inc(alone_p, 1)
                scatter()
                pool.wait_ge(scattered.sem, 16 * NBLK * TOPK * (B + 1))
                for s in (rstd_ok, hrs_ok, rstd2_ok):
                    s.whole()

            @block.scalar
            def _(act):
                a = nc.scalar

                def head_q(b, tile, n):
                    act.wait_ge(proj.sem, in_head(b, proj, n))
                    for h in range(HT):
                        ins = a.activation(qX[:, tile, h, :], psS[:, n - 1, :], ACT.Identity,
                                           bias=qbias[:, tile, h:h + 1], scale=qscale[:, h:h + 1])
                    raise_head(b, proj_a, ins)

                def head_qk(b):
                    act.wait_ge(xnT_tr.sem, in_head(b, xnT_tr, 1))
                    raise_head(b, xnT_ok, a.activation(xnT[:, :, :].rearrange("p t s -> p (t s)"), psT[:, :], ACT.Copy))
                    head_q(b, 0, 1)
                    for tile in range(QT):
                        act.wait_ge(proj.sem, in_head(b, proj, 2 + tile))
                        raise_head(b, proj_a, a.activation(kT[:, tile, :], psS[:, 1 + tile, :], ACT.Identity,
                                                           bias=bk[:, tile:tile + 1], scale=1.0))

                def head_latent(b):
                    act.wait_ge(proj.sem, in_head(b, proj, 9))
                    for h in range(LH):
                        ins = a.activation(rqX[:, h, :], psS[:, 0, :], ACT.Identity, bias=rqbias[:, h:h + 1],
                                           scale=qscale[:, h:h + 1])
                    raise_head(b, proj_a, ins)
                    act.wait_ge(proj.sem, in_head(b, proj, 10))
                    raise_head(b, proj_a, a.activation(rkT[:, :], psS[:, 1, 0:LAT], ACT.Identity,
                                                       bias=brk[:, 0:1], scale=1.0))
                    raise_head(b, proj_a, a.activation(rvv[:, :, 0:HD],
                                                       psS[0:LAT, 1, LAT:2 * LAT].rearrange("p (h d) -> p h d", d=HD),
                                                       ACT.Copy))

                head_qk(None)
                head_q(None, 1, 4)
                head_latent(None)
                with act.Fori(0, B) as b:
                    def wait(s, n):
                        act.wait_ge(s.sem, s.value(b, n))

                    for u in range(NU):
                        k0, nk = span(u)
                        at = 2 * P - nk if nk > LAT else 0
                        wait(max_ok, u + 1)
                        if u >= 2:
                            wait(tr_ok, u - 1)
                        for h in range(G):
                            ins = a.activation(pr[:, u % 2, h, at:at + nk], scored(u)[:, h, :], ACT.Exp,
                                               bias=nmax[:, u % 2, h:h + 1], scale=1.0)
                        exp_ok.raised_by(ins)
                        if u > HG and u % (HG + 1) == 3:
                            q = u // (HG + 1)
                            wait(gate_in, q)
                            gate_ok.raised_by(a.activation(eg[:, :], zg[:, :], ACT.Exp, scale=-1.0))
                    wait(gate_in, NBLK)
                    gate_ok.raised_by(a.activation(eg[:, :], zg[:, :], ACT.Exp, scale=-1.0))

                    def gelu(j):
                        wait(h_ok, j + 1)
                        if j >= 2:
                            wait(ht_tr, j - 1)
                            wait(hvar_ok, j - 1)
                        gelu_ok.raised_by(a.activation(
                            hid[:, j % 2, :].rearrange("p (c n) -> p c n", c=2),
                            psS[:, 2 * (j % 2):2 * (j % 2) + 2, :], ACT.Gelu))

                    gelu(0)
                    gelu(1)
                    for j in range(NBLK):
                        wait(ht_tr, j + 1)
                        if j >= 2:
                            wait(pj_ok, j - 1)
                        ht_ok.raised_by(a.activation(hidT[:, j % 2, :, :].rearrange("p t n -> p (t n)"),
                                                     psT[:, :], ACT.Copy))
                        if j + 2 < NBLK:
                            gelu(j + 2)
                    wait(ff_ok, NBLK)
                    silu_ok.raised_by(a.activation(ff[:, :, :], ff[:, :, :], ACT.Silu))
                    head_qk(b)
                    wait(xn2T_tr, 1)
                    act.wait_ge(stored.sem, stored.value(b, 0))
                    xn2T_ok.raised_by(a.activation(xn2T[:, :, :].rearrange("p t s -> p (t s)"), psT[:, :], ACT.Copy))
                    wait(logit_ok, 1)
                    esc_ok.raised_by(a.activation(esc[:, :, :].rearrange("p a b -> p (a b)"), po[:, 0, 0:NBLK * E],
                                                  ACT.Exp, scale=-1.0))
                    head_q(b, 1, 4)
                    head_latent(b)
                for s in (xnT_ok, proj_a, exp_ok, gate_ok, gelu_ok, ht_ok, silu_ok, xn2T_ok, esc_ok):
                    s.whole()

            @block.vector
            def _(dve):
                v = nc.vector
                xa_free.n = 0
                dve.sem_inc(slot_ok.sem, 1)
                dve.sem_inc(xr_free.sem, 1)

                def stats(src, link):
                    for j in range(NBLK):
                        ins = v.bn_stats(bnst[:, j, :], src[:, j, :])
                    link(ins)
                    dve.sem_inc(alone_v, 1)
                    for j in range(NBLK):
                        ins = v.bn_aggr(mv[:, j, :], bnst[:, j, :])
                    return ins

                def normalize(dst, src):
                    for j in range(NBLK):
                        ins = v.tensor_scalar(dst[:, j, :], src[:, j, :], mv[:, j, 0:1], rstd[:, j:j + 1],
                                              ALU.subtract, ALU.mult)
                    return ins

                def head_norm(b):
                    def link(ins):
                        raise_head(b, headchain, ins)
                        dve.wait_ge(headchain.sem, in_head(b, headchain, 1))

                    dve.wait_ge(xa_in.sem, in_head(b, xa_in, 16))
                    raise_head(b, var_ok, stats(xa, link))
                    dve.wait_ge(var_ok.sem, in_head(b, var_ok, 1))
                    dve.wait_ge(rstd_ok.sem, in_head(b, rstd_ok, 2))
                    raise_head(b, xn_ok, normalize(xn, xa))
                    dve.wait_ge(xn_ok.sem, in_head(b, xn_ok, 1))
                    dve.sem_inc(xa_free.sem, 1)

                def head_pool(b):
                    dve.wait_ge(xnT_ok.sem, in_head(b, xnT_ok, 1))
                    raise_head(b, headchain, v.tensor_reduce(
                        pooled[:, :, :], xnT[:, :, :].rearrange("p t (l c) -> p t l c", c=CH), axis=AX.X, op=ALU.add))
                    dve.wait_ge(headchain.sem, in_head(b, headchain, 2))
                    raise_head(b, pooled_ok, v.tensor_scalar(pooled[:, :, :], pooled[:, :, :], 1.0 / CH, None, ALU.mult))

                def head_values(b):
                    for j in range(NBLK):
                        dve.wait_ge(proj.sem, in_head(b, proj, 5 + j))
                        raise_head(b, proj_v, v.tensor_copy(vv[:, j, :, 0:HD],
                                                            psS[:, j, 0:D].rearrange("p (h d) -> p h d", d=HD)))

                head_norm(None)
                head_pool(None)
                head_values(None)
                with dve.Fori(0, B) as b:
                    def wait(s, n):
                        dve.wait_ge(s.sem, s.value(b, n))

                    def link(ins):
                        dchain.raised_by(ins)
                        wait(dchain, dchain.n)

                    def tell(ins, s):
                        s.raised_by(ins)
                        wait(s, s.n)

                    def maxima(u):
                        wait(s_ok, u + 1)
                        tell(v.tensor_reduce(nmax[:, u % 2, :], scored(u), axis=AX.X, op=ALU.max,
                                             negate=True), max_ok)

                    def copy_probs(u):
                        k0, nk = span(u)
                        wait(tr_ok, u + 1)
                        if u >= 2:
                            wait(pv_ok, u - 1)
                        if nk == LAT:
                            ins = v.tensor_copy(prT[0:LAT, u % 2, :, 0, :],
                                                psT[0:LAT, :].rearrange("p (h k q) -> p h k q", h=G, k=2)[:, :, 0, :])
                        elif nk == P:
                            ins = v.tensor_copy(prT[:, u % 2, :, 1, :],
                                                psT[:, :].rearrange("p (h k q) -> p h k q", h=G, k=2)[:, :, 1, :])
                        else:
                            ins = v.tensor_copy(prT[:, u % 2, :, :, :].rearrange("p h k q -> p (h k q)"), psT[:, :])
                        tell(ins, cp_ok)

                    def post(q, stage):
                        if stage == 0:
                            wait(pv_ok, (HG + 1) * (q + 1))
                            o = po[:, q % 2, 0:H * VW].rearrange("p (h d) -> p h d", d=VW)
                            l = po[:, q % 2, H * VW:(H + LH) * VW].rearrange("p (h d) -> p h d", d=VW)
                            link(v.reciprocal(rinv[:, :], o[:, :, HD]))
                            link(v.reciprocal(linv[:, :], l[:, :, HD]))
                            if q == 0:
                                link(v.tensor_scalar(rinv[:, :], rinv[:, :], row_ok[:, 0:1], None, ALU.mult))
                                link(v.tensor_scalar(linv[:, :], linv[:, :], lat_ok[:, 0:1], None, ALU.mult))
                            link(v.tensor_tensor(loc[:, :, :], o[:, :, 0:HD],
                                                 rinv[:, :].unsqueeze(2).to_broadcast([P, H, HD]), ALU.mult))
                            tell(v.tensor_tensor(lat[:, :, :], l[:, :, 0:HD],
                                                 linv[:, :].unsqueeze(2).to_broadcast([P, LH, HD]), ALU.mult), lat_done)
                        if stage == 1:
                            wait(post_t, 4 * q + 1)
                            tell(v.tensor_copy(latT[:, :], psT[0:LAT, 0:P]), post_cp)
                        if stage == 2:
                            wait(post_t, 4 * q + 2)
                            tell(v.tensor_copy(rem[:, :, :].rearrange("p h d -> p (h d)"), psT[:, 0:D]), post_cp)
                            link(v.tensor_tensor(t1[:, :, :], loc[:, :, :],
                                                 gl[:, :].unsqueeze(1).to_broadcast([P, H, HD]), ALU.mult))
                            link(v.tensor_tensor(t2[:, :, :], rem[:, :, :],
                                                 gr[:, :].unsqueeze(1).to_broadcast([P, H, HD]), ALU.mult))
                            link(v.tensor_tensor(t1[:, :, :], t1[:, :, :], t2[:, :, :], ALU.add))
                            tell(v.tensor_reduce(zg[:, :], t1[:, :, :], axis=AX.X, op=ALU.add), gate_in)
                        if stage == 3:
                            wait(gate_ok, q + 1)
                            link(v.tensor_scalar(eg[:, :], eg[:, :], 1.0, None, ALU.add))
                            link(v.reciprocal(eg[:, :], eg[:, :]))
                            link(v.tensor_tensor(t1[:, :, :], loc[:, :, :], rem[:, :, :], ALU.subtract))
                            link(v.tensor_tensor(t1[:, :, :], t1[:, :, :],
                                                 eg[:, :].unsqueeze(2).to_broadcast([P, H, HD]), ALU.mult))
                            tell(v.tensor_tensor(mix[:, :, :], t1[:, :, :], rem[:, :, :], ALU.add), mix_ok)
                            wait(post_t, 4 * q + 3)
                            tell(v.tensor_copy(mixT[:, :, :].rearrange("p t n -> p (t n)"), psT[:, 0:D]), post_cp)
                        if stage == 4:
                            wait(post_t, 4 * q + 4)
                            tell(v.tensor_copy(s0[:, q, :], psT[:, 0:D]), post_cp)

                    maxima(0)
                    maxima(1)
                    for u in range(NU):
                        copy_probs(u)
                        if u + 2 < NU:
                            maxima(u + 2)
                        if u > HG:
                            post(u // (HG + 1) - 1, u % (HG + 1))
                    for stage in range(HG + 1):
                        post(NBLK - 1, stage)

                    head_norm(b)
                    xa_free.n += 1

                    def project(j):
                        wait(pj_ok, j + 1)
                        wait(hrs_ok, 2 * j + 2)
                        tell(v.scalar_tensor_tensor(ff[:, j, :], po[:, j % 2, 0:D], hrs[:, j % 2:j % 2 + 1],
                                                    ffb[:, :], ALU.mult, ALU.add), ff_ok)

                    for j in range(NBLK):
                        wait(gelu_ok, j + 1)
                        link(v.bn_stats(hst[:, j % 2, 0, :], hid[:, j % 2, 0:512]))
                        link(v.bn_stats(hst[:, j % 2, 1, :], hid[:, j % 2, 512:1024]))
                        dve.sem_inc(alone_v, 1)
                        tell(v.bn_aggr(hmv[:, j % 2, :], hst[:, j % 2, :, :].rearrange("p a b -> p (a b)")), hvar_ok)
                        if j >= 1:
                            project(j - 1)
                    project(NBLK - 1)

                    wait(silu_ok, 1)
                    wait(xr_in, 16)
                    dve.wait_ge(stored.sem, stored.value(b, 0))
                    dve.wait_ge(scattered.sem, scattered.value(b, 16 * NBLK * TOPK))
                    link(v.tensor_tensor(s0[:, :, :], s0[:, :, :], ff[:, :, :], ALU.mult))
                    tell(v.tensor_tensor(x1[:, :, :], s0[:, :, :], xr[:, :, :], ALU.add), x1_ok)
                    xr_free.n += 1
                    dve.sem_inc(xr_free.sem, 1)
                    tell(stats(x1, link), var2_ok)
                    wait(rstd2_ok, 2)
                    tell(normalize(xn2, x1), xn2_ok)
                    head_pool(b)

                    wait(esc_ok, 1)
                    link(v.tensor_scalar(esc[:, :, :], esc[:, :, :], 1.0, None, ALU.add))
                    link(v.reciprocal(sc[:, :, :], esc[:, :, :]))
                    link(v.tensor_tensor(sbias[:, :, :], sc[:, :, :],
                                         ebias[:, :].unsqueeze(1).to_broadcast([P, NBLK, E]), ALU.add))
                    dve.sem_inc(alone_v, 1)
                    for j in range(NBLK):
                        ins = v.max(top[:, j, :], sbias[:, j, :])
                    link(ins)
                    dve.sem_inc(alone_v, 1)
                    for j in range(NBLK):
                        ins = v.max_index(topi[:, j, :], top[:, j, :], sbias[:, j, :])
                    link(ins)
                    link(v.tensor_copy(topf[:, :, :], topi[:, :, 0:TOPK]))
                    for j in range(NBLK):
                        link(v.tensor_tensor(hot[:, j, :, :], iota_e[:, :].unsqueeze(1).to_broadcast([P, TOPK, E]),
                                             topf[:, j, :].unsqueeze(2).to_broadcast([P, TOPK, E]), ALU.is_equal))
                    link(v.tensor_reduce(sel[:, :, :], hot[:, :, :, :].rearrange("p j k e -> p j e k"),
                                         axis=AX.X, op=ALU.add))
                    tell(v.tensor_copy(sel_h[:, :, :], sel[:, :, :]), sel_ok)
                    head_values(b)
                    for j in range(NBLK):
                        link(v.tensor_tensor(tmp[:, j, :, :], hot[:, j, :, :],
                                             sc[:, j, :].unsqueeze(1).to_broadcast([P, TOPK, E]), ALU.mult))
                    link(v.tensor_reduce(gw[:, :, :], tmp[:, :, :, :], axis=AX.X, op=ALU.add))
                    link(v.tensor_reduce(gsum[:, :], gw[:, :, :], axis=AX.X, op=ALU.add))
                    link(v.tensor_scalar(gsum[:, :], gsum[:, :], 1e-12, None, ALU.max))
                    link(v.reciprocal(gsum[:, :], gsum[:, :]))
                    link(v.tensor_tensor(gw[:, :, :], gw[:, :, :],
                                         gsum[:, :].unsqueeze(2).to_broadcast([P, NBLK, TOPK]), ALU.mult))
                    wait(count_ok, 1)
                    cnt = po[:, 1, 0:(NBLK + 1) * E].rearrange("p (j e) -> p j e", e=E)
                    link(v.tensor_tensor(pos[:, :, :], cnt[:, 0:NBLK, :],
                                         taken[:, :].unsqueeze(1).to_broadcast([P, NBLK, E]), ALU.add))
                    link(v.tensor_tensor(taken[:, :], cnt[:, NBLK, :], taken[:, :], ALU.add))
                    link(v.tensor_scalar(over[:, :, :], pos[:, :, :], float(CAP), FAR, ALU.is_ge, ALU.mult))
                    link(v.tensor_tensor(pos[:, :, :], pos[:, :, :],
                                         iota_s[:, :].unsqueeze(1).to_broadcast([P, NBLK, E]), ALU.add))
                    link(v.tensor_tensor(pos[:, :, :], pos[:, :, :], over[:, :, :], ALU.add))
                    for j in range(NBLK):
                        link(v.tensor_tensor(tmp[:, j, :, :], hot[:, j, :, :],
                                             pos[:, j, :].unsqueeze(1).to_broadcast([P, TOPK, E]), ALU.mult))
                    link(v.tensor_reduce(slotf[:, :, :], tmp[:, :, :, :], axis=AX.X, op=ALU.add))
                    link(v.tensor_copy(slot[:, :, :], slotf[:, :, :]))
                    link(v.tensor_scalar(keep[:, :, :], slotf[:, :, :], float(E * CAP), None, ALU.is_lt))
                    tell(v.tensor_tensor(gout[:, :, :], gw[:, :, :], keep[:, :, :], ALU.mult), slot_ok)
                for s in (var_ok, xn_ok, pooled_ok, proj_v, max_ok, cp_ok, lat_done, gate_in, mix_ok, post_cp,
                          hvar_ok, ff_ok, x1_ok, var2_ok, xn2_ok, sel_ok, slot_ok, dchain, headchain):
                    s.whole()

            @block.tensor
            def _(pe):
                t = nc.tensor

                def flip(src):
                    for j in range(NBLK):
                        for k in range(KD):
                            ins = t.transpose(psT[:, k * S + j * P:k * S + (j + 1) * P],
                                              src[:, j, k * P:(k + 1) * P], ident[:, :])
                    return ins

                def through(out, w, x, n=KD, last=True):
                    for k in range(n):
                        ins = t.matmul(out, w(k), x(k), start=(k == 0), stop=(last and k == n - 1))
                    return ins

                def head_qk(b):
                    pe.wait_ge(xn_ok.sem, in_head(b, xn_ok, 1))
                    raise_head(b, xnT_tr, flip(xn))
                    pe.wait_ge(xnT_ok.sem, in_head(b, xnT_ok, 1))
                    for n, (w, g_) in enumerate(((wq, 0), (wk, 0), (wk, 1), (wq, 1))):
                        raise_head(b, proj, through(psS[:, n % 4, :], lambda k: w[:, k, g_ * P:(g_ + 1) * P],
                                                    lambda k: xnT[:, k, :]))

                def head_v(b):
                    for j in range(NBLK):
                        pe.wait_ge(proj_a.sem, in_head(b, proj_a, 1 + j))
                        through(psS[:, j, 0:D], lambda k: xnT[:, k, j * P:(j + 1) * P], lambda k: wv[:, k, :], last=False)
                        raise_head(b, proj, t.matmul(psS[:, j, 0:D], ones_row[:, :], bv[:, :], start=False, stop=True))

                def head_latent(b):
                    pe.wait_ge(proj_v.sem, in_head(b, proj_v, 1))
                    raise_head(b, proj, through(psS[:, 0, :], lambda k: wrq[:, k, :], lambda k: xnT[:, k, :]))
                    pe.wait_ge(proj_v.sem, in_head(b, proj_v, 2))
                    pe.wait_ge(pooled_ok.sem, in_head(b, pooled_ok, 1))
                    through(psS[:, 1, 0:LAT], lambda k: wrk[:, k, :], lambda k: pooled[:, k, :])
                    through(psS[0:LAT, 1, LAT:2 * LAT], lambda k: pooled[:, k, :], lambda k: wrv[:, k, :],
                            last=False)
                    raise_head(b, proj, t.matmul(psS[0:LAT, 1, LAT:2 * LAT], ones_row[:, 0:LAT], brv[:, :],
                                                 start=False, stop=True))

                head_qk(None)
                head_v(None)
                head_latent(None)
                with pe.Fori(0, B) as b:
                    def wait(s, n):
                        pe.wait_ge(s.sem, s.value(b, n))

                    def scores(u):
                        j, g_ = u // (HG + 1), u % (HG + 1)
                        k0, nk = span(u)
                        if u >= 2:
                            wait(exp_ok, u - 1)
                        if g_ == HG:
                            t.matmul(psS[:, 2 * (u % 2), 0:LH * LAT], ident_h[:, :],
                                     lmask[:, j, :, :].rearrange("p h n -> p (h n)"), start=True, stop=False)
                        else:
                            for c in range(2):
                                t.matmul(psS[:, 2 * (u % 2) + c, :], ident_h[:, :],
                                         mask[:, :, :, :].rearrange("p r k n -> p (r k n)"), start=True, stop=False)
                        for h in range(G):
                            tile, at = divmod(g_ * G + h, HT)
                            qs = qX[:, tile, at, j * P:(j + 1) * P] if g_ < HG else rqX[:, h, j * P:(j + 1) * P]
                            ks = kT[:, tile, k0:k0 + nk] if g_ < HG else rkT[:, 0:LAT]
                            ins = t.matmul(scored(u)[:, h, :], qs, ks, start=False,
                                           stop=(h == G - 1 if g_ == HG else h % 2 == 1))
                        s_ok.raised_by(ins)

                    def turn(u):
                        k0, nk = span(u)
                        wait(exp_ok, u + 1)
                        if u >= 1:
                            wait(cp_ok, u)
                        if nk == LAT:
                            pe.sem_inc(alone_t, 1)
                        for h in range(G):
                            if nk == LAT:
                                ins = t.transpose(psT[0:LAT, 2 * h * P:(2 * h + 1) * P], pr[:, u % 2, h, 0:LAT], ident[:, :])
                            else:
                                for k in range(nk // P):
                                    k += 2 - nk // P
                                    c = 2 * h + k
                                    ins = t.transpose(psT[:, c * P:(c + 1) * P], pr[:, u % 2, h, k * P:(k + 1) * P],
                                                      ident[:, :])
                        tr_ok.raised_by(ins)

                    def values(u):
                        j, g_ = u // (HG + 1), u % (HG + 1)
                        k0, nk = span(u)
                        wait(cp_ok, u + 1)
                        for h in range(G):
                            hh = g_ * G + h
                            o = po[:, j % 2, hh * VW:(hh + 1) * VW]
                            if g_ == HG:
                                ins = t.matmul(o, prT[0:LAT, u % 2, h, 0, :], rvv[:, h, :], start=True, stop=True)
                            else:
                                ks = [0, 1] if nk > P else [1]
                                for k in ks:
                                    ins = t.matmul(o, prT[:, u % 2, h, k, :], vv[:, j - 1 + k, hh, :],
                                                   start=(k == ks[0]), stop=(k == 1))
                        pv_ok.raised_by(ins)

                    def post(q, stage):
                        if stage == 1:
                            wait(lat_done, q + 1)
                            pe.sem_inc(alone_t, 1)
                            post_t.raised_by(t.transpose(psT[0:LAT, 0:P], lat[:, :, :].rearrange("p h d -> p (h d)"),
                                                         ident[:, :]))
                        if stage == 2:
                            wait(post_cp, 4 * q + 1)
                            t.matmul(psT[:, 0:D], latT[:, :], wro[:, :], start=True, stop=False)
                            post_t.raised_by(t.matmul(psT[:, 0:D], ones_row[:, :], bro[:, :], start=False, stop=True))
                        if stage == 3:
                            wait(mix_ok, q + 1)
                            wait(post_cp, 4 * q + 2)
                            for k in range(KD):
                                ins = t.transpose(psT[:, k * P:(k + 1) * P],
                                                  mix[:, 8 * k:8 * k + 8, :].rearrange("p h d -> p (h d)"), ident[:, :])
                            post_t.raised_by(ins)
                        if stage == 4:
                            wait(post_cp, 4 * q + 3)
                            through(psT[:, 0:D], lambda k: mixT[:, k, :], lambda k: wo[:, k, :], last=False)
                            post_t.raised_by(t.matmul(psT[:, 0:D], ones_row[:, :], bo[:, :], start=False, stop=True))

                    wait(proj_v, 0)
                    wait(proj_a, 0)
                    scores(0)
                    scores(1)
                    for u in range(NU):
                        if u > HG and u % (HG + 1) > 1:
                            wait(post_cp, 4 * (u // (HG + 1) - 1) + u % (HG + 1) - 1)
                        elif u > 2 * HG + 1 and u % (HG + 1) == 0:
                            wait(post_cp, 4 * (u // (HG + 1) - 1))
                        turn(u)
                        if u + 2 < NU:
                            scores(u + 2)
                        if u > HG:
                            if u % (HG + 1):
                                wait(cp_ok, u + 1)
                            post(u // (HG + 1) - 1, u % (HG + 1))
                        values(u)
                    for stage in range(HG + 1):
                        post(NBLK - 1, stage)

                    def expand(j):
                        wait(gelu_ok, j - 1) if j >= 2 else wait(exp_ok, NU)
                        for c in range(2):
                            ins = through(psS[:, 2 * (j % 2) + c, :], lambda k: xnT[:, k, j * P:(j + 1) * P],
                                          lambda k: wfc[:, k, c * 512:(c + 1) * 512])
                        h_ok.raised_by(ins)

                    expand(0)
                    expand(1)
                    wait(post_cp, 4 * NBLK)
                    for j in range(NBLK):
                        wait(gelu_ok, j + 1)
                        if j >= 1:
                            wait(ht_ok, j)
                        for k in range(HID // P):
                            ins = t.transpose(psT[:, k * P:(k + 1) * P], hid[:, j % 2, k * P:(k + 1) * P], ident[:, :])
                        ht_tr.raised_by(ins)
                        if j + 2 < NBLK:
                            expand(j + 2)
                        wait(ht_ok, j + 1)
                        if j >= 2:
                            wait(ff_ok, j - 1)
                        pj_ok.raised_by(through(po[:, j % 2, 0:D], lambda k: hidT[:, j % 2, k, :],
                                                lambda k: wpj[:, k, :], HID // P))

                    wait(ht_ok, NBLK)
                    wait(gelu_ok, NBLK)
                    head_qk(b)
                    wait(xn2_ok, 1)
                    xn2T_tr.raised_by(flip(xn2))
                    wait(ff_ok, NBLK)
                    wait(xn2T_ok, 1)
                    for j in range(NBLK):
                        ins = through(po[:, 0, j * E:(j + 1) * E], lambda k: xn2T[:, k, j * P:(j + 1) * P],
                                      lambda k: gate_w[:, k, :])
                    logit_ok.raised_by(ins)
                    head_v(b)
                    wait(sel_ok, 1)
                    for j in range(NBLK + 1):
                        for k in range(min(j + 1, NBLK)):
                            m = before if k == j else ones_h
                            ins = t.matmul(po[:, 1, j * E:(j + 1) * E], m[:, :], sel_h[:, k, :],
                                           start=(k == 0), stop=(k == min(j, NBLK - 1)))
                    count_ok.raised_by(ins)
                    head_latent(b)
                for s in (xnT_tr, proj, s_ok, tr_ok, pv_ok, post_t, h_ok, ht_tr, pj_ok, xn2T_tr, logit_ok, count_ok):
                    s.whole()


DI = 512
M = DI // P
NS = 16
RK = 16
TAPS = 4
NP_ = NS // 2
W = NP_ * M
NA, NH, NQ = 4, 2, 2


def layer1_mixer(nc, A, XNT, S1):
    ctx = ExitStack()
    with ctx:
        sb = lambda name, shape, dt=F32: ctx.enter_context(nc.sbuf_tensor("m_" + name, shape, dt))
        sem = lambda name: ctx.enter_context(nc.semaphore("m_" + name))
        win = sb("win", [P, 2, KD, 2 * DI])
        wbc = sb("wbc", [P, 2, M, 6 * NS])
        wdr = sb("wdr", [P, 2, M, RK])
        wdt = sb("wdt", [RK, 2, DI])
        wout = sb("wout", [P, 2, M, D])
        cw = sb("cw", [P, 2, M, TAPS])
        cb = sb("cb", [P, 2, M])
        db = sb("db", [P, 2, M])
        dd = sb("dd", [P, 2, M])
        al = sb("al", [P, 2, M, NS])
        gam = sb("gam", [P, D])
        bet = sb("bet", [P, D])
        ident = sb("ident", [P, P])
        pick = sb("pick", [6 * NS, 2 * NS, P], BF16)
        half = sb("half", [P, NBLK])

        xT = sb("xT", [P, KD, S])
        xi = sb("xi", [P, M, TAPS - 1 + S])
        z = sb("z", [P, 2, M, S])
        xc = sb("xc", [P, 2, M, S])
        dt = sb("dt", [P, 2, M, S])
        u = sb("u", [P, 2, M, S])
        rest = sb("rest", [P, M, S])
        bc = sb("bc", [6 * NS, 2, S], BF16)
        bcr = sb("bcr", [6 * NS, S])
        bcm = sb("bcm", [6 * NS, S], BF16)
        dtr = sb("dtr", [RK, S])
        Bs = sb("Bs", [P, 2, 2, S])
        Cs = sb("Cs", [P, 2, 2, S])
        dA = sb("dA", [P, NA, 2, S])
        dBu = sb("dBu", [P, NH, 2, S])
        hh = sb("hh", [P, 2, S])
        hC = sb("hC", [P, NQ, 2, S])
        yt = sb("yt", [P, S])
        yo0 = sb("yo0", [P, NBLK, D])
        yo = sb("yo", [P, NBLK, D])
        bnst = sb("bnst", [P, NBLK, 6])
        mv = sb("mv", [P, NBLK, 2])
        rstd = sb("rstd", [P, NBLK])
        psY = ctx.enter_context(nc.psum_tensor("psY", [P, M, S], F32))
        psB = ctx.enter_context(nc.psum_tensor("psB", [P, 2, S], F32))
        psP = ctx.enter_context(nc.psum_tensor("psP", [P, 2, S], F32))

        w_in, made, prep = sem("w_in"), sem("made"), sem("prep")
        loads = []
        for d, n in enumerate(("f", "b")):
            loads += [(win[:, d], A[n + "_win"].rearrange("(t p) n -> p t n", p=P)),
                      (wbc[:, d], A[n + "_wbc"].rearrange("(t p) n -> p t n", p=P)),
                      (wdr[:, d], A[n + "_wdr"].rearrange("(t p) n -> p t n", p=P)),
                      (wdt[:, d], A[n + "_wdt"]),
                      (wout[:, d], A[n + "_wout"].rearrange("(t p) n -> p t n", p=P)),
                      (cw[:, d], A[n + "_cw"].rearrange("(t p) n -> p t n", p=P)),
                      (cb[:, d], A[n + "_cb"]), (db[:, d], A[n + "_db"]), (dd[:, d], A[n + "_dd"]),
                      (al[:, d], A[n + "_al"].rearrange("(t p) n -> p t n", p=P))]
        loads += [(gam[:, :], A["gam"].partition_broadcast(P)), (bet[:, :], A["bet"].partition_broadcast(P))]
        with nc.Block() as block:
            @block.sync
            def _(sp):
                for t, s in loads:
                    sp.dma_start(t, s).then_inc(w_in, 16)
                sp.wait_ge(w_in, 16 * len(loads))

            @block.gpsimd
            def _(pool):
                g = nc.gpsimd
                m = [0]

                def link(ins):
                    ins.then_inc(made, 1)
                    m[0] += 1
                    pool.wait_ge(made, m[0])

                link(g.memset(ident[:, :], 0.0))
                link(g.affine_select(out=ident[:, :], in_=ident[:, :], compare_op=ALU.not_equal, fill=1.0,
                                     base=0, pattern=[[-1, P]], channel_multiplier=1))
                link(g.memset(pick[:, :, :], 0.0))
                for k in range(3):
                    link(g.affine_select(out=pick[:, :, :], in_=pick[:, :, :], compare_op=ALU.not_equal,
                                         fill=1.0, base=-32 * k, pattern=[[-1, 2 * NS], [0, P]],
                                         channel_multiplier=1))
                link(g.memset(half[:, :], -0.5))
                link(g.memset(xi[:, :, 0:TAPS - 1], 0.0))
                link(g.memset(z[:, 1, :, :], 0.0))
                link(g.memset(yo0[:, :, :], 0.0))

            @block.scalar
            def _(act):
                act.wait_ge(w_in, 16 * len(loads))
                nc.scalar.activation(al[:, :, :, :], al[:, :, :, :], ACT.Exp).then_inc(prep, 1)

            @block.vector
            def _(dve):
                dve.wait_ge(prep, 1)
                nc.vector.tensor_scalar(al[:, :, :, :], al[:, :, :, :], -1.0, None, ALU.mult).then_inc(prep, 1)

        sig = lambda name, per, first=0: Signal(sem(name), per, first)
        xT_in = sig("xT_in", 16, 16)
        p_ok = sig("p_ok", 36, 14)
        pa = sig("pa", 26, 13)
        pv = sig("pv", 10, 1)
        conv_ok = sig("conv_ok", 2 * M, M)
        xc_ok = sig("xc_ok", 2, 1)
        z_ok = sig("z_ok", 2, 1)
        bc_ok = sig("bc_ok", 2, 1)
        na_ok = sig("na_ok", 2, 1)
        e_ok = sig("e_ok", 2, 1)
        l_ok = sig("l_ok", 2, 1)
        rest_ok = sig("rest_ok", 2, 1)
        diff_ok = sig("diff_ok", 2 * M, M)
        t_ok = sig("t_ok", 2 * M, M)
        dt_ok = sig("dt_ok", 2 * M, M)
        u_ok = sig("u_ok", 2 * M, M)
        bcast = sig("bcast", 4 * NP_, 2)
        bcopy = sig("bcopy", 4 * NP_, 1)
        dA_ok = sig("dA_ok", 2 * W)
        dBu_ok = sig("dBu_ok", 2 * W, 1)
        scan_ok = sig("scan_ok", 2 * W, NA)
        hC_ok = sig("hC_ok", 2 * W, M)
        y_ok = sig("y_ok", 2 * W, M)
        fin_ok = sig("fin_ok", 2 * M)
        mvar = sig("mvar", 1)
        mrstd = sig("mrstd", 2)
        s1_ok = sig("s1_ok", 1)
        s1_out = sig("s1_out", 16, 16)
        mchain = sig("mchain", MCHAIN, MFIRST)
        alone_v, alone_p = sem("alone_v"), sem("alone_p")

        JOBS = [("xi", m) for m in range(M)] + [("out", j) for j in range(NBLK)] + [("z", m) for m in range(M)] + \
               [("bc", 0), ("dtr", 0)] + [("dt", m) for m in range(M)]
        PEEL = [x for x in JOBS if x[0] != "out"]
        on_dve = lambda kind: kind in ("out", "bc")
        UNIT_OF = {}
        for m in range(M):
            UNIT_OF[("xi", m)] = m
            UNIT_OF[("out", m)] = 4 + m
            UNIT_OF[("z", m)] = 8 + m
            UNIT_OF[("dt", m)] = 16 + m
        UNIT_OF[("bc", 0)] = 12
        UNIT_OF[("dtr", 0)] = 13
        CONV_AT = {}
        for n in range(M * (TAPS - 1)):
            CONV_AT.setdefault(3 + n * 2 * M // (M * (TAPS - 1)), []).append(divmod(n, TAPS - 1))
        AHEAD = 5

        class Place:

            def __init__(self, b, d):
                self.b, self.d = b, d

            def ph(self, s, per_phase, n):
                if self.b is None:
                    return n
                return s.value(self.b, self.d * per_phase + n)

        def job_count(pl, kind, idx):
            jobs = PEEL if pl.b is None else JOBS
            return pl.ph(p_ok, 18, jobs.index((kind, idx)) + 1)

        def evac_before(pl, pos):
            jobs = PEEL if pl.b is None else JOBS
            if pos >= 2:
                seen = jobs[:pos - 1]
                k = jobs[pos - 2][0]
                n = sum(on_dve(x[0]) == on_dve(k) for x in seen)
                return (pv, pl.ph(pv, 5, n)) if on_dve(k) else (pa, pl.ph(pa, 13, n))
            if pl.b is None:
                return None
            return (pa, pl.ph(pa, 13, pos - 1))

        with nc.Block() as block:
            @block.sync
            def _(sp):
                sp.sem_inc(s1_out.sem, 16)
                sp.dma_start(xT[:, :, :], XNT[0].rearrange("(t p) s -> p t s", p=P)).then_inc(xT_in.sem, 16)

                def store(b, slot):
                    sp.wait_ge(s1_ok.sem, s1_ok.value(b, 1))
                    sp.dma_start(slot, yo[:, :, :]).then_inc(s1_out.sem, 16)

                with sp.Fori(0, B - 1) as b:
                    store(b, S1[bass.ds(b, 1), :, :].rearrange("a (j p) d -> p (a j) d", p=P))
                    sp.wait_ge(p_ok.sem, p_ok.value(b, 12))
                    sp.dma_start(xT[:, :, :], XNT[bass.ds(b + 1, 1), :, :].rearrange("a (t p) s -> p (a t) s", p=P)
                                 ).then_inc(xT_in.sem, 16)
                store(B - 1, S1[B - 1].rearrange("(j p) d -> p j d", p=P))
                sp.wait_ge(p_ok.sem, p_ok.value(B - 1, 12))
                sp.dma_start(xT[:, :, :], XNT[B - 1].rearrange("(t p) s -> p t s", p=P)).then_inc(xT_in.sem, 16)
                store(B, S1[B].rearrange("(j p) d -> p j d", p=P))
                sp.wait_ge(s1_out.sem, 16 * (B + 2))

            @block.tensor
            def _(pe):
                t = nc.tensor

                def job(pl, kind, idx):
                    jobs = PEEL if pl.b is None else JOBS
                    dn = pl.d if pl.b is None else 1 - pl.d
                    pos = jobs.index((kind, idx))
                    before = evac_before(pl, pos)
                    if before:
                        pe.wait_ge(before[0].sem, before[1])
                    o = psP[:, pos % 2, :]
                    if kind in ("xi", "z"):
                        if kind == "xi" and idx == 0 and dn == 0:
                            pe.wait_ge(xT_in.sem, 16 if pl.b is None else xT_in.value(pl.b, 16))
                        c = (0 if kind == "xi" else DI) + idx * P
                        for k in range(KD):
                            x = xT[:, k, :] if dn == 0 or kind == "z" else xT[:, k, ::-1]
                            ins = t.matmul(o, win[:, dn, k, c:c + P], x, start=(k == 0), stop=(k == KD - 1))
                    elif kind == "bc":
                        pe.wait_ge(xc_ok.sem, pl.ph(xc_ok, 1, 1))
                        for k in range(M):
                            ins = t.matmul(o[0:6 * NS, :], wbc[:, dn, k, :], xc[:, dn, k, :],
                                           start=(k == 0), stop=(k == M - 1))
                    elif kind == "dtr":
                        for k in range(M):
                            ins = t.matmul(o[0:RK, :], wdr[:, dn, k, :], xc[:, dn, k, :],
                                           start=(k == 0), stop=(k == M - 1))
                    elif kind == "dt":
                        pe.wait_ge(pa.sem, pl.ph(pa, 13, 9))
                        ins = t.matmul(o, wdt[:, dn, idx * P:(idx + 1) * P], dtr[:, :], start=True, stop=True)
                    else:
                        for m in range(M):
                            y = z[:, dn, m, idx * P:(idx + 1) * P]
                            ins = t.matmul(o[:, 0:D], y, wout[:, dn, m, :], start=(m == 0), stop=(m == M - 1))
                    p_ok.raised_by(ins) if pl.b is not None else ins.then_inc(p_ok.sem, 1)

                def spread(pl, d, j, c, n):
                    pe.wait_ge(bcopy.sem, pl.ph(bcopy, 2 * NP_, n))
                    for k in range(2):
                        ins = t.matmul(psB[:, k, :], pick[:, c * NS + 2 * j + k, :], bc[:, d, :], start=True, stop=True)
                    bcast.raised_by(ins)

                pl0 = Place(None, 0)
                for kind, idx in PEEL:
                    job(pl0, kind, idx)
                pe.wait_ge(bc_ok.sem, 1)
                for c in range(2):
                    if c:
                        pe.wait_ge(bcopy.sem, 1)
                    for k in range(2):
                        ins = t.matmul(psB[:, k, :], pick[:, c * NS + k, :], bc[:, 0, :], start=True, stop=True)
                    ins.then_inc(bcast.sem, 1)
                pe.sem_inc(y_ok.sem, M)
                with pe.Fori(0, B) as b:
                    for d in range(2):
                        pl = Place(b, d)
                        for w in range(W):
                            j, m = w // M, w % M
                            if j == 0:
                                pe.wait_ge(fin_ok.sem, pl.ph(fin_ok, M, m + 1))
                            pe.wait_ge(hC_ok.sem, pl.ph(hC_ok, W, w + 1))
                            for k in range(2):
                                ins = t.matmul(psY[:, m, :], ident[:, :], hC[:, w % NQ, k, :],
                                               start=(j == 0 and k == 0), stop=(j == NP_ - 1 and k == 1))
                            y_ok.raised_by(ins)
                            for kind, idx in JOBS:
                                if UNIT_OF[(kind, idx)] == w:
                                    job(pl, kind, idx)
                            if m in (0, 1):
                                nj, nd = (j + 1, d) if j + 1 < NP_ else (0, 1 - d)
                                if nj == 0 and m == 0:
                                    pe.wait_ge(bc_ok.sem, pl.ph(bc_ok, 1, 1))
                                spread(pl, nd, nj, m, 2 * j + m + 1)
                plE = Place(B, 0)
                for j in range(NBLK):
                    if j < 2:
                        pe.wait_ge(fin_ok.sem, fin_ok.value(B, M))
                        pe.wait_ge(pa.sem, pa.value(B, 0))
                    else:
                        pe.wait_ge(pv.sem, pv.value(B, j - 1))
                    for m in range(M):
                        y = z[:, 1, m, j * P:(j + 1) * P]
                        ins = t.matmul(psP[:, j % 2, 0:D], y, wout[:, 1, m, :], start=(m == 0), stop=(m == M - 1))
                    ins.then_inc(p_ok.sem, 1)
                for s in (p_ok, bcast, y_ok):
                    s.whole()

            @block.scalar
            def _(act):
                a = nc.scalar

                def raise_(pl, s, ins):
                    s.raised_by(ins) if pl.b is not None else ins.then_inc(s.sem, 1)

                def evac(pl, kind, idx):
                    dn = pl.d if pl.b is None else 1 - pl.d
                    jobs = PEEL if pl.b is None else JOBS
                    pos = jobs.index((kind, idx))
                    act.wait_ge(p_ok.sem, job_count(pl, kind, idx))
                    src = psP[:, pos % 2, :]
                    if kind == "xi":
                        if pl.b is not None:
                            act.wait_ge(t_ok.sem, pl.ph(t_ok, M, 0))
                            act.wait_ge(fin_ok.sem, pl.ph(fin_ok, M, idx + 1))
                        a.activation(xc[:, dn, idx, :], src, ACT.Identity, bias=cb[:, dn, idx:idx + 1],
                                     scale=cw[:, dn, idx, TAPS - 1:TAPS])
                        ins = a.activation(xi[:, idx, TAPS - 1:], src, ACT.Copy)
                    elif kind == "z":
                        ins = a.activation(z[:, dn, idx, :], src, ACT.Copy)
                    elif kind == "dtr":
                        ins = a.activation(dtr[:, :], psP[0:RK, pos % 2, :], ACT.Copy)
                    else:
                        ins = a.activation(dt[:, dn, idx, :], src, ACT.Identity, bias=db[:, dn, idx:idx + 1], scale=1.0)
                    raise_(pl, pa, ins)

                def silu_x(pl):
                    dn = pl.d if pl.b is None else 1 - pl.d
                    act.wait_ge(conv_ok.sem, pl.ph(conv_ok, M, M))
                    raise_(pl, xc_ok, a.activation(xc[:, dn, :, :], xc[:, dn, :, :], ACT.Silu))

                def silu_z(pl):
                    dn = pl.d if pl.b is None else 1 - pl.d
                    act.wait_ge(pa.sem, pl.ph(pa, 13, 8))
                    raise_(pl, z_ok, a.activation(z[:, dn, :, :], z[:, dn, :, :], ACT.Silu))

                def exp_abs(pl):
                    dn = pl.d if pl.b is None else 1 - pl.d
                    act.wait_ge(pa.sem, pl.ph(pa, 13, 13))
                    raise_(pl, na_ok, a.activation(u[:, dn, :, :], dt[:, dn, :, :], ACT.Abs))
                    act.wait_ge(na_ok.sem, pl.ph(na_ok, 1, 1))
                    raise_(pl, e_ok, a.activation(u[:, dn, :, :], u[:, dn, :, :], ACT.Exp, scale=-1.0))

                def log1(pl):
                    dn = pl.d if pl.b is None else 1 - pl.d
                    act.wait_ge(rest_ok.sem, pl.ph(rest_ok, 1, 1))
                    raise_(pl, l_ok, a.activation(xi[:, :, TAPS - 1:], rest[:, :, :], ACT.Ln, bias=1.0))

                def copy_bc(pl, nj, c, n):
                    act.wait_ge(bcast.sem, pl.ph(bcast, 2 * NP_, n))
                    dst = (Bs, Cs)[c][:, nj % 2, :, :]
                    raise_(pl, bcopy, a.activation(dst, psB[:, :, :], ACT.Copy))

                pl0 = Place(None, 0)
                for kind, idx in PEEL:
                    if kind == "bc":
                        silu_x(pl0)
                        silu_z(pl0)
                    if not on_dve(kind):
                        evac(pl0, kind, idx)
                exp_abs(pl0)
                log1(pl0)
                copy_bc(pl0, 0, 0, 1)
                with act.Fori(0, B) as b:
                    for d in range(2):
                        pl = Place(b, d)
                        for w in range(W):
                            j, m = w // M, w % M
                            if w == 0:
                                act.wait_ge(dt_ok.sem, pl.ph(dt_ok, M, 0))
                            act.wait_ge(scan_ok.sem, pl.ph(scan_ok, W, w + 1 - NA))
                            for k in range(2):
                                ins = a.activation(dA[:, (d * W + w) % NA, k, :], dt[:, d, m, :], ACT.Exp,
                                                   scale=al[:, d, m, 2 * j + k:2 * j + k + 1])
                            dA_ok.raised_by(ins)
                            for kind, idx in JOBS:
                                if UNIT_OF[(kind, idx)] + AHEAD == w and not on_dve(kind):
                                    evac(pl, kind, idx)
                            if w == 14:
                                silu_x(pl)
                            if w == 24:
                                exp_abs(pl)
                            if w == 27:
                                log1(pl)
                                silu_z(pl)
                            if m == 0:
                                act.wait_ge(hC_ok.sem, pl.ph(hC_ok, W, (j - 1) * M + 1))
                                copy_bc(pl, j, 1, 2 * j)
                            if m == M - 1:
                                act.wait_ge(dBu_ok.sem, pl.ph(dBu_ok, W, j * M))
                                copy_bc(pl, (j + 1) % NP_, 0, 2 * j + 1)
                for s in (na_ok, pa, xc_ok, z_ok, e_ok, l_ok, bcopy, dA_ok):
                    s.whole()

            @block.gpsimd
            def _(pool):
                g = nc.gpsimd

                def raise_(pl, s, ins):
                    s.raised_by(ins) if pl.b is not None else ins.then_inc(s.sem, 1)

                def soft(pl, m):
                    dn = pl.d if pl.b is None else 1 - pl.d
                    pool.wait_ge(l_ok.sem, pl.ph(l_ok, 1, 1))
                    pool.wait_ge(diff_ok.sem, pl.ph(diff_ok, M, m + 1))
                    raise_(pl, t_ok, g.tensor_tensor(u[:, dn, m, :], u[:, dn, m, :], xi[:, m, TAPS - 1:], ALU.add))

                def inputs(pl, m):
                    dn = pl.d if pl.b is None else 1 - pl.d
                    pool.wait_ge(dt_ok.sem, pl.ph(dt_ok, M, m + 1))
                    raise_(pl, u_ok, g.tensor_tensor(u[:, dn, m, :], dt[:, dn, m, :], xc[:, dn, m, :], ALU.mult))

                pl0 = Place(None, 0)
                for m in range(M):
                    soft(pl0, m)
                for m in range(M):
                    inputs(pl0, m)

                pool.sem_inc(dBu_ok.sem, 1)

                def rsqrt(value):
                    pool.wait_ge(mvar.sem, value)
                    pool.sem_inc(alone_p, 1)
                    mrstd.raised_by(g.tensor_scalar(rstd[:, :], mv[:, :, 1], LN_EPS, None, ALU.add))

                with pool.Fori(0, B) as b:
                    for d in range(2):
                        pl = Place(b, d)
                        for w in range(W):
                            j, m = w // M, w % M
                            pool.wait_ge(bcopy.sem, pl.ph(bcopy, 2 * NP_, 2 * j))
                            pool.wait_ge(u_ok.sem, pl.ph(u_ok, M, 0 if j else m + 1 - M))
                            pool.wait_ge(scan_ok.sem, pl.ph(scan_ok, W, w + 1 - NH))
                            dBu_ok.raised_by(g.tensor_tensor(
                                dBu[:, w % NH, :, :], u[:, d, m, :].unsqueeze(1).to_broadcast([P, 2, S]),
                                Bs[:, j % 2, :, :], ALU.mult))
                            if d == 0 and w == 15:
                                rsqrt(mvar.value(b, 1))
                                pool.wait_ge(mrstd.sem, mrstd.value(b, 1))
                                mrstd.raised_by(g.tensor_tensor(rstd[:, :], rstd[:, :], half[:, :], ALU.pow))
                            if 26 <= w < 26 + M:
                                soft(pl, w - 26)
                            if w in (29, 30, 31):
                                inputs(pl, w - 29)
                            if w == W - 1:
                                inputs(pl, M - 1)
                pool.wait_ge(mvar.sem, mvar.value(B, 1))
                g.tensor_scalar(rstd[:, :], mv[:, :, 1], LN_EPS, None, ALU.add).then_inc(mrstd.sem, 1)
                pool.wait_ge(mrstd.sem, mrstd.value(B, 1))
                g.tensor_tensor(rstd[:, :], rstd[:, :], half[:, :], ALU.pow).then_inc(mrstd.sem, 1)
                for s in (t_ok, u_ok, dBu_ok, mrstd):
                    s.whole()

            @block.vector
            def _(dve):
                v = nc.vector

                def raise_(pl, s, ins, n, per):
                    s.raised_by(ins) if pl.b is not None else ins.then_inc(s.sem, 1)
                    dve.wait_ge(s.sem, pl.ph(s, per, n))

                c = [0]

                def link(pl, ins):
                    ins.then_inc(mchain.sem, 1)
                    c[0] += 1
                    dve.wait_ge(mchain.sem, c[0] if pl.b is None else mchain.value(pl.b, c[0]))

                def conv(pl, m, taps=range(TAPS - 1)):
                    dn = pl.d if pl.b is None else 1 - pl.d
                    y = xc[:, dn, m, :]
                    for k in taps:
                        if k == 0:
                            dve.wait_ge(pa.sem, pl.ph(pa, 13, m + 1))
                        ins = v.scalar_tensor_tensor(y, xi[:, m, k:k + S], cw[:, dn, m, k:k + 1], y, ALU.mult, ALU.add)
                        if k < TAPS - 2:
                            link(pl, ins)
                        else:
                            raise_(pl, conv_ok, ins, m + 1, M)

                def split(pl, part):
                    dn = pl.d if pl.b is None else 1 - pl.d
                    jobs = PEEL if pl.b is None else JOBS
                    o = psP[0:6 * NS, jobs.index(("bc", 0)) % 2, :]
                    if part == 0:
                        dve.wait_ge(p_ok.sem, job_count(pl, "bc", 0))
                        link(pl, v.tensor_copy(bc[:, dn, :], o))
                        raise_(pl, pv, v.tensor_tensor(bcr[:, :], o, bc[:, dn, :], ALU.subtract),
                               1 if pl.b is None else 5, 5)
                    if part == 1:
                        link(pl, v.tensor_copy(bcm[:, :], bcr[:, :]))
                        link(pl, v.tensor_copy(bc[32:64, dn, :], bcr[32:64, :]))
                    if part == 2:
                        link(pl, v.tensor_tensor(bcr[:, :], bcr[:, :], bcm[:, :], ALU.subtract))
                        raise_(pl, bc_ok, v.tensor_copy(bc[64:96, dn, :], bcr[64:96, :]), 1, 1)

                def remainder(pl):
                    dn = pl.d if pl.b is None else 1 - pl.d
                    dve.wait_ge(e_ok.sem, pl.ph(e_ok, 1, 1))
                    raise_(pl, rest_ok, v.tensor_scalar(rest[:, :, :], u[:, dn, :, :], 1.0, -1.0,
                                                        ALU.add, ALU.add), 1, 1)

                def difference(pl, m):
                    dn = pl.d if pl.b is None else 1 - pl.d
                    raise_(pl, diff_ok, v.tensor_tensor(u[:, dn, m, :], u[:, dn, m, :], rest[:, m, :], ALU.subtract),
                           m + 1, M)

                def steps(pl, m):
                    dn = pl.d if pl.b is None else 1 - pl.d
                    dve.wait_ge(t_ok.sem, pl.ph(t_ok, M, m + 1))
                    raise_(pl, dt_ok, v.scalar_tensor_tensor(dt[:, dn, m, :], dt[:, dn, m, :], 0.0, u[:, dn, m, :],
                                                             ALU.max, ALU.add), m + 1, M)

                def out(pl, dn, j, count, value):
                    dve.wait_ge(p_ok.sem, count)
                    o = psP[:, j % 2, 0:D]
                    if dn == 0:
                        ins = v.tensor_copy(yo0[:, j, :], o)
                    else:
                        if j == 0:
                            dve.wait_ge(s1_out.sem, s1_out.value(pl.b, 0))
                        ins = v.tensor_tensor(yo[:, j, :], o, yo0[:, j, :], ALU.add)
                    ins.then_inc(pv.sem, 1)
                    pv.n += 1
                    dve.wait_ge(pv.sem, value)

                def stats(pl, value):
                    for j in range(NBLK):
                        ins = v.bn_stats(bnst[:, j, :], yo[:, j, :])
                    link(pl, ins)
                    dve.sem_inc(alone_v, 1)
                    for j in range(NBLK):
                        ins = v.bn_aggr(mv[:, j, :], bnst[:, j, :])
                    ins.then_inc(mvar.sem, 1)
                    dve.wait_ge(mvar.sem, value)

                def norm(pl, ready):
                    dve.wait_ge(mrstd.sem, ready)
                    for j in range(NBLK):
                        ins = v.tensor_scalar(yo[:, j, :], yo[:, j, :], mv[:, j, 0:1], rstd[:, j:j + 1],
                                              ALU.subtract, ALU.mult)
                    link(pl, ins)
                    link(pl, v.tensor_tensor(yo[:, :, :], yo[:, :, :], gam[:, :].unsqueeze(1).to_broadcast([P, NBLK, D]),
                                             ALU.mult))
                    v.tensor_tensor(yo[:, :, :], yo[:, :, :], bet[:, :].unsqueeze(1).to_broadcast([P, NBLK, D]),
                                    ALU.add).then_inc(s1_ok.sem, 1)

                def finish(pl, m, ready):
                    dn = 1 - pl.d
                    dve.wait_ge(y_ok.sem, ready)
                    if m == 0:
                        dve.wait_ge(z_ok.sem, pl.ph(z_ok, 1, 0))
                    link(pl, v.scalar_tensor_tensor(yt[:, :], xc[:, dn, m, :], dd[:, dn, m:m + 1], psY[:, m, :],
                                                    ALU.mult, ALU.add))
                    return v.tensor_tensor(z[:, dn, m, :], yt[:, :] if dn == 0 else yt[:, ::-1], z[:, dn, m, :], ALU.mult)

                def y_value(pl, m):
                    return pl.ph(y_ok, W, m + 1 - M)

                def y_free(pl, w):
                    return pl.ph(y_ok, W, w + 1 - NQ)

                def outputs(pl, w):
                    j = w // M
                    dve.wait_ge(scan_ok.sem, pl.ph(scan_ok, W, w + 1))
                    dve.wait_ge(bcopy.sem, pl.ph(bcopy, 2 * NP_, 2 * j + 1))
                    dve.wait_ge(y_ok.sem, y_free(pl, w))
                    hC_ok.raised_by(v.tensor_tensor(hC[:, w % NQ, :, :], hh[:, :, :], Cs[:, j % 2, :, :],
                                                    ALU.mult))

                pl0 = Place(None, 0)
                for m in range(M):
                    conv(pl0, m)
                for part in range(3):
                    split(pl0, part)
                remainder(pl0)
                for m in range(M):
                    difference(pl0, m)
                for m in range(M):
                    steps(pl0, m)
                dve.sem_inc(scan_ok.sem, NA)
                link(pl0, v.memset(psY[:, :, :], 0.0))
                dve.sem_inc(hC_ok.sem, M)
                link(pl0, v.memset(xc[:, 1, :, :], 0.0))
                assert c[0] == MFIRST, ("MFIRST", c[0])
                c[0] = 0
                with dve.Fori(0, B) as b:
                    for d in range(2):
                        pl = Place(b, d)
                        for w in range(W):
                            j, m = w // M, w % M
                            if j == 0:
                                ins = finish(pl, m, y_value(pl, m))
                                fin_ok.raised_by(ins)
                                dve.wait_ge(fin_ok.sem, pl.ph(fin_ok, M, m + 1))
                            dve.wait_ge(dA_ok.sem, pl.ph(dA_ok, W, w + 1))
                            dve.wait_ge(dBu_ok.sem, pl.ph(dBu_ok, W, w + 1))
                            dve.wait_ge(hC_ok.sem, pl.ph(hC_ok, W, w))
                            for k in range(2):
                                ins = v.tensor_tensor_scan(hh[:, k, :], dA[:, (d * W + w) % NA, k, :],
                                                           dBu[:, w % NH, k, :], 0.0, ALU.mult, ALU.add)
                            scan_ok.raised_by(ins)
                            outputs(pl, w)
                            if w in CONV_AT:
                                for m_, k in CONV_AT[w]:
                                    conv(pl, m_, (k,))
                            if 6 <= w < 6 + NBLK:
                                out(pl, 1 - d, w - 6, pl.ph(p_ok, 18, w - 1), pl.ph(pv, 5, w - 5))
                            if d == 0 and w == 11:
                                stats(pl, mvar.value(b, 1))
                            if d == 0 and w == 20:
                                norm(pl, mrstd.value(b, 2))
                            if 14 <= w < 17:
                                split(pl, w - 14)
                            if w == 23:
                                remainder(pl)
                            if w in (24, 25):
                                difference(pl, 2 * (w - 24))
                                difference(pl, 2 * (w - 24) + 1)
                            if 27 <= w < 27 + M:
                                steps(pl, w - 27)
                assert c[0] == MCHAIN, ("MCHAIN", c[0])
                plE = Place(B, 0)
                c[0] = 0
                for m in range(M):
                    ins = finish(plE, m, y_value(plE, m))
                    ins.then_inc(fin_ok.sem, 1)
                    dve.wait_ge(fin_ok.sem, fin_ok.value(B, m + 1))
                for j in range(NBLK):
                    out(plE, 1, j, p_ok.value(B, j + 1), pv.value(B, 0) + j + 1)
                pv.n -= NBLK
                stats(plE, mvar.value(B, 1))
                norm(plE, mrstd.value(B, 2))
                for s in (conv_ok, pv, bc_ok, rest_ok, diff_ok, dt_ok, scan_ok, hC_ok, fin_ok):
                    s.whole()


def experts(nc, A, XE, YE):
    ctx = ExitStack()
    with ctx:
        sb = lambda name, shape, dt=F32: ctx.enter_context(nc.sbuf_tensor("e_" + name, shape, dt))
        sem = lambda name: ctx.enter_context(nc.semaphore("e_" + name))
        NB_ = 2
        CB = CAP // P
        ident = sb("ident", [P, P])
        xe = sb("xe", [P, NB_, CB, D])
        w_h = sb("w_h", [P, NB_, 3, 2 * P], BF16)
        w = sb("w", [P, NB_, 3, 2 * P])
        xeT = sb("xeT", [P, NB_, KD, CAP])
        hs = sb("hs", [P, NB_, CAP])
        hT = sb("hT", [P, NB_, CAP])
        ye = sb("ye", [P, NB_, CB, D])
        psX = ctx.enter_context(nc.psum_tensor("psX", [P, NB_, KD * CAP], F32))
        psH = ctx.enter_context(nc.psum_tensor("psH", [P, NB_, 2, CAP], F32))
        psO = ctx.enter_context(nc.psum_tensor("psO", [P, NB_, CB * D], F32))
        made = sem("made")
        with nc.Block() as block:
            @block.gpsimd
            def _(pool):
                nc.gpsimd.memset(ident[:, :], 0.0).then_inc(made, 1)
                pool.wait_ge(made, 1)
                nc.gpsimd.affine_select(out=ident[:, :], in_=ident[:, :], compare_op=ALU.not_equal, fill=1.0,
                                        base=0, pattern=[[-1, P]], channel_multiplier=1).then_inc(made, 1)
                pool.wait_ge(made, 2)

        sig = lambda name, per, first=0: Signal(sem(name), per, first)
        each = lambda name, per, first=0: [sig(name + str(c), per, first) for c in range(2)]
        x_in = each("x_in", 16)
        w_in = each("w_in", 48)
        w_ok = sig("w_ok", 2, 2)
        tr_ok = sig("tr_ok", 2, 2)
        xT_ok = sig("xT_ok", 2, 2)
        h_ok = sig("h_ok", 2, 2)
        sil_ok = sig("sil_ok", 2, 2)
        hT_ok = sig("hT_ok", 2, 2)
        o_ok = sig("o_ok", 2, 2)
        ye_ok = sig("ye_ok", 2, 2)
        y_out = each("y_out", 16, 16)
        alone_w = sem("alone_w")
        with nc.Block() as block:
            @block.sync
            def _(sp):
                for c in range(2):
                    sp.sem_inc(y_out[c].sem, 16)
                with sp.Fori(0, E // 2) as i:
                    for c in range(2):
                        sp.wait_ge(tr_ok.sem, tr_ok.value(i, c - 1))
                        sp.dma_start(xe[:, c, :, :], XE[bass.ds(2 * CAP * i + CAP * c, CAP), :].rearrange(
                            "(j p) d -> p j d", p=P)).then_inc(x_in[c].sem, 16)
                        sp.wait_ge(w_ok.sem, w_ok.value(i, c - 1))
                        for k, n in enumerate(("W1", "W3")):
                            sp.dma_start(w_h[:, c, k, :].rearrange("p (t n) -> p t n", n=I),
                                         A[n][bass.ds(2 * i + c, 1), :, :].rearrange("a (t p) n -> p (a t) n", p=P)
                                         ).then_inc(w_in[c].sem, 16)
                        sp.dma_start(w_h[:, c, 2, :], A["W2"][bass.ds(2 * i + c, 1), :, :].rearrange("a p n -> (a p) n")
                                     ).then_inc(w_in[c].sem, 16)

            @block.gpsimd
            def _(pool):
                pool.sem_inc(w_ok.sem, 2)
                with pool.Fori(0, E // 2) as i:
                    for c in range(2):
                        pool.wait_ge(w_in[c].sem, w_in[c].value(i, 48))
                        pool.wait_ge(o_ok.sem, o_ok.value(i, c - 1))
                        pool.sem_inc(alone_w, 1)
                        w_ok.raised_by(nc.gpsimd.tensor_copy(w[:, c, :, :], w_h[:, c, :, :]))

            @block.tensor
            def _(pe):
                t = nc.tensor
                pe.sem_inc(tr_ok.sem, 2)
                pe.sem_inc(h_ok.sem, 2)
                pe.sem_inc(o_ok.sem, 2)

                def flip(i, c):
                    pe.wait_ge(x_in[c].sem, x_in[c].value(i, 16))
                    pe.wait_ge(xT_ok.sem, xT_ok.value(i, c - 1))
                    for j in range(CB):
                        for k in range(KD):
                            ins = t.transpose(psX[:, c, k * CAP + j * P:k * CAP + (j + 1) * P],
                                              xe[:, c, j, k * P:(k + 1) * P], ident[:, :])
                    tr_ok.raised_by(ins)

                def hidden(i, c):
                    pe.wait_ge(w_ok.sem, w_ok.value(i, c + 1))
                    pe.wait_ge(xT_ok.sem, xT_ok.value(i, c + 1))
                    pe.wait_ge(hT_ok.sem, hT_ok.value(i, c - 1))
                    for n in range(2):
                        for k in range(KD):
                            ins = t.matmul(psH[:, c, n, :], w[:, c, n, k * I:(k + 1) * I], xeT[:, c, k, :],
                                           start=(k == 0), stop=(k == KD - 1))
                    h_ok.raised_by(ins)

                def output(i, c):
                    pe.wait_ge(hT_ok.sem, hT_ok.value(i, c + 1))
                    pe.wait_ge(ye_ok.sem, ye_ok.value(i, c - 1))
                    for j in range(CB):
                        ins = t.matmul(psO[:, c, j * D:(j + 1) * D], hT[:, c, j * P:(j + 1) * P], w[:, c, 2, :],
                                       start=True, stop=True)
                    o_ok.raised_by(ins)

                with pe.Fori(0, E // 2) as i:
                    flip(i, 0)
                    flip(i, 1)
                    hidden(i, 0)
                    hidden(i, 1)
                    output(i, 0)
                    output(i, 1)

            @block.vector
            def _(dve):
                v = nc.vector
                dve.sem_inc(xT_ok.sem, 2)
                dve.sem_inc(hT_ok.sem, 2)
                with dve.Fori(0, E // 2) as i:
                    for c in range(2):
                        dve.wait_ge(tr_ok.sem, tr_ok.value(i, c + 1))
                        dve.wait_ge(h_ok.sem, h_ok.value(i, c - 1))
                        xT_ok.raised_by(v.tensor_copy(xeT[:, c, :, :].rearrange("p t n -> p (t n)"), psX[:, c, :]))
                    for c in range(2):
                        dve.wait_ge(sil_ok.sem, sil_ok.value(i, c + 1))
                        dve.wait_ge(o_ok.sem, o_ok.value(i, c - 1))
                        hT_ok.raised_by(v.tensor_tensor(hT[:, c, :], hs[:, c, :], psH[:, c, 1, :], ALU.mult))

            @block.scalar
            def _(act):
                a = nc.scalar
                act.sem_inc(sil_ok.sem, 2)
                act.sem_inc(ye_ok.sem, 2)
                with act.Fori(0, E // 2) as i:
                    for c in range(2):
                        act.wait_ge(h_ok.sem, h_ok.value(i, c + 1))
                        act.wait_ge(hT_ok.sem, hT_ok.value(i, c - 1))
                        sil_ok.raised_by(a.activation(hs[:, c, :], psH[:, c, 0, :], ACT.Silu))
                    for c in range(2):
                        act.wait_ge(o_ok.sem, o_ok.value(i, c + 1))
                        act.wait_ge(y_out[c].sem, y_out[c].value(i, 0))
                        ye_ok.raised_by(a.activation(ye[:, c, :, :].rearrange("p j d -> p (j d)"), psO[:, c, :], ACT.Copy))
                        act.wait_ge(ye_ok.sem, ye_ok.value(i, c + 1))
                        act.dma_start(YE[bass.ds(2 * CAP * i + CAP * c, CAP), :].rearrange("(j p) d -> p j d", p=P),
                                      ye[:, c, :, :]).then_inc(y_out[c].sem, 16)
                for c in range(2):
                    act.wait_ge(y_out[c].sem, 16 * (E // 2 + 1))


def combine(nc, A, X1, XNT, YE, S1, slots_dram, gates_dram, OUT):
    ctx = ExitStack()
    with ctx:
        sb = lambda name, shape, dt=F32: ctx.enter_context(nc.sbuf_tensor("c_" + name, shape, dt))
        sem = lambda name: ctx.enter_context(nc.semaphore("c_" + name))
        NROW = NBLK * TOPK
        sw_h = sb("sw_h", [P, 3, 2 * P], BF16)
        sw = sb("sw", [P, 3, 2 * P])
        xT = sb("xT", [P, 2, KD, S])
        x1 = sb("x1", [P, 2, NBLK, D])
        s1 = sb("s1", [P, 2, NBLK, D])
        hs = sb("hs", [P, S])
        hT = sb("hT", [P, S])
        slot = sb("slot", [P, 2, NROW], U32)
        gates = sb("gates", [P, 2, NROW])
        yr = sb("yr", [P, 2, NROW, D])
        acc = sb("acc", [P, NBLK, D])
        g1 = sb("g1", [P, NBLK, D])
        res = sb("res", [P, 2, NBLK, D])
        psH = ctx.enter_context(nc.psum_tensor("psHc", [P, 2, S], F32))
        psO = ctx.enter_context(nc.psum_tensor("psOc", [P, NBLK, D], F32))
        w_in, made, prep = sem("w_in"), sem("made"), sem("prep")
        with nc.Block() as block:
            @block.sync
            def _(sp):
                for k, n in enumerate(("sw1T", "sw3T")):
                    sp.dma_start(sw_h[:, k, :].rearrange("p (t n) -> p t n", n=I),
                                 A[n].rearrange("(t p) n -> p t n", p=P)).then_inc(w_in, 16)
                sp.dma_start(sw_h[:, 2, :], A["sw2T"]).then_inc(w_in, 16)
                sp.wait_ge(w_in, 48)

            @block.gpsimd
            def _(pool):
                nc.gpsimd.memset(yr[:, :, :, :], 0.0).then_inc(made, 1)
                pool.wait_ge(made, 1)

            @block.vector
            def _(dve):
                dve.wait_ge(w_in, 48)
                nc.vector.tensor_copy(sw[:, :, :], sw_h[:, :, :]).then_inc(prep, 1)
                dve.wait_ge(prep, 1)

        sig = lambda name, per, first=0: Signal(sem(name), per, first)
        each = lambda name, per, first=0: [sig(name + str(c), per, first) for c in range(2)]
        xT_in = each("xT_in", 16)
        x1_in = each("x1_in", 16)
        s1_in = each("s1_in", 16)
        r_in = each("r_in", 32)
        y_in = each("y_in", 16 * NROW)
        h_ok = sig("h_ok", 2, 2)
        sil_ok = sig("sil_ok", 2, 2)
        hT_ok = sig("hT_ok", 2, 2)
        o_ok = sig("o_ok", 2, 2)
        acc_ok = sig("acc_ok", 2, 2)
        g_ok = sig("g_ok", 2, 2)
        out_ok = sig("out_ok", 2, 2)
        stored = each("stored", 16, 16)
        cchain = sig("cchain", 2 * TOPK)
        alone_c = sem("alone_c")
        with nc.Block() as block:
            @block.sync
            def _(sp):
                for c in range(2):
                    sp.sem_inc(stored[c].sem, 16)
                with sp.Fori(0, B // 2) as i:
                    for c in range(2):
                        seq = lambda T: T[bass.ds(2 * i + c, 1), :, :]
                        sp.wait_ge(acc_ok.sem, acc_ok.value(i, c - 1))
                        sp.dma_start(slot[:, c, :], seq(slots_dram).rearrange("a p n -> (a p) n")).then_inc(r_in[c].sem, 16)
                        sp.dma_start(gates[:, c, :], seq(gates_dram).rearrange("a p n -> (a p) n")).then_inc(r_in[c].sem, 16)
                        sp.wait_ge(h_ok.sem, h_ok.value(i, c - 1))
                        sp.dma_start(xT[:, c, :, :], seq(XNT).rearrange("a (t p) s -> p (a t) s", p=P)).then_inc(xT_in[c].sem, 16)
                        sp.wait_ge(out_ok.sem, out_ok.value(i, c - 1))
                        sp.dma_start(x1[:, c, :, :], seq(X1).rearrange("a (j p) d -> p (a j) d", p=P)).then_inc(x1_in[c].sem, 16)
                        sp.dma_start(s1[:, c, :, :], S1[bass.ds(2 * i + c + 1, 1), :, :].rearrange("a (j p) d -> p (a j) d", p=P)
                                     ).then_inc(s1_in[c].sem, 16)

            @block.gpsimd
            def _(pool):
                g = nc.gpsimd
                with pool.Fori(0, B // 2) as i:
                    for c in range(2):
                        pool.wait_ge(r_in[c].sem, r_in[c].value(i, 32))
                        pool.sem_inc(alone_c, 1)
                        for r in range(NROW):
                            g.indirect_dma_start(
                                out=yr[:, c, r, :], out_offset=None, in_=YE,
                                in_offset=bass.IndirectOffsetOnAxis(ap=slot[:, c, r:r + 1], axis=0),
                                bounds_check=E * CAP - 1, oob_is_err=False).then_inc(y_in[c].sem, 16)

            @block.tensor
            def _(pe):
                t = nc.tensor
                pe.sem_inc(h_ok.sem, 2)
                pe.sem_inc(o_ok.sem, 2)
                with pe.Fori(0, B // 2) as i:
                    for c in range(2):
                        pe.wait_ge(xT_in[c].sem, xT_in[c].value(i, 16))
                        pe.wait_ge(hT_ok.sem, hT_ok.value(i, c))
                        for n in range(2):
                            for k in range(KD):
                                ins = t.matmul(psH[:, n, :], sw[:, n, k * I:(k + 1) * I], xT[:, c, k, :],
                                               start=(k == 0), stop=(k == KD - 1))
                        h_ok.raised_by(ins)
                        pe.wait_ge(hT_ok.sem, hT_ok.value(i, c + 1))
                        pe.wait_ge(acc_ok.sem, acc_ok.value(i, c))
                        for j in range(NBLK):
                            ins = t.matmul(psO[:, j, :], hT[:, j * P:(j + 1) * P], sw[:, 2, :], start=True, stop=True)
                        o_ok.raised_by(ins)

            @block.scalar
            def _(act):
                a = nc.scalar
                act.sem_inc(sil_ok.sem, 2)
                act.sem_inc(g_ok.sem, 2)
                with act.Fori(0, B // 2) as i:
                    for c in range(2):
                        act.wait_ge(h_ok.sem, h_ok.value(i, c + 1))
                        act.wait_ge(hT_ok.sem, hT_ok.value(i, c))
                        sil_ok.raised_by(a.activation(hs[:, :], psH[:, 0, :], ACT.Silu))
                        act.wait_ge(acc_ok.sem, acc_ok.value(i, c + 1))
                        act.wait_ge(out_ok.sem, out_ok.value(i, c))
                        g_ok.raised_by(a.activation(g1[:, :, :], acc[:, :, :], ACT.Silu))
                        act.wait_ge(out_ok.sem, out_ok.value(i, c + 1))
                        act.dma_start(OUT[bass.ds(2 * i + c, 1), :, :].rearrange("a (j p) d -> p (a j) d", p=P),
                                      res[:, c, :, :]).then_inc(stored[c].sem, 16)
                for c in range(2):
                    act.wait_ge(stored[c].sem, 16 * (B // 2 + 1))

            @block.vector
            def _(dve):
                v = nc.vector
                for s in (hT_ok, acc_ok, out_ok):
                    dve.sem_inc(s.sem, 2)
                with dve.Fori(0, B // 2) as i:
                    def link(ins):
                        cchain.raised_by(ins)
                        dve.wait_ge(cchain.sem, cchain.value(i, cchain.n))

                    for c in range(2):
                        dve.wait_ge(sil_ok.sem, sil_ok.value(i, c + 1))
                        dve.wait_ge(o_ok.sem, o_ok.value(i, c))
                        hT_ok.raised_by(v.tensor_tensor(hT[:, :], hs[:, :], psH[:, 1, :], ALU.mult))
                        dve.wait_ge(o_ok.sem, o_ok.value(i, c + 1))
                        dve.wait_ge(g_ok.sem, g_ok.value(i, c))
                        dve.wait_ge(y_in[c].sem, y_in[c].value(i, 16 * NROW))
                        for k in range(TOPK):
                            for j in range(NBLK):
                                r = j * TOPK + k
                                ins = v.scalar_tensor_tensor(acc[:, j, :], yr[:, c, r, :], gates[:, c, r:r + 1],
                                                             psO[:, j, :] if k == 0 else acc[:, j, :], ALU.mult, ALU.add)
                            if k < TOPK - 1:
                                link(ins)
                        acc_ok.raised_by(ins)
                        dve.wait_ge(g_ok.sem, g_ok.value(i, c + 1))
                        dve.wait_ge(s1_in[c].sem, s1_in[c].value(i, 16))
                        dve.wait_ge(stored[c].sem, stored[c].value(i, 0))
                        link(v.tensor_tensor(res[:, c, :, :], g1[:, :, :], s1[:, c, :, :], ALU.mult))
                        dve.wait_ge(x1_in[c].sem, x1_in[c].value(i, 16))
                        ins = v.tensor_tensor(res[:, c, :, :], res[:, c, :, :], x1[:, c, :, :], ALU.add)
                        out_ok.raised_by(ins)
                assert cchain.n == 2 * TOPK, cchain.n


def program(nc, A, out):
    X1 = nc.dram_tensor("x1_rows", [B, S, D], F32).ap()
    XNT = nc.dram_tensor("xn_feature_major", [B, D, S], F32).ap()
    XE = nc.dram_tensor("expert_rows", [E * CAP, D], F32).ap()
    YE = nc.dram_tensor("expert_outputs", [E * CAP, D], F32).ap()
    S1 = nc.dram_tensor("mixed_rows", [B + 1, S, D], F32).ap()
    slots = nc.dram_tensor("token_slots", [B, P, NBLK * TOPK], U32).ap()
    gates = nc.dram_tensor("token_gates", [B, P, NBLK * TOPK], F32).ap()
    layer0(nc, A, X1, XNT, XE, slots, gates)
    layer1_mixer(nc, A, XNT, S1)
    experts(nc, A, XE, YE)
    combine(nc, A, X1, XNT, YE, S1, slots, gates, out)


def layouts(i):
    c = np.ascontiguousarray

    column = lambda v: c(v.reshape(-1, P).T)
    wide = lambda w: c(np.concatenate([w, np.zeros_like(w)], axis=1))
    high = lambda v: c(np.concatenate([v, np.zeros_like(v)]).reshape(P, 1))
    q, qb = i["L0_attn_qkv_w"], i["L0_attn_qkv_b"]
    r, rb = i["L0_attn_rkv_w"], i["L0_attn_rkv_b"]
    A = {"x": c(i["L0_attn_x"]),
         "wq": c(q[:, 0:D]), "wk": c(q[:, D:2 * D]), "wv": c(q[:, 2 * D:]),
         "bq": column(qb[0:D]), "bk": column(qb[D:2 * D]), "bv": c(qb[2 * D:]),
         "wrq": wide(i["L0_attn_rq_w"]), "brq": high(i["L0_attn_rq_b"]),
         "wrk": wide(r[:, :LAT]), "brk": high(rb[:LAT]), "wrv": c(r[:, LAT:]), "brv": c(rb[LAT:]),
         "wro": c(i["L0_attn_rout_w"]), "bro": c(i["L0_attn_rout_b"]),
         "wo": c(i["L0_attn_out_w"]), "bo": c(i["L0_attn_out_b"]),
         "gl": c(i["L0_attn_gl_w"][:, 0]), "gr": c(i["L0_attn_gr_w"][:, 0]),
         "wfcT": c(i["L0_ffn_W_fc"].T), "wpjT": c(i["L0_ffn_W_proj"].T),
         "lnw": column(i["L0_ffn_ln_w"]), "lnb": column(i["L0_ffn_ln_b"]),
         "gateT": c(i["L1_ffn_gate_w"].T), "ebias": c(i["L1_ffn_bias"]),
         "gam": c(i["L1_attn_ln_gamma"]), "bet": c(i["L1_attn_ln_beta"]),
         "W1": c(i["L1_ffn_W1"]), "W3": c(i["L1_ffn_W3"]), "W2": c(i["L1_ffn_W2"]),
         "sw1T": c(i["L1_ffn_sw1"].T), "sw3T": c(i["L1_ffn_sw3"].T), "sw2T": c(i["L1_ffn_sw2"].T)}
    for way, n in (("fwd", "f"), ("bwd", "b")):
        g = lambda k: i["L1_attn_" + way + "_" + k]
        xp = g("x_proj_w")
        A[n + "_win"] = c(g("in_proj_w").T)
        A[n + "_wbc"] = c(np.concatenate([xp[RK:].T] * 3, axis=1))
        A[n + "_wdr"] = c(xp[:RK].T)
        A[n + "_wdt"] = c(g("dt_proj_w").T)
        A[n + "_wout"] = c(g("out_proj_w").T)
        A[n + "_cw"] = c(g("conv_w"))
        A[n + "_cb"], A[n + "_db"], A[n + "_dd"] = column(g("conv_b")), column(g("dt_proj_b")), column(g("D"))
        A[n + "_al"] = c(g("A_log"))
    return A


def kernel(**inputs):
    import concourse.bacc as bacc
    from concourse.bass_utils import run_bass_kernel_spmd

    arrays = layouts({k: np.asarray(v) for k, v in inputs.items()})
    nc = bacc.Bacc("TRN2", target_bir_lowering=False, num_devices=1)
    A = {k: nc.dram_tensor(k, a.shape, mybir.dt.from_np(a.dtype), kind="ExternalInput").ap() for k, a in arrays.items()}
    out = nc.dram_tensor("out", (B, S, D), F32, kind="ExternalOutput").ap()
    program(nc, A, out)
    r = run_bass_kernel_spmd(nc, [arrays], core_ids=[0])
    return r.results[0]["out"]
```
